# Optimizing a Trainium2 kernel written in Bass

```python
import numpy as np
import jax
import jax.numpy as jnp

def _softmax(x, axis=-1):
    return jax.nn.softmax(x, axis=axis)

def _gelu(x):
    return jax.nn.gelu(x, approximate=True)

def _silu(x):
    return jax.nn.silu(x)

def _sigmoid(x):
    return jax.nn.sigmoid(x)

def _layernorm(x, axis=-1, eps=1e-05):
    m = jnp.mean(x, axis=axis, keepdims=True)
    v = jnp.var(x, axis=axis, keepdims=True)
    return (x - m) / jnp.sqrt(v + eps)

def _scatter_add(tgt, idx, src, axis=0):
    return tgt.at[idx].add(src)

def _segment_sum(src, seg, n):
    return jax.ops.segment_sum(src, seg, n)
kernel_name = 'mk_perceiver_d2_seqx_r4_36f12f'

def setup_inputs(seed: int=0):
    np.random.seed(seed)
    _w = jnp.asarray

    def _rec_inputs():
        import jax
        import jax.numpy as jnp
        _rk = jax.random.key(seed)
        x = -0.0002928 + 1 * jax.random.normal(jax.random.fold_in(_rk, 1), (32, 32, 256), jnp.float32)
        _lenS = 32 - jax.random.randint(jax.random.fold_in(_rk, 7), (32,), 0, max(1, 32 // 4) + 1, jnp.int32)
        _lenS2 = 257 - jax.random.randint(jax.random.fold_in(_rk, 8), (32,), 0, max(1, 257 // 4) + 1, jnp.int32)
        _ctx_1024P = jax.random.normal(jax.random.fold_in(_rk, 11), (32, 16, 256), jnp.float32)
        _ctx_1024c = jax.random.dirichlet(jax.random.fold_in(_rk, 511), 0.3 * jnp.ones((16,), jnp.float32), (32, 257))
        _ctx_1024t = jnp.einsum('bsk,bkd->bsd', _ctx_1024c, _ctx_1024P)
        _ctx_1024t = _ctx_1024t * jax.lax.rsqrt(jnp.mean(jnp.square(_ctx_1024t)) + 1e-12) * 0.953939
        ctx_1024 = -1.39393e-06 + 0.999914 * (_ctx_1024t + 0.3 * jax.random.normal(jax.random.fold_in(_rk, 611), (32, 257, 256), jnp.float32))
        _validS = jnp.arange(32)[None, :] < _lenS[:, None]
        _validS2 = jnp.arange(257)[None, :] < _lenS2[:, None]
        _causal = jnp.tril(jnp.ones((32, 32), dtype=bool))
        mask_Bx1xSxS2_if1 = jnp.where(jnp.ones((32, 1, 32, 257), dtype=bool), 1, 0).astype(jnp.int32)
        return (x, ctx_1024, mask_Bx1xSxS2_if1)
    x, ctx_1024, mask_Bx1xSxS2_if1 = _rec_inputs()

    def _L0_xattn_setup():
        import jax, jax.numpy as jnp
        import numpy as np
        B, S, D, H = (2, 512, 256, 16)
        HD = D // H
        key = jax.random.key(seed)
        ks = jax.random.split(key, 12)
        scale = 1.0 / np.sqrt(D)
        inp = {'q': jax.random.normal(ks[0], (B, S, D), jnp.float32), 'k': jax.random.normal(ks[1], (B, S, D), jnp.float32), 'v': jax.random.normal(ks[2], (B, S, D), jnp.float32), 'mask': jnp.ones((B, 1, S, S), jnp.int32), 'Wq': jax.random.normal(ks[3], (D, D), jnp.float32) * scale, 'bq': jnp.zeros((D,), jnp.float32), 'Wk': jax.random.normal(ks[4], (D, D), jnp.float32) * scale, 'bk': jnp.zeros((D,), jnp.float32), 'Wv': jax.random.normal(ks[5], (D, D), jnp.float32) * scale, 'bv': jnp.zeros((D,), jnp.float32), 'Wo': jax.random.normal(ks[6], (D, D), jnp.float32) * scale, 'bo': jnp.zeros((D,), jnp.float32)}
        return inp
    _L0_xattn_all = _L0_xattn_setup()
    _L0_xattn_in = {k: v for k, v in _L0_xattn_all.items() if k in ('Wq', 'bq', 'Wk', 'bk', 'Wv', 'bv', 'Wo', 'bo')}
    del _L0_xattn_all

    def _L0_attn_setup():
        import jax, jax.numpy as jnp
        import numpy as np
        HEADS = 16
        KERNEL_SIZE = 4
        STRIDE = 2
        DIM = 256
        key = jax.random.key(seed)
        k1, k2, k3, k4 = jax.random.split(key, 4)
        B, L, C = (4, 1024, DIM)
        x = jax.random.normal(k1, (B, L, C), dtype=jnp.float32)
        w_qkv = jax.random.normal(k2, (C, 3 * C), dtype=jnp.float32) * C ** (-0.5)
        w_out = jax.random.normal(k3, (C, C), dtype=jnp.float32) * C ** (-0.5)
        b_out = jax.random.normal(k4, (C,), dtype=jnp.float32) * 0.01
        return {'x': x, 'w_qkv': w_qkv, 'w_out': w_out, 'b_out': b_out}
    _L0_attn_all = _L0_attn_setup()
    _L0_attn_in = {k: v for k, v in _L0_attn_all.items() if k in ('w_qkv', 'w_out', 'b_out')}
    del _L0_attn_all

    def _L0_ffn_setup():
        import jax, jax.numpy as jnp
        import numpy as np
        D = 256
        H = 1024
        E = 8
        B = 2
        T = 512
        LN_EPS = 1e-05

        def _layer_norm(r, gamma, beta):
            mu = jnp.mean(r, axis=-1, keepdims=True)
            var = jnp.mean(jnp.square(r - mu), axis=-1, keepdims=True)
            return (r - mu) * jax.lax.rsqrt(var + LN_EPS) * gamma + beta
        key = jax.random.key(seed)
        ks = jax.random.split(key, 9)
        s_in = 1.0 / np.sqrt(D)
        s_hid = 1.0 / np.sqrt(H)
        x = jax.random.normal(ks[0], (B, T, D), dtype=jnp.float32)
        Wg = jax.random.uniform(ks[1], (D, E), jnp.float32, -s_in, s_in)
        bg = jax.random.uniform(ks[2], (E,), jnp.float32, -s_in, s_in)
        W1 = jax.random.uniform(ks[3], (E, D, H), jnp.float32, -s_in, s_in)
        b1 = jax.random.uniform(ks[4], (E, H), jnp.float32, -s_in, s_in)
        W2 = jax.random.uniform(ks[5], (E, H, D), jnp.float32, -s_hid, s_hid)
        b2 = jax.random.uniform(ks[6], (E, D), jnp.float32, -s_hid, s_hid)
        gamma = jnp.ones((D,), jnp.float32)
        beta = jnp.zeros((D,), jnp.float32)
        return {'x': x, 'Wg': Wg, 'bg': bg, 'W1': W1, 'b1': b1, 'W2': W2, 'b2': b2, 'gamma': gamma, 'beta': beta}
    _L0_ffn_all = _L0_ffn_setup()
    _L0_ffn_in = {k: v for k, v in _L0_ffn_all.items() if k in ('Wg', 'bg', 'W1', 'b1', 'W2', 'b2', 'gamma', 'beta')}
    del _L0_ffn_all

    def _L1_xattn_setup():
        import jax, jax.numpy as jnp
        import numpy as np
        D = 256
        NUM_ITERS = 3
        EPS = 1e-06
        SCALE = D ** (-0.5)

        def rmsnorm(x, w, eps=EPS):
            return x * jax.lax.rsqrt(jnp.mean(x * x, axis=-1, keepdims=True) + eps) * w

        def gru_cell(x, h, wih, whh, bih, bhh):
            gx = x @ wih.T + bih
            gh = h @ whh.T + bhh
            xr, xz, xn = jnp.split(gx, 3, axis=-1)
            hr, hz, hn = jnp.split(gh, 3, axis=-1)
            r = jax.nn.sigmoid(xr + hr)
            z = jax.nn.sigmoid(xz + hz)
            n = jnp.tanh(xn + r * hn)
            return (1.0 - z) * n + z * h
        key = jax.random.key(seed)
        ks = jax.random.split(key, 8)
        B, K, M, d = (8, 64, 1024, D)
        w_std = d ** (-0.5)
        return {'slots': jax.random.normal(ks[0], (B, K, d), jnp.float32), 'P': jax.random.normal(ks[1], (B, M, d), jnp.float32), 'Wq': jax.random.normal(ks[2], (d, d), jnp.float32) * w_std, 'Wk': jax.random.normal(ks[3], (d, d), jnp.float32) * w_std, 'Wv': jax.random.normal(ks[4], (d, d), jnp.float32) * w_std, 'gru_wih': jax.random.normal(ks[5], (3 * d, d), jnp.float32) * w_std, 'gru_whh': jax.random.normal(ks[6], (3 * d, d), jnp.float32) * w_std, 'gru_bih': jnp.zeros((3 * d,), jnp.float32), 'gru_bhh': jnp.zeros((3 * d,), jnp.float32), 'slot_norm_w': jnp.ones((d,), jnp.float32), 'input_norm_w': jnp.ones((d,), jnp.float32)}
    _L1_xattn_all = _L1_xattn_setup()
    _L1_xattn_in = {k: v for k, v in _L1_xattn_all.items() if k in ('Wq', 'Wk', 'Wv', 'gru_wih', 'gru_whh', 'gru_bih', 'gru_bhh', 'slot_norm_w', 'input_norm_w')}
    del _L1_xattn_all

    def _L1_attn_setup():
        import jax, jax.numpy as jnp
        import numpy as np
        B, T, E = (4, 512, 256)
        NUM_HEADS = 16
        HEAD_SIZE = E // NUM_HEADS

        def _rope_tables(T, E):
            thetas = 10000.0 ** (-jnp.arange(0, E, 2, dtype=jnp.float32) / E)
            thetas = jnp.repeat(thetas, 2)
            angles = jnp.arange(T, dtype=jnp.float32)[:, None] * thetas[None, :]
            return (jnp.sin(angles), jnp.cos(angles))

        def _rotate(x, sin, cos):
            Bx, Tx, Ex = x.shape
            xp = x.reshape(Bx, Tx, Ex // 2, 2)
            rot = jnp.stack([-xp[..., 1], xp[..., 0]], axis=-1).reshape(Bx, Tx, Ex)
            return x * cos + rot * sin
        key = jax.random.key(seed)
        ks = jax.random.split(key, 6)
        scale = 1.0 / np.sqrt(E)
        return {'input': jax.random.normal(ks[0], (B, T, E), dtype=jnp.float32), 'Wq': jax.random.normal(ks[1], (E, E), dtype=jnp.float32) * scale, 'Wk': jax.random.normal(ks[2], (E, E), dtype=jnp.float32) * scale, 'Wv': jax.random.normal(ks[3], (E, E), dtype=jnp.float32) * scale, 'Wo': jax.random.normal(ks[4], (E, E), dtype=jnp.float32) * scale, 'bo': jnp.zeros((E,), dtype=jnp.float32)}
    _L1_attn_all = _L1_attn_setup()
    _L1_attn_in = {k: v for k, v in _L1_attn_all.items() if k in ('Wq', 'Wk', 'Wv', 'Wo', 'bo')}
    del _L1_attn_all

    def _L1_ffn_setup():
        import jax, jax.numpy as jnp
        import numpy as np
        E, K = (8, 2)
        B, S, H, F = (2, 512, 256, 1024)
        EPS = 1e-12

        def _expert_ffn(xf, Wi_e, bi_e, Wg_e, bg_e, Wo_e, bo_e, g_e, b_e):
            h = jax.nn.gelu(xf @ Wi_e + bi_e, approximate=False) * jax.nn.sigmoid(xf @ Wg_e + bg_e)
            r = xf + (h @ Wo_e + bo_e)
            mu = jnp.mean(r, axis=-1, keepdims=True)
            var = jnp.mean(jnp.square(r - mu), axis=-1, keepdims=True)
            return (r - mu) * jax.lax.rsqrt(var + EPS) * g_e + b_e
        key = jax.random.key(seed)
        ks = jax.random.split(key, 8)
        s = 0.02
        return {'x': jax.random.normal(ks[0], (B, S, H), jnp.float32), 'Wr': jax.random.normal(ks[1], (H, E), jnp.float32) * s, 'br': jnp.zeros((E,), jnp.float32), 'Wi': jax.random.normal(ks[2], (E, H, F), jnp.float32) * s, 'bi': jnp.zeros((E, F), jnp.float32), 'Wg': jax.random.normal(ks[3], (E, H, F), jnp.float32) * s, 'bg': jnp.zeros((E, F), jnp.float32), 'Wo': jax.random.normal(ks[4], (E, F, H), jnp.float32) * s, 'bo': jnp.zeros((E, H), jnp.float32), 'gamma': jnp.ones((E, H), jnp.float32), 'beta': jnp.zeros((E, H), jnp.float32)}
    _L1_ffn_all = _L1_ffn_setup()
    _L1_ffn_in = {k: v for k, v in _L1_ffn_all.items() if k in ('Wr', 'br', 'Wi', 'bi', 'Wg', 'bg', 'Wo', 'bo', 'gamma', 'beta')}
    del _L1_ffn_all
    return {'x': x, 'ctx_1024': ctx_1024, 'mask_Bx1xSxS2_if1': mask_Bx1xSxS2_if1, 'L0_xattn_Wq': _L0_xattn_in['Wq'], 'L0_xattn_bq': _L0_xattn_in['bq'], 'L0_xattn_Wk': _L0_xattn_in['Wk'], 'L0_xattn_bk': _L0_xattn_in['bk'], 'L0_xattn_Wv': _L0_xattn_in['Wv'], 'L0_xattn_bv': _L0_xattn_in['bv'], 'L0_xattn_Wo': _L0_xattn_in['Wo'], 'L0_xattn_bo': _L0_xattn_in['bo'], 'L0_attn_w_qkv': _L0_attn_in['w_qkv'], 'L0_attn_w_out': _L0_attn_in['w_out'], 'L0_attn_b_out': _L0_attn_in['b_out'], 'L0_ffn_Wg': _L0_ffn_in['Wg'], 'L0_ffn_bg': _L0_ffn_in['bg'], 'L0_ffn_W1': _L0_ffn_in['W1'], 'L0_ffn_b1': _L0_ffn_in['b1'], 'L0_ffn_W2': _L0_ffn_in['W2'], 'L0_ffn_b2': _L0_ffn_in['b2'], 'L0_ffn_gamma': _L0_ffn_in['gamma'], 'L0_ffn_beta': _L0_ffn_in['beta'], 'L1_xattn_Wq': _L1_xattn_in['Wq'], 'L1_xattn_Wk': _L1_xattn_in['Wk'], 'L1_xattn_Wv': _L1_xattn_in['Wv'], 'L1_xattn_gru_wih': _L1_xattn_in['gru_wih'], 'L1_xattn_gru_whh': _L1_xattn_in['gru_whh'], 'L1_xattn_gru_bih': _L1_xattn_in['gru_bih'], 'L1_xattn_gru_bhh': _L1_xattn_in['gru_bhh'], 'L1_xattn_slot_norm_w': _L1_xattn_in['slot_norm_w'], 'L1_xattn_input_norm_w': _L1_xattn_in['input_norm_w'], 'L1_attn_Wq': _L1_attn_in['Wq'], 'L1_attn_Wk': _L1_attn_in['Wk'], 'L1_attn_Wv': _L1_attn_in['Wv'], 'L1_attn_Wo': _L1_attn_in['Wo'], 'L1_attn_bo': _L1_attn_in['bo'], 'L1_ffn_Wr': _L1_ffn_in['Wr'], 'L1_ffn_br': _L1_ffn_in['br'], 'L1_ffn_Wi': _L1_ffn_in['Wi'], 'L1_ffn_bi': _L1_ffn_in['bi'], 'L1_ffn_Wg': _L1_ffn_in['Wg'], 'L1_ffn_bg': _L1_ffn_in['bg'], 'L1_ffn_Wo': _L1_ffn_in['Wo'], 'L1_ffn_bo': _L1_ffn_in['bo'], 'L1_ffn_gamma': _L1_ffn_in['gamma'], 'L1_ffn_beta': _L1_ffn_in['beta']}

def reference(x, ctx_1024, mask_Bx1xSxS2_if1, L0_xattn_Wq, L0_xattn_bq, L0_xattn_Wk, L0_xattn_bk, L0_xattn_Wv, L0_xattn_bv, L0_xattn_Wo, L0_xattn_bo, L0_attn_w_qkv, L0_attn_w_out, L0_attn_b_out, L0_ffn_Wg, L0_ffn_bg, L0_ffn_W1, L0_ffn_b1, L0_ffn_W2, L0_ffn_b2, L0_ffn_gamma, L0_ffn_beta, L1_xattn_Wq, L1_xattn_Wk, L1_xattn_Wv, L1_xattn_gru_wih, L1_xattn_gru_whh, L1_xattn_gru_bih, L1_xattn_gru_bhh, L1_xattn_slot_norm_w, L1_xattn_input_norm_w, L1_attn_Wq, L1_attn_Wk, L1_attn_Wv, L1_attn_Wo, L1_attn_bo, L1_ffn_Wr, L1_ffn_br, L1_ffn_Wi, L1_ffn_bi, L1_ffn_Wg, L1_ffn_bg, L1_ffn_Wo, L1_ffn_bo, L1_ffn_gamma, L1_ffn_beta):
    import jax
    import jax.numpy as jnp

    def _L0_xattn_ref(q, k, v, mask, Wq, bq, Wk, bk, Wv, bv, Wo, bo):
        import jax, jax.numpy as jnp
        import numpy as np
        B, S, D, H = (2, 512, 256, 16)
        HD = D // H
        b = q.shape[0]
        qh = (q @ Wq + bq).reshape(b, -1, H, HD).transpose(0, 2, 1, 3)
        kh = (k @ Wk + bk).reshape(b, -1, H, HD).transpose(0, 2, 1, 3)
        vh = (v @ Wv + bv).reshape(b, -1, H, HD).transpose(0, 2, 1, 3)
        scores = jnp.einsum('bhqd,bhkd->bhqk', qh, kh) / jnp.sqrt(jnp.float32(HD))
        scores = jnp.where(mask == 0, jnp.float32(-1000000000.0), scores)
        p_attn = jax.nn.softmax(scores, axis=-1)
        x = jnp.einsum('bhqk,bhkd->bhqd', p_attn, vh)
        x = x.transpose(0, 2, 1, 3).reshape(b, -1, H * HD)
        return x @ Wo + bo

    def _L0_attn_ref(x, w_qkv, w_out, b_out):
        import jax, jax.numpy as jnp
        import numpy as np
        HEADS = 16
        KERNEL_SIZE = 4
        STRIDE = 2
        DIM = 256
        B, L, C = x.shape
        ks, stride, heads = (KERNEL_SIZE, STRIDE, HEADS)
        hd = C // heads
        scale = C ** (-0.5)
        W = (L - ks) // stride + 1
        idx = jnp.arange(W)[:, None] * stride + jnp.arange(ks)[None, :]
        xw = x[:, idx]
        qkv = xw @ w_qkv
        q, k, v = jnp.split(qkv, 3, axis=-1)
        q = q.reshape(B, W, ks, heads, hd)
        k = k.reshape(B, W, ks, heads, hd)
        v = v.reshape(B, W, ks, heads, hd)
        dots = jnp.einsum('bwqhd,bwkhd->bwhqk', q, k) * scale
        attn = jax.nn.softmax(dots, axis=-1)
        o = jnp.einsum('bwhqk,bwkhd->bwqhd', attn, v).reshape(B, W, ks, C)
        o = o @ w_out + b_out
        out = jnp.zeros_like(x).at[:, idx.reshape(-1)].add(o.reshape(B, W * ks, C))
        return out

    def _L0_ffn_ref(x, Wg, bg, W1, b1, W2, b2, gamma, beta):
        import jax, jax.numpy as jnp
        import numpy as np
        D = 256
        H = 1024
        E = 8
        B = 2
        T = 512
        LN_EPS = 1e-05

        def _layer_norm(r, gamma, beta):
            mu = jnp.mean(r, axis=-1, keepdims=True)
            var = jnp.mean(jnp.square(r - mu), axis=-1, keepdims=True)
            return (r - mu) * jax.lax.rsqrt(var + LN_EPS) * gamma + beta
        logits = jnp.einsum('btd,de->bte', x, Wg) + bg
        top2_vals, top2_idx = jax.lax.top_k(logits, 2)
        scores = jax.nn.softmax(top2_vals, axis=-1)
        onehot = jax.nn.one_hot(top2_idx, E, dtype=x.dtype)
        combine = jnp.einsum('btk,btke->bte', scores, onehot)
        h = jnp.einsum('btd,edh->bteh', x, W1) + b1[None, None]
        h = jax.nn.gelu(h, approximate=False)
        y = jnp.einsum('bteh,ehd->bted', h, W2) + b2[None, None]
        out = jnp.einsum('bted,bte->btd', y, combine)
        return _layer_norm(x + out, gamma, beta)

    def _L1_xattn_ref(slots, P, Wq, Wk, Wv, gru_wih, gru_whh, gru_bih, gru_bhh, slot_norm_w, input_norm_w):
        import jax, jax.numpy as jnp
        import numpy as np
        D = 256
        NUM_ITERS = 3
        EPS = 1e-06
        SCALE = D ** (-0.5)

        def rmsnorm(x, w, eps=EPS):
            return x * jax.lax.rsqrt(jnp.mean(x * x, axis=-1, keepdims=True) + eps) * w

        def gru_cell(x, h, wih, whh, bih, bhh):
            gx = x @ wih.T + bih
            gh = h @ whh.T + bhh
            xr, xz, xn = jnp.split(gx, 3, axis=-1)
            hr, hz, hn = jnp.split(gh, 3, axis=-1)
            r = jax.nn.sigmoid(xr + hr)
            z = jax.nn.sigmoid(xz + hz)
            n = jnp.tanh(xn + r * hn)
            return (1.0 - z) * n + z * h
        Pn = rmsnorm(P, input_norm_w)
        k_proj = Pn @ Wk.T
        v_proj = Pn @ Wv.T
        for _ in range(NUM_ITERS):
            sn = rmsnorm(slots, slot_norm_w)
            q_proj = sn @ Wq.T
            scores = jnp.einsum('bkd,bmd->bkm', q_proj, k_proj) * SCALE
            attn = jax.nn.softmax(scores, axis=-2)
            attn = attn / (jnp.sum(attn, axis=-1, keepdims=True) + EPS)
            updates = jnp.einsum('bkm,bmd->bkd', attn, v_proj)
            slots = gru_cell(updates, slots, gru_wih, gru_whh, gru_bih, gru_bhh)
        return slots

    def _L1_attn_ref(input, Wq, Wk, Wv, Wo, bo):
        import jax, jax.numpy as jnp
        import numpy as np
        B, T, E = (4, 512, 256)
        NUM_HEADS = 16
        HEAD_SIZE = E // NUM_HEADS

        def _rope_tables(T, E):
            thetas = 10000.0 ** (-jnp.arange(0, E, 2, dtype=jnp.float32) / E)
            thetas = jnp.repeat(thetas, 2)
            angles = jnp.arange(T, dtype=jnp.float32)[:, None] * thetas[None, :]
            return (jnp.sin(angles), jnp.cos(angles))

        def _rotate(x, sin, cos):
            Bx, Tx, Ex = x.shape
            xp = x.reshape(Bx, Tx, Ex // 2, 2)
            rot = jnp.stack([-xp[..., 1], xp[..., 0]], axis=-1).reshape(Bx, Tx, Ex)
            return x * cos + rot * sin
        Bx, Tx, Ex = input.shape
        sin, cos = _rope_tables(Tx, Ex)
        rx = _rotate(input, sin, cos)
        q = rx @ Wq.T
        k = rx @ Wk.T
        v = input @ Wv.T

        def split_heads(t):
            return t.reshape(Bx, Tx, NUM_HEADS, HEAD_SIZE).transpose(0, 2, 1, 3)
        q, k, v = (split_heads(q), split_heads(k), split_heads(v))
        scores = jnp.einsum('bhqd,bhkd->bhqk', q, k)
        causal = jnp.tril(jnp.ones((Tx, Tx), dtype=bool))
        scores = jnp.where(causal[None, None], scores, -jnp.inf) / np.sqrt(HEAD_SIZE)
        attn = jax.nn.softmax(scores, axis=-1)
        out = jnp.einsum('bhqk,bhkd->bhqd', attn, v)
        out = out.transpose(0, 2, 1, 3).reshape(Bx, Tx, Ex)
        return out @ Wo.T + bo

    def _L1_ffn_ref(x, Wr, br, Wi, bi, Wg, bg, Wo, bo, gamma, beta):
        import jax, jax.numpy as jnp
        import numpy as np
        E, K = (8, 2)
        B, S, H, F = (2, 512, 256, 1024)
        EPS = 1e-12

        def _expert_ffn(xf, Wi_e, bi_e, Wg_e, bg_e, Wo_e, bo_e, g_e, b_e):
            h = jax.nn.gelu(xf @ Wi_e + bi_e, approximate=False) * jax.nn.sigmoid(xf @ Wg_e + bg_e)
            r = xf + (h @ Wo_e + bo_e)
            mu = jnp.mean(r, axis=-1, keepdims=True)
            var = jnp.mean(jnp.square(r - mu), axis=-1, keepdims=True)
            return (r - mu) * jax.lax.rsqrt(var + EPS) * g_e + b_e
        b, s, h = x.shape
        T = b * s
        xf = x.reshape(T, h)
        probs = jax.nn.softmax(xf @ Wr + br, axis=-1)
        topw, topi = jax.lax.top_k(probs, K)
        topw = topw / jnp.sum(topw, axis=-1, keepdims=True)
        c = jnp.zeros((T, E), x.dtype).at[jnp.arange(T)[:, None], topi].set(topw)
        y = jax.vmap(_expert_ffn, in_axes=(None, 0, 0, 0, 0, 0, 0, 0, 0))(xf, Wi, bi, Wg, bg, Wo, bo, gamma, beta)
        out = jnp.einsum('te,eth->th', c, y)
        return out.reshape(b, s, h)
    x = x + _L0_xattn_ref(_layernorm(x, axis=-1), ctx_1024, ctx_1024, mask_Bx1xSxS2_if1, L0_xattn_Wq, L0_xattn_bq, L0_xattn_Wk, L0_xattn_bk, L0_xattn_Wv, L0_xattn_bv, L0_xattn_Wo, L0_xattn_bo)
    x = x + _L0_attn_ref(_layernorm(x, axis=-1), L0_attn_w_qkv, L0_attn_w_out, L0_attn_b_out)
    x = x + _L0_ffn_ref(_layernorm(x, axis=-1), L0_ffn_Wg, L0_ffn_bg, L0_ffn_W1, L0_ffn_b1, L0_ffn_W2, L0_ffn_b2, L0_ffn_gamma, L0_ffn_beta)
    x = x + _L1_xattn_ref(_layernorm(x, axis=-1), ctx_1024, L1_xattn_Wq, L1_xattn_Wk, L1_xattn_Wv, L1_xattn_gru_wih, L1_xattn_gru_whh, L1_xattn_gru_bih, L1_xattn_gru_bhh, L1_xattn_slot_norm_w, L1_xattn_input_norm_w)
    x = x + _L1_attn_ref(_layernorm(x, axis=-1), L1_attn_Wq, L1_attn_Wk, L1_attn_Wv, L1_attn_Wo, L1_attn_bo)
    x = x + _L1_ffn_ref(_layernorm(x, axis=-1), L1_ffn_Wr, L1_ffn_br, L1_ffn_Wi, L1_ffn_bi, L1_ffn_Wg, L1_ffn_bg, L1_ffn_Wo, L1_ffn_bo, L1_ffn_gamma, L1_ffn_beta)
    return x

_drawn_inputs = setup_inputs


def setup_inputs(seed=0):
    import zlib

    import numpy as np

    out = dict(_drawn_inputs(seed))
    spreads = {'L0_xattn_bq': (0.0, 0.279),
     'L0_xattn_bk': (0.0, 0.8),
     'L0_xattn_bv': (0.0, 0.1),
     'L0_xattn_bo': (0.0, 0.1),
     'L0_ffn_gamma': (1.0, 0.2),
     'L0_ffn_beta': (0.0, 0.1),
     'L1_xattn_gru_bih': (0.0, 0.295),
     'L1_xattn_gru_bhh': (0.0, 0.474),
     'L1_xattn_slot_norm_w': (1.0, 0.6),
     'L1_xattn_input_norm_w': (1.0, 0.554),
     'L1_attn_bo': (0.0, 0.1),
     'L1_ffn_br': (0.0, 0.367),
     'L1_ffn_bi': (0.0, 0.8),
     'L1_ffn_bg': (0.0, 0.8),
     'L1_ffn_bo': (0.0, 0.429),
     'L1_ffn_gamma': (1.0, 0.2),
     'L1_ffn_beta': (0.0, 0.448)}
    factors = {'L0_attn_b_out': 4.408,
     'L0_ffn_bg': 4.686,
     'L0_ffn_b1': 8.0,
     'L0_ffn_b2': 8.0,
     'L1_ffn_Wi': 5.552,
     'L1_ffn_Wg': 8.0,
     'L1_ffn_Wo': 5.152}
    for name, (base, spread) in spreads.items():
        noise = np.random.default_rng([zlib.crc32(name.encode()), seed]).standard_normal(out[name].shape)
        drawn = base * np.exp(spread * noise) if base else spread * noise
        out[name] = jnp.asarray(drawn.astype(out[name].dtype))
    for name, factor in factors.items():
        out[name] = (out[name] * factor).astype(out[name].dtype)
    return out
```

```python
import concourse.bass as bass
from concourse import mybir
from contextlib import ExitStack

F32 = mybir.dt.float32
I32 = mybir.dt.int32
ALU = mybir.AluOpType
ACT = mybir.ActivationFunctionType
AX = mybir.AxisListType

P = 128
B, S, D = 32, 32, 256
KEYS = 257
HEADS, HD = 16, 16
C = D // P
NT = B * S // P
TB = P // S
HG = P // S
E, FF = 8, 1024
SLOT = 256
SLOTS = (2 * B * S + E * (SLOT - 1)) // SLOT
SLOTS_EACH = B * S // SLOT
NG = HEADS // HG
HC = P // HD
KT2 = KEYS // P
MASKED = -1.0e30

CONST_COLS = {}
_at = 0
for _n, _w in [("ident", P), ("ones", P), ("before", P), ("head_of_row", HC), ("group_of_row", HG), ("query", S),
               ("window_pen", 2 * S), ("window_on", 2), ("causal_pen", S), ("cos", D), ("sin", D), ("minus_half", 16),
               ("prefer", 8), ("slot_floor", 4), ("slot", 15), ("window_count", P), ("last_key", 3 * B)]:
    CONST_COLS[_n] = (_at, _at + _w)
    _at += _w
CONST_WIDTH = _at


class Count:

    def __init__(self, eng, sem):
        self.eng, self.sem, self.base, self.n = eng, sem, 0, 0

    def after(self, ins):
        self.n += 1
        ins.then_inc(self.sem, 1)
        self.eng.wait_ge(self.sem, self.base + self.n)

    def enter(self, trip, per_trip):
        self.start, self.per = self.base + self.n, per_trip
        self.base, self.n = self.start + trip * per_trip, 0

    def leave_open(self):
        assert self.n == self.per, (self.n, self.per)
        self.base, self.n = self.start, 0

    def leave(self, trips):
        assert self.n == self.per, (self.n, self.per)
        self.base, self.n = self.start + trips * self.per, 0


class Core:
    pass


def build(nc, ins, out):
    with ExitStack() as ctx:
        k = Core()
        k.nc, k.ins = nc, ins
        k.sem = nc.alloc_semaphore
        k.consts = ctx.enter_context(nc.sbuf_tensor("consts", [P, CONST_WIDTH], F32))
        k.x = ctx.enter_context(nc.sbuf_tensor("x", [P, NT, D], F32))
        k.z = ctx.enter_context(nc.sbuf_tensor("z", [P, NT, D], F32))
        k.zT = ctx.enter_context(nc.sbuf_tensor("zT", [P, C, NT * P], F32))
        k.stats = ctx.enter_context(nc.sbuf_tensor("stats", [P, NT, 6], F32))
        k.mean_var = ctx.enter_context(nc.sbuf_tensor("mean_var", [P, NT, 2], F32))
        k.rstd = ctx.enter_context(nc.sbuf_tensor("rstd", [P, NT], F32))
        k.ps = ctx.enter_context(nc.psum_tensor("ps", [P, 8, 512], F32))

        def const(name):
            a, b = CONST_COLS[name]
            return k.consts[:, a:b]
        k.const = const
        k.ident = const("ident")
        k.consts_loaded = k.sem("consts_loaded")
        k.passed = k.sem("passed")
        k.sorted_x = nc.dram_tensor("sorted_x", [SLOTS * SLOT, D], F32)
        k.sorted_y = nc.dram_tensor("sorted_y", [SLOTS * SLOT, D], F32)
        k.cleared = k.sem("sorted_x_cleared")
        zero_set = k.sem("zero_set")
        with nc.Block() as block:
            @block.vector
            def _(dve):
                nc.vector.memset(k.z[:, 0, :], 0.0).then_inc(zero_set, 1)

            @block.scalar
            def _(act):
                act.wait_ge(zero_set, 1)
                for n in range(2 * SLOTS):
                    act.dma_start(k.sorted_x.ap()[n * P:(n + 1) * P, :], k.z[:, 0, :]).then_inc(k.cleared, 16)
                act.wait_ge(k.cleared, 16 * 2 * SLOTS)
        for stage in (cross_attention, local_attention, experts_one, slot_attention, causal_attention,
                      experts_two):
            used = []

            def stage_sem(name):
                used.append(nc.alloc_semaphore(name))
                return used[-1]
            k.sem = stage_sem
            stage(nc, k)
            nc.clear_and_free_semaphores(used)
            nc.all_engine_barrier()
        k.sem = nc.alloc_semaphore
        x_stored = k.sem("x_stored")
        with nc.Block() as block:
            @block.sync
            def _(sp):
                sp.dma_start(out.rearrange("b s d -> (b s) d").rearrange("(t p) d -> p t d", p=P),
                             k.x[:, :, :]).then_inc(x_stored, 16)
                sp.wait_ge(x_stored, 16)


class Transpose:

    def __init__(self, nc, k, name, src, dst, bank0=0):
        self.nc, self.k, self.src, self.dst, self.bank0 = nc, k, src, dst, bank0
        self.src_ready = k.sem(name + "_rows_ready")
        self.done = k.sem(name + "_transposed")
        self.ready = k.sem(name + "_columns_ready")

    def tensor(self, pe):
        for half in range(2):
            for t in range(4 * half, 4 * half + 4):
                pe.wait_ge(self.src_ready, t + 1)
                for c in range(C):
                    last = self.nc.tensor.transpose(
                        self.k.ps[:, self.bank0 + 2 * c + half, (t % 4) * P:(t % 4 + 1) * P],
                        self.src[:, t, c * P:(c + 1) * P], self.k.ident)
            last.then_inc(self.done, 1)

    def vector(self, dve):
        for half in range(2):
            dve.wait_ge(self.done, half + 1)
            self.nc.vector.tensor_copy(self.dst[:, 1, half * 512:half * 512 + 512],
                                       self.k.ps[:, self.bank0 + 2 + half, :]).then_inc(self.ready, 1)

    def scalar(self, act):
        for half in range(2):
            act.wait_ge(self.done, half + 1)
            self.nc.scalar.copy(self.dst[:, 0, half * 512:half * 512 + 512],
                                self.k.ps[:, self.bank0 + half, :]).then_inc(self.ready, 1)


class Norm:

    def __init__(self, nc, k, name, eps, src, dst, dst_ready=None):
        self.nc, self.k, self.eps, self.src, self.dst = nc, k, eps, src, dst
        self.stats_ready = k.sem(name + "_stats_ready")
        self.var_ready = k.sem(name + "_var_ready")
        self.rstd_ready = k.sem(name + "_rstd_ready")
        self.dst_ready = dst_ready or k.sem(name + "_rows_ready")

    def vector(self, dve, order):
        nc, k = self.nc, self.k
        for t in range(NT):
            last = nc.vector.bn_stats(k.stats[:, t, :], self.src[:, t, :])
        order.after(last)
        for t in range(NT):
            last = nc.vector.bn_aggr(k.mean_var[:, t, :], k.stats[:, t, :])
        last.then_inc(self.stats_ready, 1)
        dve.wait_ge(self.rstd_ready, 1)
        for t in range(NT):
            nc.vector.tensor_scalar(self.dst[:, t, :], self.src[:, t, :], k.mean_var[:, t, 0:1], k.rstd[:, t:t + 1],
                                    ALU.subtract, ALU.mult).then_inc(self.dst_ready, 1)

    def gpsimd(self, pool):
        nc, k = self.nc, self.k
        pool.wait_ge(self.stats_ready, 1)
        nc.gpsimd.tensor_scalar(k.rstd[:, :], k.mean_var[:, :, 1], self.eps, None, ALU.add).then_inc(self.var_ready, 1)
        pool.wait_ge(self.var_ready, 1)
        nc.gpsimd.tensor_tensor(k.rstd[:, :], k.rstd[:, :], k.const("minus_half")[:, 0:NT],
                                ALU.pow).then_inc(self.rstd_ready, 1)


def seen(b, lag):
    return not isinstance(b, int) or b >= lag


def own_wait(eng, k):
    eng.sem_inc(k.passed, 1)


def exists(n, count):
    return not isinstance(n, int) or n < count


def per_batch(eng, body):
    body(0, 0, 0)
    body(1, 0, 1)
    with eng.Fori(1, B // 2 - 1) as pair:
        for par in range(2):
            body(pair * 2 + par, pair, par)
    body(B - 2, B // 2 - 1, 0)
    body(B - 1, B // 2 - 1, 1)


def cross_attention(nc, k):
    ins, ps = k.ins, k.ps
    with ExitStack() as ctx:
        def sb(name, shape, dt=F32):
            return ctx.enter_context(nc.sbuf_tensor("ca_" + name, shape, dt))

        def sem(name):
            return k.sem("ca_" + name)

        wq, wk, wv, wo = (sb(n, [P, C, D]) for n in ("wq", "wk", "wv", "wo"))
        bq, bk, bv = (sb(n, [P, C]) for n in ("bq", "bk", "bv"))
        bo = sb("bo", [1, D])
        lastT = sb("lastT", [P, C, B])
        lastV = sb("lastV", [B, D])
        lastV_by_group = sb("lastV_by_group", [NG, B, D])
        QT = sb("QT", [P, C, B * S])
        attnT = sb("attnT", [P, C, B * S])
        ctxT = sb("ctxT", [P, 2, C, KEYS])
        mask = sb("mask", [P, 2, KEYS], I32)
        hide = sb("hide", [P, 2, KEYS])
        Qblk = sb("Qblk", [P, C, HC, S])
        KT = sb("KT", [P, C, KEYS])
        V = sb("V", [P, 2, KT2, D])
        masked = sb("masked", [P, NG, KEYS])
        top = sb("top", [P, NG])
        nbias = sb("nbias", [P, NG])
        probs = sb("probs", [P, NG, KEYS])
        rowsum = sb("rowsum", [P, 2, NG])
        rinv = sb("rinv", [P, NG])
        PT = sb("PT", [P, NG, KT2, P])
        PTlast = sb("PTlast", [NG, P])
        pick = sb("pick", [P, NG, S])
        blocked = sb("blocked", [P, NG, HG * HD])

        consts_loaded = k.consts_loaded
        x_loaded, weights_loaded = sem("x_loaded"), sem("weights_loaded")
        ctxT_loaded = [sem("ctxT_loaded0"), sem("ctxT_loaded1")]
        mask_loaded = [sem("mask_loaded0"), sem("mask_loaded1")]
        zT = Transpose(nc, k, "ca_z", k.z, k.zT)
        norm = Norm(nc, k, "ca_norm", 1e-5, k.x, k.z, zT.src_ready)
        q_done, qt_ready = sem("q_done"), sem("qt_ready")
        lastv_done, lastv_ready, zeroed, lastv_placed = (
            sem(n) for n in ("lastv_done", "lastv_ready", "zeroed", "lastv_placed"))
        qblk_ready, keys_done, values_done, scores_done = (
            sem(n) for n in ("qblk_ready", "keys_done", "values_done", "scores_done"))
        kt_ready, v_ready, hide_ready, masked_ready = (
            sem(n) for n in ("kt_ready", "v_ready", "hide_ready", "masked_ready"))
        nbias_ready, probs_ready, pt_done = sem("nbias_ready"), sem("probs_ready"), sem("pt_done")
        pt_ready, ptlast_ready, av_done, blocked_ready, attn_done, attn_ready = (
            sem(n) for n in ("pt_ready", "ptlast_ready", "av_done", "blocked_ready", "attn_done", "attn_ready"))
        pick_ready, rinv_ready = sem("pick_ready"), sem("rinv_ready")
        attn_biased, proj_done, order_sem = sem("attn_biased"), sem("proj_done"), sem("vector_order")

        BK, BV, BS, BP, BM = 0, 2, 3, 5, 7
        AV = ps[:, BM, 0:D]
        BESIDE = -(-KEYS // S) * S
        PTL = ps[0:NG, BK, BESIDE:BESIDE + P]
        OT = ps[:, BS + 1, BESIDE:BESIDE + C * S]
        NWEIGHTS = 8 + C

        with nc.Block() as block:
            @block.sync
            def _(sp):
                sp.dma_start(k.x[:, :, :], ins["x"].rearrange("b s d -> (b s) d").rearrange("(t p) d -> p t d", p=P)
                             ).then_inc(x_loaded, 16)
                sp.dma_start(k.consts[:, :], ins["consts"]).then_inc(consts_loaded, 16)
                for t, n in ((wq, "Wq"), (wk, "Wk"), (wv, "Wv"), (wo, "Wo")):
                    sp.dma_start(t[:, :, :], ins["L0_xattn_" + n].rearrange("(c p) n -> p c n", p=P)
                                 ).then_inc(weights_loaded, 16)
                for t, n in ((bq, "bq"), (bk, "bk"), (bv, "bv")):
                    sp.dma_start(t[:, :], ins["L0_xattn_" + n]).then_inc(weights_loaded, 16)
                sp.dma_start(bo[:, :], ins["L0_xattn_bo"].unsqueeze(0)).then_inc(weights_loaded, 16)
                for c in range(C):
                    sp.dma_start(lastT[:, c, :], ins["ctx_lastT"][c * P:(c + 1) * P, :]).then_inc(weights_loaded, 16)

                def load(b, par):
                    sp.dma_start(ctxT[:, par, :, :],
                                 ins["ctxT"][:, bass.ds(b, 1), :].rearrange("(c p) b n -> p (c b) n", p=P)
                                 ).then_inc(ctxT_loaded[par], 16)
                    for h in range(HG):
                        sp.dma_start(mask[h * S:(h + 1) * S, par, :],
                                     ins["mask"][bass.ds(b, 1), 0].rearrange("b q n -> (b q) n")
                                     ).then_inc(mask_loaded[par], 16)
                load(0, 0)
                load(1, 1)
                sp.wait_ge(zeroed, 1)
                sp.wait_ge(lastv_ready, 1)
                for g in range(NG):
                    sp.dma_start(lastV_by_group[g:g + 1, :, g * HG * HD:(g + 1) * HG * HD],
                                 lastV[:, g * HG * HD:(g + 1) * HG * HD]).then_inc(lastv_placed, 16)
                with sp.Fori(0, B // 2 - 1) as pair:
                    for par in range(2):
                        sp.wait_ge(values_done, pair * 2 + par + 1)
                        sp.wait_ge(hide_ready, pair * 2 + par + 1)
                        load(pair * 2 + par + 2, par)

            @block.gpsimd
            def _(pool):
                nc.gpsimd.memset(lastV_by_group[:, :, :], 0.0).then_inc(zeroed, 1)
                pool.wait_ge(consts_loaded, 16)
                norm.gpsimd(pool)

                def body(b, pair, par):
                    pool.wait_ge(mask_loaded[par], 16 * HG * (pair + 1))
                    if seen(b, 2):
                        pool.wait_ge(masked_ready, NG * (b - 1))
                    own_wait(pool, k)
                    nc.gpsimd.tensor_scalar(hide[:, par, :], mask[:, par, :], 0.0, MASKED,
                                            ALU.is_equal, ALU.mult).then_inc(hide_ready, 1)
                per_batch(pool, body)

            @block.tensor
            def _(pe):
                pe.wait_ge(consts_loaded, 16)
                zT.tensor(pe)
                pe.wait_ge(weights_loaded, 16 * NWEIGHTS)

                for c in range(C):
                    last = nc.tensor.matmul(ps[0:B, BM, 0:D], lastT[:, c, :], wv[:, c, :], start=c == 0, stop=c == C - 1)
                last.then_inc(lastv_done, 1)
                pe.wait_ge(zT.ready, 4)
                for m in range(C):
                    for half in range(2):
                        bank = 2 * m + half
                        for c in range(C):
                            last = nc.tensor.matmul(ps[:, bank, :], wq[:, c, m * P:(m + 1) * P],
                                                    k.zT[:, c, half * 512:(half + 1) * 512], start=c == 0, stop=c == C - 1)
                        last.then_inc(q_done, 1)

                def keys(b, pair, par):
                    pe.wait_ge(ctxT_loaded[par], 16 * (pair + 1))
                    if seen(b, 1):
                        pe.wait_ge(kt_ready, C * b)
                    for m in range(C):
                        for c in range(C):
                            last = nc.tensor.matmul(ps[:, BK + m, 0:KEYS], wk[:, c, m * P:(m + 1) * P], ctxT[:, par, c, :],
                                                    start=c == 0, stop=c == C - 1)
                        last.then_inc(keys_done, 1)

                def values(b, par):
                    if seen(b, 1):
                        pe.wait_ge(v_ready, b)
                    for t in range(KT2):
                        for c in range(C):
                            last = nc.tensor.matmul(ps[:, BV, t * D:(t + 1) * D], ctxT[:, par, c, t * P:(t + 1) * P],
                                                    wv[:, c, :], start=c == 0, stop=c == C - 1)
                    last.then_inc(values_done, 1)

                def scores(b, groups):
                    pe.wait_ge(qblk_ready, b + 1)
                    pe.wait_ge(kt_ready, C * b + C)
                    for g in groups:
                        c, j = g // 2, g % 2
                        if g == 1 and seen(b, 2):
                            pe.wait_ge(attn_ready, b - 1)
                        if g >= 2 or seen(b, 1):
                            pe.wait_ge(masked_ready, NG * b + g - 1)
                        nc.tensor.matmul(ps[:, BS + g % 2, 0:KEYS],
                                         Qblk[:, c, j * HG:(j + 1) * HG, :].rearrange("p h q -> p (h q)"),
                                         KT[:, c, :], start=True, stop=True).then_inc(scores_done, 1)

                pe.wait_ge(qt_ready, 4)
                pe.wait_ge(lastv_ready, 1)
                pe.wait_ge(lastv_placed, 16 * NG)
                keys(0, 0, 0)
                values(0, 0)
                scores(0, range(NG))
                keys(1, 0, 1)
                values(1, 1)

                def body(b, pair, par):
                    pe.wait_ge(probs_ready, NG * b + NG)
                    if seen(b, 1):
                        pe.wait_ge(pt_ready, 2 * b)
                        pe.wait_ge(ptlast_ready, b)
                    if exists(b + 1, B):
                        pe.wait_ge(kt_ready, C * b + 2 * C)
                    for g in range(NG):
                        for t in range(KT2):
                            nc.tensor.transpose(ps[:, BP + g // 2, ((g % 2) * KT2 + t) * P:((g % 2) * KT2 + t + 1) * P],
                                                probs[:, g, t * P:(t + 1) * P], k.ident)
                    nc.tensor.transpose(PTL, probs[:, :, KEYS - 1], k.ident).then_inc(pt_done, 1)
                    if exists(b + 1, B):
                        scores(b + 1, range(NG // 2))
                    pe.wait_ge(ptlast_ready, b + 1)
                    own_wait(pe, k)
                    nc.tensor.matmul(AV, PTlast[:, :], lastV_by_group[:, bass.ds(b, 1), :].rearrange("g b d -> g (b d)"),
                                     start=True, stop=False, skip_group_check=True)
                    if exists(b + 1, B):
                        scores(b + 1, range(NG // 2, NG))
                    pe.wait_ge(pt_ready, 2 * b + 2)
                    pe.wait_ge(v_ready, b + 1)
                    for g in range(NG):
                        for t in range(KT2):
                            last = nc.tensor.matmul(ps[:, BM, g * HG * HD:(g + 1) * HG * HD], PT[:, g, t, :],
                                                    V[:, par, t, g * HG * HD:(g + 1) * HG * HD],
                                                    start=False, stop=g == NG - 1 and t == KT2 - 1, skip_group_check=True)
                    last.then_inc(av_done, 1)
                    if exists(b + 2, B):
                        keys(b + 2, pair + 1, par)
                    gather_heads(b)
                    if exists(b + 2, B):
                        values(b + 2, par)

                def gather_heads(b):
                    pe.wait_ge(blocked_ready, b + 1)
                    if seen(b, 1):
                        pe.wait_ge(attn_ready, b)
                    if exists(b + 1, B):
                        pe.wait_ge(masked_ready, NG * b + 2 * NG)
                    for g in range(NG):
                        last = nc.tensor.matmul(OT[(g % 2) * 64:(g % 2) * 64 + 64, (g // 2) * S:(g // 2 + 1) * S],
                                                blocked[:, g, :], pick[:, g, :], start=True, stop=True)
                    last.then_inc(attn_done, 1)

                per_batch(pe, body)
                pe.wait_ge(attn_ready, B)

                pe.wait_ge(attn_biased, 1)
                for t in range(NT):
                    nc.tensor.matmul(ps[:, t, 0:D], k.const("ones")[0:1, :], bo[:, :], start=True, stop=False)
                    for c in range(C):
                        last = nc.tensor.matmul(ps[:, t, 0:D], attnT[:, c, t * P:(t + 1) * P], wo[:, c, :],
                                                start=False, stop=c == C - 1)
                    last.then_inc(proj_done, 1)

            @block.scalar
            def _(act):
                zT.scalar(act)
                act.wait_ge(weights_loaded, 16 * NWEIGHTS)
                act.wait_ge(lastv_done, 1)
                nc.scalar.copy(lastV[:, :], ps[0:B, BM, 0:D]).then_inc(lastv_ready, 1)
                for m in range(C):
                    for half in range(2):
                        act.wait_ge(q_done, 2 * m + half + 1)
                        nc.scalar.activation(QT[:, m, half * 512:(half + 1) * 512], ps[:, 2 * m + half, :], ACT.Identity,
                                             bias=bq[:, m:m + 1]).then_inc(qt_ready, 1)

                def keys_out(b):
                    if seen(b, 1):
                        act.wait_ge(scores_done, NG * b)
                    for m in range(C):
                        act.wait_ge(keys_done, C * b + m + 1)
                        nc.scalar.activation(KT[:, m, :], ps[:, BK + m, 0:KEYS], ACT.Identity,
                                             bias=bk[:, m:m + 1]).then_inc(kt_ready, 1)

                def values_out(b, par):
                    act.wait_ge(values_done, b + 1)
                    if seen(b, 2):
                        act.wait_ge(av_done, b - 1)
                    nc.scalar.copy(V[:, par, :, :].rearrange("p t d -> p (t d)"), ps[:, BV, :]).then_inc(v_ready, 1)

                def exponentials(b, par):
                    act.wait_ge(nbias_ready, b + 1)
                    if seen(b, 2):
                        act.wait_ge(pick_ready, b - 1)
                    for g in range(NG):
                        nc.scalar.activation(probs[:, g, :], masked[:, g, :], ACT.Exp, bias=nbias[:, g:g + 1],
                                             scale=float(HD) ** -0.5, accum_out=rowsum[:, par, g:g + 1]).then_inc(probs_ready, 1)

                keys_out(0)
                values_out(0, 0)
                exponentials(0, 0)
                keys_out(1)
                values_out(1, 1)

                def body(b, pair, par):
                    act.wait_ge(pt_done, b + 1)
                    if seen(b, 1):
                        act.wait_ge(av_done, b)
                    for half in range(2):
                        nc.scalar.copy(PT[:, 2 * half:2 * half + 2, :, :].rearrange("p g t q -> p (g t q)"),
                                       ps[:, BP + half, :]).then_inc(pt_ready, 1)
                    if exists(b + 1, B):
                        exponentials(b + 1, 1 - par)
                    if exists(b + 2, B):
                        keys_out(b + 2)
                        values_out(b + 2, par)
                per_batch(act, body)

            @block.vector
            def _(dve):
                order = Count(dve, order_sem)
                dve.wait_ge(x_loaded, 16)
                norm.vector(dve, order)
                zT.vector(dve)
                dve.wait_ge(qt_ready, 4)

                def block_queries(b):
                    if seen(b, 1):
                        dve.wait_ge(scores_done, NG * b)
                    nc.vector.tensor_tensor(
                        Qblk[:, :, :, :],
                        QT[:, :, bass.ds(b * S, S)].unsqueeze(2).broadcast_to([P, C, HC, S]),
                        k.const("head_of_row").unsqueeze(1).unsqueeze(3).broadcast_to([P, C, HC, S]),
                        ALU.mult).then_inc(qblk_ready, 1)

                def attention_out(b):
                    dve.wait_ge(attn_done, b + 1)
                    nc.vector.tensor_copy(attnT[:, :, bass.ds(b * S, S)],
                                          OT.rearrange("p (c q) -> p c q", c=C)).then_inc(attn_ready, 1)

                def mask_scores(b, par):
                    dve.wait_ge(hide_ready, b + 1)
                    if seen(b, 1):
                        dve.wait_ge(probs_ready, NG * b)
                    for g in range(NG):
                        dve.wait_ge(scores_done, NG * b + g + 1)
                        own_wait(dve, k)
                        nc.vector.tensor_tensor_reduce(out=masked[:, g, :], in0=ps[:, BS + g % 2, 0:KEYS], in1=hide[:, par, :],
                                                       scale=1.0, scalar=-3.0e38, op0=ALU.add, op1=ALU.max,
                                                       accum_out=top[:, g:g + 1]).then_inc(masked_ready, 1)
                    dve.wait_ge(masked_ready, NG * b + NG)
                    nc.vector.tensor_scalar(nbias[:, :], top[:, :], -float(HD) ** -0.5, None, ALU.mult).then_inc(nbias_ready, 1)

                block_queries(0)
                mask_scores(0, 0)
                block_queries(1)

                def body(b, pair, par):
                    dve.wait_ge(pt_done, b + 1)
                    if seen(b, 1):
                        dve.wait_ge(av_done, b)
                    nc.vector.tensor_copy(PTlast[:, :], PTL).then_inc(ptlast_ready, 1)
                    if exists(b + 1, B):
                        mask_scores(b + 1, 1 - par)
                    nc.vector.reciprocal(rinv[:, :], rowsum[:, par, :]).then_inc(rinv_ready, 1)
                    dve.wait_ge(rinv_ready, b + 1)
                    if seen(b, 1):
                        dve.wait_ge(attn_done, b)
                    own_wait(dve, k)
                    nc.vector.tensor_tensor(pick[:, :, :], k.const("query").unsqueeze(1).broadcast_to([P, NG, S]),
                                            rinv[:, :].unsqueeze(2).broadcast_to([P, NG, S]), ALU.mult).then_inc(pick_ready, 1)
                    dve.wait_ge(av_done, b + 1)
                    nc.vector.tensor_tensor(
                        blocked[:, :, :].rearrange("p g (h d) -> p g h d", h=HG),
                        AV.rearrange("p (g h d) -> p g h d", g=NG, h=HG),
                        k.const("group_of_row").unsqueeze(1).unsqueeze(3).broadcast_to([P, NG, HG, HD]),
                        ALU.mult).then_inc(blocked_ready, 1)
                    if exists(b + 2, B):
                        block_queries(b + 2)
                    attention_out(b)
                per_batch(dve, body)
                dve.wait_ge(attn_ready, B)
                for c in range(C):
                    last = nc.vector.tensor_scalar(attnT[:, c, :], attnT[:, c, :], bv[:, c:c + 1], None, ALU.add)
                last.then_inc(attn_biased, 1)
                add_projection(nc, k, dve, proj_done)


def add_projection(nc, k, dve, proj_done):
    for t in range(NT):
        dve.wait_ge(proj_done, t + 1)
        nc.vector.tensor_tensor(k.x[:, t, :], k.ps[:, t, 0:D], k.x[:, t, :], ALU.add)


def self_attention(nc, k, name, weights, scale, windows, rope, bias_name, bias_weight):
    ins, ps = k.ins, k.ps
    W = len(windows)
    with ExitStack() as ctx:
        def sb(n, shape, dt=F32):
            return ctx.enter_context(nc.sbuf_tensor(name + "_" + n, shape, dt))

        def sem(n):
            return k.sem(name + "_" + n)

        wq, wk, wv, wo = (sb(n, [P, C, D]) for n in ("wq", "wk", "wv", "wo"))
        bo = sb("bo", [1, D])
        QT, KT, attnT = (sb(n, [P, C, B * S]) for n in ("QT", "KT", "attnT"))
        V = sb("V", [P, NT, D])
        Qblk = sb("Qblk", [P, C, TB, HC, S])
        Vblk = sb("Vblk", [P, NG, TB, HG * HD])
        shifted = sb("shifted", [P, W, NG * TB, S])
        top = sb("top", [P, W * NG * TB])
        weight = sb("weight", [P, W, NG * TB, S])
        rowsum = sb("rowsum", [P, W * NG * TB])
        rinv = sb("rinv", [P, W, NG * TB])
        probs = sb("probs", [P, NG * TB, S])
        PT = sb("PT", [P, NG, P])
        blocked = sb("blocked", [P, 2, TB, NG, HG * HD])

        zT = Transpose(nc, k, name + "_z", k.z, k.zT)
        norm = Norm(nc, k, name + "_norm", 1e-5, k.x, k.z, zT.src_ready)
        if rope:
            rx, rxT = sb("rx", [P, NT, D]), sb("rxT", [P, C, B * S])
            turned = sb("turned", [P, NT, D])
            rT = Transpose(nc, k, name + "_rope", rx, rxT, bank0=4)
        else:
            rxT, rT = k.zT, zT
        weights_loaded, proj_in_done, proj_in_ready = sem("weights_loaded"), sem("proj_in_done"), sem("proj_in_ready")
        qblk_ready, vblk_ready, scores_done, shifted_ready, centred, weight_ready = (
            sem(n) for n in ("qblk_ready", "vblk_ready", "scores_done", "shifted_ready", "centred", "weight_ready"))
        probs_ready, pt_done, pt_ready, av_done, blocked_ready, attn_done, attn_ready, proj_done = (
            sem(n) for n in ("probs_ready", "pt_done", "pt_ready", "av_done", "blocked_ready", "attn_done",
                             "attn_ready", "proj_done"))
        order_sem = sem("vector_order")
        BS, BP, BA, BO = 0, 2, 3, 7
        GB = NG * TB

        def each_tile(eng, body, order=None, per_tile=0):
            body(0, 0)
            body(1, 1)
            with eng.Fori(1, NT // 2 - 1) as pair:
                if order:
                    order.enter(pair - 1, 2 * per_tile)
                for par in range(2):
                    body(pair * 2 + par, par)
                if order:
                    order.leave(NT // 2 - 2)
            body(NT - 2, 0)
            body(NT - 1, 1)

        with nc.Block() as block:
            @block.sync
            def _(sp):
                for t, src in zip((wq, wk, wv, wo), weights):
                    sp.dma_start(t[:, :, :], src.rearrange("(c p) n -> p c n", p=P)).then_inc(weights_loaded, 16)
                sp.dma_start(bo[:, :], ins[bias_name].unsqueeze(0)).then_inc(weights_loaded, 16)

            @block.gpsimd
            def _(pool):
                norm.gpsimd(pool)

                def block_queries(t):
                    if seen(t, 1):
                        pool.wait_ge(scores_done, t)
                        own_wait(pool, k)
                    for c in range(C):
                        last = nc.gpsimd.tensor_tensor(
                            Qblk[:, c, :, :, :],
                            QT[:, c, bass.ds(t * P, P)].rearrange("p (b q) -> p b q", b=TB).unsqueeze(2)
                            .broadcast_to([P, TB, HC, S]),
                            k.const("head_of_row").unsqueeze(1).unsqueeze(3).broadcast_to([P, TB, HC, S]), ALU.mult)
                    last.then_inc(qblk_ready, 1)

                pool.wait_ge(proj_in_ready, 4)
                block_queries(0)
                block_queries(1)
                pool.wait_ge(proj_in_ready, 16)

                def step(t, par):
                    if seen(t, 1):
                        pool.wait_ge(av_done, t)
                        own_wait(pool, k)
                    nc.gpsimd.tensor_tensor(
                        Vblk[:, :, :, :],
                        V[:, bass.ds(t, 1), :].rearrange("p t (g e) -> p (t g) e", g=NG).unsqueeze(2)
                        .broadcast_to([P, NG, TB, HG * HD]),
                        k.const("group_of_row").unsqueeze(1).unsqueeze(3).broadcast_to([P, NG, TB, HG * HD]),
                        ALU.mult).then_inc(vblk_ready, 1)
                    if exists(t + 2, NT):
                        block_queries(t + 2)
                each_tile(pool, step)

            @block.tensor
            def _(pe):
                zT.tensor(pe)
                if rope:
                    rT.tensor(pe)
                pe.wait_ge(weights_loaded, 16 * 5)
                pe.wait_ge(zT.ready, 4)
                pe.wait_ge(rT.ready, 4)
                for n, w in enumerate((wq, wk)):
                    for m in range(C):
                        for half in range(2):
                            for c in range(C):
                                last = nc.tensor.matmul(ps[:, 4 * n + 2 * m + half, :], w[:, c, m * P:(m + 1) * P],
                                                        rxT[:, c, half * 512:(half + 1) * 512],
                                                        start=c == 0, stop=c == C - 1)
                            last.then_inc(proj_in_done, 1)
                for t in range(NT):
                    pe.wait_ge(proj_in_ready, t + 1)
                    for c in range(C):
                        last = nc.tensor.matmul(ps[:, t, 0:D], k.zT[:, c, t * P:(t + 1) * P], wv[:, c, :],
                                                start=c == 0, stop=c == C - 1)
                    last.then_inc(proj_in_done, 1)
                pe.wait_ge(proj_in_ready, 16)

                def scores(t, par):
                    pe.wait_ge(qblk_ready, t + 1)
                    if seen(t, 2):
                        pe.wait_ge(shifted_ready, W * (t - 1))
                    for g in range(NG):
                        c, j = g // 2, g % 2
                        for b in range(TB):
                            last = nc.tensor.matmul(ps[:, BS + par, (g * TB + b) * S:(g * TB + b + 1) * S],
                                                    Qblk[:, c, b, j * HG:(j + 1) * HG, :].rearrange("p h q -> p (h q)"),
                                                    KT[:, c, bass.ds(t * P + b * S, S)], start=True, stop=True)
                    last.then_inc(scores_done, 1)

                def gather_heads(t, par):
                    pe.wait_ge(blocked_ready, NG * t + NG)
                    if isinstance(t, int) and t:
                        pe.wait_ge(attn_ready, t)
                    for c in range(C):
                        for b in range(TB):
                            last = nc.tensor.matmul(ps[:, BO, (c * TB + b) * S:(c * TB + b + 1) * S],
                                                    blocked[:, par, b, 2 * c:2 * c + 2, :].rearrange("p g e -> p (g e)"),
                                                    k.const("query"), start=True, stop=True)
                    last.then_inc(attn_done, 1)

                def step(t, par):
                    pe.wait_ge(probs_ready, t + 1)
                    if seen(t, 1):
                        pe.wait_ge(pt_ready, t)
                    for g in range(NG):
                        last = nc.tensor.transpose(ps[:, BP, g * P:(g + 1) * P],
                                                   probs[:, g * TB:(g + 1) * TB, :].rearrange("p b s -> p (b s)"), k.ident)
                    last.then_inc(pt_done, 1)
                    if seen(t, 2):
                        gather_heads(t - 2, par)
                    pe.wait_ge(pt_ready, t + 1)
                    pe.wait_ge(vblk_ready, t + 1)
                    if seen(t, 2):
                        pe.wait_ge(blocked_ready, NG * (t - 1))
                    for g in range(NG):
                        last = nc.tensor.matmul(ps[:, BA + 2 * par + g // 2, (g % 2) * D:(g % 2 + 1) * D], PT[:, g, :],
                                                Vblk[:, g, :, :].rearrange("p b e -> p (b e)"), start=True, stop=True)
                    last.then_inc(av_done, 1)
                    if exists(t + 2, NT):
                        scores(t + 2, par)

                scores(0, 0)
                scores(1, 1)
                each_tile(pe, step)
                gather_heads(NT - 2, 0)
                gather_heads(NT - 1, 1)
                pe.wait_ge(attn_ready, NT)
                for t in range(NT):
                    nc.tensor.matmul(ps[:, t, 0:D], bias_weight[0:1, :], bo[:, :], start=True, stop=False)
                    for c in range(C):
                        last = nc.tensor.matmul(ps[:, t, 0:D], attnT[:, c, t * P:(t + 1) * P], wo[:, c, :],
                                                start=False, stop=c == C - 1)
                    last.then_inc(proj_done, 1)

            @block.scalar
            def _(act):
                zT.scalar(act)
                if rope:
                    rT.scalar(act)
                for n, dst in enumerate((QT, KT)):
                    for m in range(C):
                        for half in range(2):
                            act.wait_ge(proj_in_done, 4 * n + 2 * m + half + 1)
                            nc.scalar.copy(dst[:, m, half * 512:(half + 1) * 512],
                                           ps[:, 4 * n + 2 * m + half, :]).then_inc(proj_in_ready, 1)
                for t in range(NT):
                    act.wait_ge(proj_in_done, 8 + t + 1)
                    nc.scalar.copy(V[:, t, :], ps[:, t, 0:D]).then_inc(proj_in_ready, 1)

                def exponentials(t):
                    act.wait_ge(centred, t + 1)
                    nc.scalar.activation(weight[:, :, :, :], shifted[:, :, :, :], ACT.Exp, scale=scale
                                         ).then_inc(weight_ready, 1)

                def attention_out(t):
                    act.wait_ge(attn_done, t + 1)
                    own_wait(act, k)
                    nc.scalar.copy(attnT[:, :, bass.ds(t * P, P)],
                                   ps[:, BO, 0:C * P].rearrange("p (c r) -> p c r", c=C)).then_inc(attn_ready, 1)

                def step(t, par):
                    act.wait_ge(pt_done, t + 1)
                    if seen(t, 1):
                        act.wait_ge(av_done, t)
                    nc.scalar.copy(PT[:, :, :].rearrange("p g r -> p (g r)"), ps[:, BP, :]).then_inc(pt_ready, 1)
                    if seen(t, 2):
                        attention_out(t - 2)
                    if exists(t + 1, NT):
                        exponentials(t + 1)
                exponentials(0)
                each_tile(act, step)
                attention_out(NT - 2)
                attention_out(NT - 1)

            @block.vector
            def _(dve):
                order = Count(dve, order_sem)
                norm.vector(dve, order)
                if rope:
                    dve.wait_ge(zT.src_ready, NT)
                    cos = k.const("cos").unsqueeze(1).broadcast_to([P, NT, D])
                    sin = k.const("sin").rearrange("p (i two) -> p i two", two=2)
                    zp = k.z[:, :, :].rearrange("p t (i two) -> p t i two", two=2)
                    tp = turned[:, :, :].rearrange("p t (i two) -> p t i two", two=2)
                    for side in range(2):
                        last = nc.vector.tensor_tensor(
                            tp[:, :, :, side], zp[:, :, :, 1 - side],
                            sin[:, :, side].unsqueeze(1).broadcast_to([P, NT, D // 2]), ALU.mult)
                    order.after(last)
                    order.after(nc.vector.tensor_tensor(rx[:, :, :], k.z[:, :, :], cos, ALU.mult))
                    for t in range(NT):
                        nc.vector.tensor_tensor(rx[:, t, :], rx[:, t, :], turned[:, t, :], ALU.add
                                                ).then_inc(rT.src_ready, 1)
                zT.vector(dve)
                if rope:
                    rT.vector(dve)

                def centre(t, par):
                    dve.wait_ge(scores_done, t + 1)
                    for w, pen in enumerate(windows):
                        nc.vector.tensor_tensor(shifted[:, w, :, :], ps[:, BS + par, :].rearrange("p (n s) -> p n s", s=S),
                                                pen.unsqueeze(1).broadcast_to([P, GB, S]), ALU.add
                                                ).then_inc(shifted_ready, 1)
                    dve.wait_ge(shifted_ready, W * t + W)
                    flat = shifted[:, :, :, :].rearrange("p w n s -> p (w n) s")
                    order.after(nc.vector.tensor_reduce(top[:, :], flat, AX.X, ALU.max))
                    nc.vector.tensor_tensor(flat, flat, top[:, :].unsqueeze(2).broadcast_to([P, W * GB, S]), ALU.subtract
                                            ).then_inc(centred, 1)

                def probabilities(t):
                    dve.wait_ge(weight_ready, t + 1)
                    order.after(nc.vector.tensor_reduce(rowsum[:, :], weight[:, :, :, :].rearrange("p w n s -> p (w n) s"),
                                                        AX.X, ALU.add))
                    order.after(nc.vector.reciprocal(rinv[:, :, :].rearrange("p w n -> p (w n)"), rowsum[:, :]))
                    if W == 2:
                        order.after(nc.vector.tensor_tensor(rinv[:, :, :], rinv[:, :, :],
                                                            k.const("window_on").unsqueeze(2).broadcast_to([P, W, GB]),
                                                            ALU.mult))
                    if seen(t, 1):
                        dve.wait_ge(pt_done, t)
                    if W == 1:
                        nc.vector.tensor_tensor(probs[:, :, :], weight[:, 0, :, :],
                                                rinv[:, 0, :].unsqueeze(2).broadcast_to([P, GB, S]), ALU.mult
                                                ).then_inc(probs_ready, 1)
                    else:
                        order.after(nc.vector.tensor_tensor(weight[:, :, :, :], weight[:, :, :, :],
                                                            rinv[:, :, :].unsqueeze(3).broadcast_to([P, W, GB, S]), ALU.mult))
                        nc.vector.tensor_tensor(probs[:, :, :], weight[:, 0, :, :], weight[:, 1, :, :], ALU.add
                                                ).then_inc(probs_ready, 1)

                def block_attention(t, par):
                    dve.wait_ge(av_done, t + 1)
                    for g in range(NG):
                        nc.vector.tensor_tensor(
                            blocked[:, par, :, g, :].rearrange("p b (h d) -> p b h d", h=HG),
                            ps[:, BA + 2 * par + g // 2, (g % 2) * D:(g % 2 + 1) * D]
                            .rearrange("p (b h d) -> p b h d", h=HG, d=HD),
                            k.const("group_of_row").unsqueeze(1).unsqueeze(3).broadcast_to([P, TB, HG, HD]),
                            ALU.mult).then_inc(blocked_ready, 1)

                def step(t, par):
                    probabilities(t)
                    if exists(t + 1, NT):
                        centre(t + 1, 1 - par)
                    if seen(t, 1):
                        block_attention(t - 1, 1 - par)
                centre(0, 0)
                each_tile(dve, step, order, 3 if W == 1 else 5)
                block_attention(NT - 1, 1)
                add_projection(nc, k, dve, proj_done)


def local_attention(nc, k):
    w = k.ins["L0_attn_w_qkv"]
    pen = k.const("window_pen").rearrange("p (w s) -> p w s", w=2)
    self_attention(nc, k, "la", [w[:, 0:D], w[:, D:2 * D], w[:, 2 * D:3 * D], k.ins["L0_attn_w_out"]], float(D) ** -0.5,
                   [pen[:, 0, :], pen[:, 1, :]], False, "L0_attn_b_out", k.const("window_count"))


def slot_attention(nc, k):
    ins, ps = k.ins, k.ps
    with ExitStack() as ctx:
        def sb(n, shape, dt=F32):
            return ctx.enter_context(nc.sbuf_tensor("sa_" + n, shape, dt))

        def sem(n):
            return k.sem("sa_" + n)

        def pair_of(f, n, *more):
            return [f(n + str(i), *more) for i in range(2)]

        G = 3 * D
        wq, wk, wv = (sb(n, [P, C, D]) for n in ("wq", "wk", "wv"))
        wihT, whhT, wvi = (sb(n, [P, C, G]) for n in ("wihT", "whhT", "wvi"))
        wqk = sb("wqk", [P, C, D])
        bih, bhh, brz = sb("bih", [1, G]), sb("bhh", [1, G]), sb("brz", [1, 2 * D])
        w_slot, w_in = sb("w_slot", [P, C]), sb("w_in", [P, C])
        last_rows = sb("last_rows", [P, D])
        lastT = sb("lastT", [P, C, P])
        last_st, last_mv, last_ms = sb("last_st", [P, 6]), sb("last_mv", [P, 2]), sb("last_ms", [P, 1])
        rows = pair_of(sb, "rows", [P, TB * KT2, D])
        ctxT = pair_of(sb, "ctxT", [P, C, TB, KEYS])
        cst = pair_of(sb, "cst", [P, TB * KT2, 6])
        cmv = pair_of(sb, "cmv", [P, TB * KT2, 2])
        rms = pair_of(sb, "rms", [P, TB, 3])
        slots = pair_of(sb, "slots", [P, D])
        sst, smv, srs = pair_of(sb, "sst", [P, 6]), pair_of(sb, "smv", [P, 2]), pair_of(sb, "srs", [P, 1])
        normed = pair_of(sb, "normed", [P, D])
        turned = pair_of(sb, "turned", [P, 4, P])
        qT = pair_of(sb, "qT", [P, C, P])
        top, total, inv, invr = (pair_of(sb, n, [P, TB * 3]) for n in ("top", "total", "inv", "invr"))
        e, share, weight = (pair_of(sb, n, [P, TB * 3, S]) for n in ("e", "share", "weight"))
        shifted = pair_of(sb, "shifted", [P, TB * 3, S])
        colinv = pair_of(sb, "colinv", [P, P])
        uT = pair_of(sb, "uT", [P, C, P])
        trz = pair_of(sb, "trz", [P, 2 * D])
        pre, cand, diff = (pair_of(sb, n, [P, D]) for n in ("pre", "cand", "diff"))

        norm = Norm(nc, k, "sa_norm", 1e-5, k.x, k.z)
        weights_loaded, zeroed, last_loaded, fold_done, fold_ready, brz_ready, last_ready = (
            sem(n) for n in ("weights_loaded", "zeroed", "last_loaded", "fold_done", "fold_ready", "brz_ready",
                             "last_ready"))
        ctx_loaded = pair_of(sem, "ctx_loaded")
        (ms_ready, mse_ready, rms_ready, slot_stats, slot_sq, slot_ms, slot_mse, srs_ready, normed_ready, turn_done,
         turn_ready, q_done, q_ready, scores_done, centred, e_ready, inv_ready, share_ready, weight_ready, u_done,
         uT_ready, gates_done, trz_ready, pre_ready, cand_ready, diff_ready) = (
            pair_of(sem, n) for n in (
                "ms_ready", "mse_ready", "rms_ready", "slot_stats", "slot_sq", "slot_ms", "slot_mse", "srs_ready",
                "normed_ready", "turn_done", "turn_ready", "q_done", "q_ready", "scores_done", "centred", "e_ready",
                "inv_ready", "share_ready", "weight_ready", "u_done", "uT_ready", "gates_done", "trz_ready",
                "pre_ready", "cand_ready", "diff_ready"))
        slots_set = sem("slots_set")
        order_sem, tile_sem = sem("vector_order"), sem("vector_tile_order")
        ROUNDS, PAIRS = 3, NT // 2
        BA, BB, BR, BN = 0, 1, 2, 3

        def bank(par, n):
            return ps[:, 4 * par + n, :]

        def rounds(eng, before, body, after):
            with eng.Fori(0, PAIRS) as pair:
                before(pair)
                with eng.Fori(0, ROUNDS) as r:
                    body(pair * ROUNDS + r)
                after(pair)

        def nothing(pair):
            pass

        with nc.Block() as block:
            @block.sync
            def _(sp):
                for t, n in ((wq, "Wq"), (wk, "Wk"), (wv, "Wv"), (wihT, "gru_wihT"), (whhT, "gru_whhT")):
                    sp.dma_start(t[:, :, :], ins["L1_xattn_" + n].rearrange("(c p) n -> p c n", p=P)
                                 ).then_inc(weights_loaded, 16)
                for t, n in ((bih, "gru_bih"), (bhh, "gru_bhh")):
                    sp.dma_start(t[:, :], ins["L1_xattn_" + n].unsqueeze(0)).then_inc(weights_loaded, 16)
                for t, n in ((w_slot, "slot_norm_w"), (w_in, "input_norm_w")):
                    sp.dma_start(t[:, :], ins["L1_xattn_" + n]).then_inc(weights_loaded, 16)
                sp.wait_ge(zeroed, 2)
                sp.dma_start(last_rows[0:B, :], ins["ctx"][:, KEYS - 1, :]).then_inc(last_loaded, 16)
                for c in range(C):
                    sp.dma_start(lastT[:, c, 0:B], ins["ctx_lastT"][c * P:(c + 1) * P, :]).then_inc(last_loaded, 16)

                def load(pair, par):
                    tile = pair * 2 + par
                    for b in range(TB):
                        sp.dma_start(rows[par][:, b * KT2:(b + 1) * KT2, :],
                                     ins["ctx"][bass.ds(tile * TB + b, 1), 0:KT2 * P, :]
                                     .rearrange("b (t p) d -> p (b t) d", p=P)).then_inc(ctx_loaded[par], 16)
                    for c in range(C):
                        sp.dma_start(ctxT[par][:, c, :, :],
                                     ins["ctxT"][c * P:(c + 1) * P, bass.ds(tile * TB, TB), :]
                                     ).then_inc(ctx_loaded[par], 16)
                load(0, 0)
                load(0, 1)
                with sp.Fori(1, PAIRS) as pair:
                    for par in range(2):
                        sp.wait_ge(u_done[par], pair * ROUNDS)
                        sp.wait_ge(ms_ready[par], pair)
                        load(pair, par)

            @block.gpsimd
            def _(pool):
                nc.gpsimd.memset(last_rows[:, :], 0.0).then_inc(zeroed, 1)
                nc.gpsimd.memset(lastT[:, :, :], 0.0).then_inc(zeroed, 1)
                norm.gpsimd(pool)

                def before(pair):
                    for par in range(2):
                        pool.wait_ge(ms_ready[par], pair + 1)
                        own_wait(pool, k)
                        nc.gpsimd.tensor_scalar(rms[par][:, :, :], rms[par][:, :, :], 1e-6, None, ALU.add
                                                ).then_inc(mse_ready[par], 1)
                        pool.wait_ge(mse_ready[par], pair + 1)
                        own_wait(pool, k)
                        nc.gpsimd.tensor_tensor(rms[par][:, :, :].rearrange("p b t -> p (b t)"),
                                                rms[par][:, :, :].rearrange("p b t -> p (b t)"),
                                                k.const("minus_half")[:, 0:TB * 3], ALU.pow).then_inc(rms_ready[par], 1)

                def body(n):
                    for par in range(2):
                        pool.wait_ge(slot_stats[par], n + 1)
                        own_wait(pool, k)
                        nc.gpsimd.tensor_tensor(srs[par][:, :], smv[par][:, 0:1], smv[par][:, 0:1], ALU.mult
                                                ).then_inc(slot_sq[par], 1)
                        pool.wait_ge(slot_sq[par], n + 1)
                        own_wait(pool, k)
                        nc.gpsimd.tensor_tensor(srs[par][:, :], srs[par][:, :], smv[par][:, 1:2], ALU.add
                                                ).then_inc(slot_ms[par], 1)
                        pool.wait_ge(slot_ms[par], n + 1)
                        own_wait(pool, k)
                        nc.gpsimd.tensor_scalar(srs[par][:, :], srs[par][:, :], 1e-6, None, ALU.add
                                                ).then_inc(slot_mse[par], 1)
                        pool.wait_ge(slot_mse[par], n + 1)
                        own_wait(pool, k)
                        nc.gpsimd.tensor_tensor(srs[par][:, :], srs[par][:, :], k.const("minus_half")[:, 0:1], ALU.pow
                                                ).then_inc(srs_ready[par], 1)
                    for par in range(2):
                        pool.wait_ge(inv_ready[par], n + 1)
                        own_wait(pool, k)
                        nc.gpsimd.tensor_tensor(weight[par][:, :, :], e[par][:, :, :],
                                                invr[par][:, :].unsqueeze(2).broadcast_to([P, TB * 3, S]), ALU.mult
                                                ).then_inc(weight_ready[par], 1)
                    for par in range(2):
                        pool.wait_ge(cand_ready[par], n + 1)
                        own_wait(pool, k)
                        nc.gpsimd.tensor_tensor(diff[par][:, :], slots[par][:, :], cand[par][:, :], ALU.subtract
                                                ).then_inc(diff_ready[par], 1)
                rounds(pool, before, body, nothing)

            @block.tensor
            def _(pe):
                pe.wait_ge(weights_loaded, 16 * 9)
                for m in range(C):
                    for c in range(C):
                        last = nc.tensor.matmul(ps[:, m, 0:D], wq[:, c, m * P:(m + 1) * P], wk[:, c, :],
                                                start=c == 0, stop=c == C - 1)
                    last.then_inc(fold_done, 1)
                for m in range(C):
                    for j, (lo, hi) in enumerate(((0, 2 * D), (2 * D, 3 * D))):
                        for c in range(C):
                            last = nc.tensor.matmul(ps[:, 2 + 2 * m + j, 0:hi - lo], wv[:, c, m * P:(m + 1) * P],
                                                    wihT[:, c, lo:hi], start=c == 0, stop=c == C - 1)
                        last.then_inc(fold_done, 1)
                pe.wait_ge(fold_ready, 6)
                pe.wait_ge(brz_ready, 1)
                pe.wait_ge(last_loaded, 16 * 3)

                def before(pair):
                    for par in range(2):
                        pe.wait_ge(ctx_loaded[par], 16 * 6 * (pair + 1))
                    own_wait(pe, k)

                def body(n):
                    for par in range(2):
                        pe.wait_ge(normed_ready[par], n + 1)
                        for i, src in enumerate((normed[par], slots[par])):
                            for c in range(C):
                                last = nc.tensor.transpose(bank(par, BA)[:, (2 * i + c) * P:(2 * i + c + 1) * P],
                                                           src[:, c * P:(c + 1) * P], k.ident)
                        last.then_inc(turn_done[par], 1)
                    for par in range(2):
                        pe.wait_ge(turn_ready[par], n + 1)
                        for m in range(C):
                            for c in range(C):
                                last = nc.tensor.matmul(bank(par, BB)[:, m * P:(m + 1) * P], wqk[:, c, m * P:(m + 1) * P],
                                                        turned[par][:, c, :], start=c == 0, stop=c == C - 1)
                        last.then_inc(q_done[par], 1)
                    for par in range(2):
                        pe.wait_ge(q_ready[par], 2 * n + 2)
                        for b in range(TB):
                            for t in range(KT2):
                                for c in range(C):
                                    nc.tensor.matmul(bank(par, BA)[:, (b * 3 + t) * S:(b * 3 + t + 1) * S],
                                                     ctxT[par][:, c, b, t * P:(t + 1) * P],
                                                     qT[par][:, c, b * S:(b + 1) * S], start=c == 0, stop=c == C - 1)
                        lastcol = bank(par, BA)[:, 0:TB * 3 * S].rearrange("p (b t s) -> p b t s", b=TB, t=3)[:, :, 2, :]
                        for c in range(C):
                            last = nc.tensor.matmul(lastcol, lastT[:, c, :], qT[par][:, c, :].rearrange("p (b s) -> p b s", b=TB),
                                                    start=c == 0, stop=c == C - 1)
                        last.then_inc(scores_done[par], 1)
                        nc.tensor.matmul(bank(par, BR), k.const("ones")[0:1, :], brz[:, :], start=True, stop=False)
                        for c in range(C):
                            nc.tensor.matmul(bank(par, BR), turned[par][:, 2 + c, :], whhT[:, c, 0:2 * D],
                                             start=False, stop=False)
                        nc.tensor.matmul(bank(par, BN)[:, D:2 * D], k.const("ones")[0:1, :], bhh[:, 2 * D:3 * D],
                                         start=True, stop=False)
                        for c in range(C):
                            nc.tensor.matmul(bank(par, BN)[:, D:2 * D], turned[par][:, 2 + c, :], whhT[:, c, 2 * D:3 * D],
                                             start=False, stop=c == C - 1)
                    for par in range(2):
                        pe.wait_ge(share_ready[par], n + 1)
                        grid = share[par][:, :, :].rearrange("p (b t) s -> p b t s", t=3)
                        for t in range(3):
                            nc.tensor.matmul(bank(par, BB)[:, 2 * P:3 * P], k.const("ones"), grid[:, :, t, :],
                                             start=t == 0, stop=t == 2)
                        pe.wait_ge(weight_ready[par], n + 1)
                        grid = weight[par][:, :, :].rearrange("p (b t) s -> p b t s", t=3)
                        for c in range(C):
                            nc.tensor.matmul(bank(par, BB)[:, c * P:(c + 1) * P], last_rows[:, c * P:(c + 1) * P],
                                             grid[:, :, 2, :], start=True, stop=False, skip_group_check=True)
                            for b in range(TB):
                                for t in range(KT2):
                                    last = nc.tensor.matmul(
                                        bank(par, BB)[:, c * P + b * S:c * P + (b + 1) * S],
                                        rows[par][:, b * KT2 + t, c * P:(c + 1) * P], weight[par][:, b * 3 + t, :],
                                        start=False, stop=b == TB - 1 and t == KT2 - 1, skip_group_check=True)
                        last.then_inc(u_done[par], 1)
                    for par in range(2):
                        pe.wait_ge(uT_ready[par], n + 1)
                        for c in range(C):
                            nc.tensor.matmul(bank(par, BR), uT[par][:, c, :], wvi[:, c, 0:2 * D],
                                             start=False, stop=c == C - 1)
                        nc.tensor.matmul(bank(par, BN)[:, 0:D], k.const("ones")[0:1, :], bih[:, 2 * D:3 * D],
                                         start=True, stop=False)
                        for c in range(C):
                            last = nc.tensor.matmul(bank(par, BN)[:, 0:D], uT[par][:, c, :], wvi[:, c, 2 * D:3 * D],
                                                    start=False, stop=c == C - 1)
                        last.then_inc(gates_done[par], 1)
                rounds(pe, before, body, nothing)

            @block.scalar
            def _(act):
                act.wait_ge(weights_loaded, 16 * 9)
                for m in range(C):
                    act.wait_ge(fold_done, m + 1)
                    nc.scalar.activation(wqk[:, m, :], ps[:, m, 0:D], ACT.Copy, scale=w_slot[:, m:m + 1]
                                         ).then_inc(fold_ready, 1)
                for m in range(C):
                    for j, (lo, hi) in enumerate(((0, 2 * D), (2 * D, 3 * D))):
                        act.wait_ge(fold_done, 2 + 2 * m + j + 1)
                        nc.scalar.activation(wvi[:, m, lo:hi], ps[:, 2 + 2 * m + j, 0:hi - lo], ACT.Copy,
                                             scale=w_in[:, m:m + 1]).then_inc(fold_ready, 1)

                def body(n):
                    for par in range(2):
                        act.wait_ge(turn_done[par], n + 1)
                        nc.scalar.copy(turned[par][:, :, :].rearrange("p c n -> p (c n)"), bank(par, BA)
                                       ).then_inc(turn_ready[par], 1)
                    for par in range(2):
                        act.wait_ge(q_done[par], n + 1)
                        for m in range(C):
                            nc.scalar.activation(qT[par][:, m, :], bank(par, BB)[:, m * P:(m + 1) * P], ACT.Copy,
                                                 scale=w_in[:, m:m + 1]).then_inc(q_ready[par], 1)
                    for par in range(2):
                        act.wait_ge(centred[par], n + 1)
                        nc.scalar.activation(e[par][:, :, :], shifted[par][:, :, :], ACT.Exp, scale=float(D) ** -0.5
                                             ).then_inc(e_ready[par], 1)
                    for par in range(2):
                        act.wait_ge(gates_done[par], n + 1)
                        nc.scalar.activation(trz[par][:, :], bank(par, BR), ACT.Tanh, scale=0.5).then_inc(trz_ready[par], 1)
                        act.wait_ge(pre_ready[par], n + 1)
                        nc.scalar.activation(cand[par][:, :], pre[par][:, :], ACT.Tanh).then_inc(cand_ready[par], 1)
                rounds(act, nothing, body, nothing)

            @block.vector
            def _(dve):
                order, tile_order = Count(dve, order_sem), Count(dve, tile_sem)
                norm.vector(dve, tile_order)
                dve.wait_ge(norm.dst_ready, NT)
                dve.wait_ge(weights_loaded, 16 * 9)
                nc.vector.tensor_tensor(brz[:, :], bih[:, 0:2 * D], bhh[:, 0:2 * D], ALU.add).then_inc(brz_ready, 1)
                dve.wait_ge(last_loaded, 16 * 3)
                tile_order.after(nc.vector.bn_stats(last_st[:, :], last_rows[:, :]))
                tile_order.after(nc.vector.bn_aggr(last_mv[:, :], last_st[:, :]))
                tile_order.after(nc.vector.scalar_tensor_tensor(out=last_ms[:, :], in0=last_mv[:, 0:1], scalar=last_mv[:, 0:1],
                                                                in1=last_mv[:, 1:2], op0=ALU.mult, op1=ALU.add))

                def before(pair):
                    tile_order.enter(pair, 2 * 3)
                    for par in range(2):
                        dve.wait_ge(ctx_loaded[par], 16 * 6 * (pair + 1))
                        for n in range(TB * KT2):
                            last = nc.vector.bn_stats(cst[par][:, n, :], rows[par][:, n, :])
                        tile_order.after(last)
                        own_wait(dve, k)
                        for n in range(TB * KT2):
                            last = nc.vector.bn_aggr(cmv[par][:, n, :], cst[par][:, n, :])
                        tile_order.after(last)
                        mean = cmv[par][:, :, 0].rearrange("p (b t) -> p b t", b=TB)
                        tile_order.after(nc.vector.tensor_tensor(rms[par][:, :, 0:KT2], mean, mean, ALU.mult))
                        nc.vector.tensor_tensor(rms[par][:, :, 0:KT2], rms[par][:, :, 0:KT2],
                                                cmv[par][:, :, 1].rearrange("p (b t) -> p b t", b=TB), ALU.add)
                        nc.vector.tensor_copy(rms[par][:, :, 2], last_ms[:, :].broadcast_to([P, TB])
                                              ).then_inc(ms_ready[par], 1)
                        nc.vector.tensor_copy(slots[par][:, :], k.z[:, bass.ds(pair * 2 + par, 1), :]
                                              .rearrange("p t d -> p (t d)")).then_inc(slots_set, 1)
                    dve.wait_ge(slots_set, 2 * pair + 2)
                    for par in range(2):
                        dve.wait_ge(rms_ready[par], pair + 1)
                    own_wait(dve, k)
                    tile_order.leave_open()

                def body(n):
                    order.enter(n, 2 * 1 + 2 * 2 + 2 * 3 + 2 * 2 + 2 * 1 + 2 * 2)
                    for par in range(2):
                        order.after(nc.vector.bn_stats(sst[par][:, :], slots[par][:, :]))
                        own_wait(dve, k)
                        nc.vector.bn_aggr(smv[par][:, :], sst[par][:, :]).then_inc(slot_stats[par], 1)
                    for par in range(2):
                        dve.wait_ge(srs_ready[par], n + 1)
                        nc.vector.tensor_scalar(normed[par][:, :], slots[par][:, :], srs[par][:, :], None, ALU.mult
                                                ).then_inc(normed_ready[par], 1)
                    for par in range(2):
                        dve.wait_ge(scores_done[par], n + 1)
                        sc = bank(par, BA)[:, 0:TB * 3 * S].rearrange("p (n s) -> p n s", s=S)
                        wide = [P, TB * 3, S]
                        order.after(nc.vector.tensor_reduce(top[par][:, :], sc, AX.X, ALU.max))
                        order.after(nc.vector.tensor_tensor(shifted[par][:, :, :], sc, top[par][:, :].unsqueeze(2)
                                                            .broadcast_to(wide), ALU.subtract))
                        nc.vector.tensor_tensor(shifted[par][:, :, :], shifted[par][:, :, :],
                                                rms[par][:, :, :].rearrange("p b t -> p (b t)").unsqueeze(2)
                                                .broadcast_to(wide), ALU.mult).then_inc(centred[par], 1)

                def round_(pair, n):
                    for par in range(2):
                        wide = [P, TB * 3, S]
                        dve.wait_ge(e_ready[par], n + 1)
                        order.after(nc.vector.tensor_reduce(total[par][:, :], e[par][:, :, :], AX.X, ALU.add))
                        order.after(nc.vector.reciprocal(inv[par][:, :], total[par][:, :]))
                        order.after(nc.vector.tensor_tensor(inv[par][:, :], inv[par][:, :],
                                                            k.const("last_key")[:, bass.ds((pair * 2 + par) * TB * 3, TB * 3)],
                                                            ALU.mult))
                        nc.vector.tensor_tensor(invr[par][:, :], inv[par][:, :],
                                                rms[par][:, :, :].rearrange("p b t -> p (b t)"), ALU.mult
                                                ).then_inc(inv_ready[par], 1)
                        nc.vector.tensor_tensor(share[par][:, :, :], e[par][:, :, :],
                                                inv[par][:, :].unsqueeze(2).broadcast_to(wide), ALU.mult
                                                ).then_inc(share_ready[par], 1)
                    for par in range(2):
                        dve.wait_ge(u_done[par], n + 1)
                        order.after(nc.vector.tensor_scalar(colinv[par][:, :], bank(par, BB)[:, 2 * P:3 * P], 1e-6, None,
                                                            ALU.add))
                        order.after(nc.vector.reciprocal(colinv[par][:, :], colinv[par][:, :]))
                        nc.vector.tensor_tensor(uT[par][:, :, :], bank(par, BB)[:, 0:2 * P].rearrange("p (c n) -> p c n", c=C),
                                                colinv[par][:, :].unsqueeze(1).broadcast_to([P, C, P]), ALU.mult
                                                ).then_inc(uT_ready[par], 1)
                    for par in range(2):
                        dve.wait_ge(trz_ready[par], n + 1)
                        order.after(nc.vector.scalar_tensor_tensor(out=pre[par][:, :], in0=trz[par][:, 0:D], scalar=1.0,
                                                                   in1=bank(par, BN)[:, D:2 * D], op0=ALU.add, op1=ALU.mult))
                        nc.vector.scalar_tensor_tensor(out=pre[par][:, :], in0=pre[par][:, :], scalar=0.5,
                                                       in1=bank(par, BN)[:, 0:D], op0=ALU.mult, op1=ALU.add
                                                       ).then_inc(pre_ready[par], 1)
                    for par in range(2):
                        dve.wait_ge(diff_ready[par], n + 1)
                        order.after(nc.vector.scalar_tensor_tensor(out=diff[par][:, :], in0=trz[par][:, D:2 * D], scalar=1.0,
                                                                   in1=diff[par][:, :], op0=ALU.add, op1=ALU.mult))
                        order.after(nc.vector.scalar_tensor_tensor(out=slots[par][:, :], in0=diff[par][:, :], scalar=0.5,
                                                                   in1=cand[par][:, :], op0=ALU.mult, op1=ALU.add))
                    order.leave_open()

                with dve.Fori(0, PAIRS) as pair:
                    before(pair)
                    with dve.Fori(0, ROUNDS) as r:
                        n = pair * ROUNDS + r
                        body(n)
                        round_(pair, n)
                    for par in range(2):
                        tile = bass.ds(pair * 2 + par, 1)
                        nc.vector.tensor_tensor(k.x[:, tile, :].rearrange("p t d -> p (t d)"),
                                                k.x[:, tile, :].rearrange("p t d -> p (t d)"), slots[par][:, :], ALU.add)


def causal_attention(nc, k):
    self_attention(nc, k, "ra", [k.ins["L1_attn_" + n] for n in ("WqT", "WkT", "WvT", "WoT")], float(HD) ** -0.5,
                   [k.const("causal_pen")], True, "L1_attn_bo", k.const("ones"))


def per_slot(eng, body):
    body(0, 0, 0, True)
    body(1, 0, 1, True)
    with eng.Fori(1, SLOTS // 2) as pair:
        for par in range(2):
            body(pair * 2 + par, pair, par, True)
    body(SLOTS - 1, SLOTS // 2, 0, False)


def experts(nc, k, name, gated):
    ins, ps = k.ins, k.ps
    pre = "L1_ffn_" if gated else "L0_ffn_"
    with ExitStack() as ctx:
        def sb(n, shape, dt=F32):
            return ctx.enter_context(nc.sbuf_tensor(name + "_" + n, shape, dt))

        def sem(n):
            return k.sem(name + "_" + n)

        w_route = sb("w_route", [P, C, E])
        b_route = sb("b_route", [P, E])
        logits, rest, tie, first, second, both = (
            sb(n, [P, NT, E]) for n in ("logits", "rest", "tie", "first", "second", "both"))
        best = sb("best", [P, 4, NT])
        gap, share1, share2 = (sb(n, [P, NT]) for n in ("gap", "share1", "share2"))
        counted = sb("counted", [P, 2, NT, E])
        earlier = sb("earlier", [P, NT + 1, E])
        over = sb("over", [P, E, SLOTS_EACH])
        slots_of = sb("slots_of", [P, E])
        start_of = sb("start_of", [P, E])
        place = sb("place", [P, NT, E])
        at = sb("at", [P, 2, NT])
        row = sb("row", [P, 2, NT], I32)
        begun = sb("begun", [P, SLOTS, E])
        expert_f = sb("expert_f", [P, SLOTS])
        expert = sb("expert", [P, SLOTS], I32)

        win = [sb("win%d" % i, [P, 2, C, FF]) for i in range(1 + gated)]
        bin_ = [sb("bin%d" % i, [P, 2, FF // P]) for i in range(1 + gated)]
        wout = sb("wout", [P, 2, FF // P, D])
        bout = sb("bout", [P, 2, D])
        rows = sb("rows", [P, 2, SLOT // P, D])
        xT = sb("xT", [P, C, SLOT])
        hT = sb("hT", [P, 2, FF // P, SLOT])
        y = sb("y", [P, 2, SLOT // P, D])
        mixed1, mixed2 = sb("mixed1", [P, NT, D]), sb("mixed2", [P, NT, D])
        if gated:
            halfb = sb("halfb", [P, 2, FF // P])
            gelu, tanh = (sb(n, [P, 2, SLOT]) for n in ("gelu", "tanh"))
            g_e, b_e = sb("g_e", [P, 2, D]), sb("b_e", [P, 2, D])
            rbias = sb("rbias", [P, 2, SLOT // P, D])
            resid = sb("resid", [P, SLOT // P, D])
            st = sb("st", [P, SLOT // P, 6])
            mv = sb("mv", [P, SLOT // P, 2])
            rs = sb("rs", [P, SLOT // P])
        else:
            gamma, beta = sb("gamma", [P, D]), sb("beta", [P, D])

        zT = Transpose(nc, k, name + "_z", k.z, k.zT)
        norm = Norm(nc, k, name + "_norm", 1e-5, k.x, k.z, zT.src_ready)
        norm2 = None if gated else Norm(nc, k, name + "_norm2", 1e-5, mixed1, mixed1)
        route_loaded = sem("route_loaded")
        small_loaded, logits_done, gap_ready, exp_ready, both_ready, counted_done, rows_known, scattered = (
            sem(n) for n in ("small_loaded", "logits_done", "gap_ready", "exp_ready", "both_ready", "counted_done",
                             "rows_known", "scattered"))
        rows_loaded, in_loaded, out_loaded = (
            [sem(n + "0"), sem(n + "1")] for n in ("rows_loaded", "in_loaded", "out_loaded"))
        xt_done, xt_ready, h_done, h_ready, y_done, y_read, y_ready = (
            sem(n) for n in ("xt_done", "xt_ready", "h_done", "h_ready", "y_done", "y_read", "y_ready"))
        y_stored = [sem("y_stored0"), sem("y_stored1")]
        gathered = [sem("gathered0"), sem("gathered1")]
        order_sem = sem("vector_order")
        if gated:
            halfb_ready, act_done, rbias_ready = (
                sem(n) for n in ("halfb_ready", "act_done", "rbias_ready"))
            rstats_ready, rvar_ready, rrstd_ready = (sem(n) for n in ("rstats_ready", "rvar_ready", "rrstd_ready"))
        HB, XB, YB = 0, 4, 5
        HC_N = FF // P
        PER_IN, PER_OUT = (4, 4) if gated else (2, 2)
        ff_names = ("Wi", "Wg") if gated else ("W1",)
        fb_names = ("bi", "bg") if gated else ("b1",)
        out_w, out_b = ("Wo", "bo") if gated else ("W2", "b2")

        with nc.Block() as block:
            @block.sync
            def _(sp):
                sp.dma_start(w_route[:, :, :], ins[pre + ("Wr" if gated else "Wg")].rearrange("(c p) n -> p c n", p=P)
                             ).then_inc(route_loaded, 16)
                sp.dma_start(b_route[:, :], ins[pre + ("br" if gated else "bg")].partition_broadcast(P)).then_inc(route_loaded, 16)
                if not gated:
                    sp.dma_start(gamma[:, :], ins[pre + "gamma"].partition_broadcast(P)).then_inc(small_loaded, 16)
                    sp.dma_start(beta[:, :], ins[pre + "beta"].partition_broadcast(P)).then_inc(small_loaded, 16)
                sp.wait_ge(rows_known, 1)

                def load_in(s, par):
                    one = bass.ds(sp.value_load(expert[0:1, bass.ds(s, 1)], min_val=0, max_val=E - 1), 1)
                    for n, t in zip(ff_names, win):
                        sp.dma_start(t[:, par, :, :], ins[pre + n][one, :, :].rearrange("e (c p) h -> p (e c) h", p=P)
                                     ).then_inc(in_loaded[par], 16)
                    for n, t in zip(fb_names, bin_):
                        sp.dma_start(t[:, par, :], ins[pre + n][one, :, :].rearrange("e p n -> p (e n)")
                                     ).then_inc(in_loaded[par], 16)

                def load_out(s, par):
                    one = bass.ds(sp.value_load(expert[0:1, bass.ds(s, 1)], min_val=0, max_val=E - 1), 1)
                    sp.dma_start(wout[:, par, :, :], ins[pre + out_w][one, :, :].rearrange("e (c p) d -> p (e c) d", p=P)
                                 ).then_inc(out_loaded[par], 16)
                    for n, t in [(out_b, bout)] + ([("gamma", g_e), ("beta", b_e)] if gated else []):
                        sp.dma_start(t[:, par, :], ins[pre + n][one, :].rearrange("e d -> (e d)").partition_broadcast(P)
                                     ).then_inc(out_loaded[par], 16)

                def load_rows(s, par):
                    sp.dma_start(rows[:, par, :, :], k.sorted_x.ap()[bass.ds(s * SLOT, SLOT), :]
                                 .rearrange("(t p) d -> p t d", p=P)).then_inc(rows_loaded[par], 16)

                def load_ahead(s, par):
                    sp.wait_ge(h_ready, HC_N * s + HC_N)
                    own_wait(sp, k)
                    if gated:
                        sp.wait_ge(rbias_ready, s + 1)
                        own_wait(sp, k)
                    load_rows(s + 2, par)
                    load_in(s + 2, par)

                def store(s, par):
                    sp.wait_ge(y_ready, s + 1)
                    sp.dma_start(k.sorted_y.ap()[bass.ds(s * SLOT, SLOT), :].rearrange("(t p) d -> p t d", p=P),
                                 y[:, par, :, :]).then_inc(y_stored[par], 16)
                load_in(0, 0)
                load_out(0, 0)
                load_in(1, 1)
                sp.wait_ge(scattered, 16 * 2 * NT)
                for par in range(2):
                    load_rows(par, par)
                load_out(1, 1)
                with sp.Fori(0, SLOTS // 2 - 1) as pair:
                    for par in range(2):
                        load_ahead(pair * 2 + par, par)
                        store(pair * 2 + par, par)
                        load_out(pair * 2 + par + 2, par)
                load_ahead(SLOTS - 3, 0)
                store(SLOTS - 3, 0)
                load_out(SLOTS - 1, 0)
                store(SLOTS - 2, 1)
                store(SLOTS - 1, 0)
                for par in range(2):
                    sp.wait_ge(y_stored[par], 16 * ((SLOTS + 1 - par) // 2))

            @block.gpsimd
            def _(pool):
                norm.gpsimd(pool)
                pool.wait_ge(k.cleared, 16 * 2 * SLOTS)
                pool.wait_ge(rows_known, 1)
                for t in range(NT):
                    for way in range(2):
                        pool.indirect_dma_start(out=k.sorted_x.ap(), in_=k.z[:, t, :], in_offset=None,
                                                out_offset=bass.IndirectOffsetOnAxis(ap=row[:, way, t:t + 1], axis=0)
                                                ).then_inc(scattered, 16)
                if gated:
                    def prepare(s, pair, par):
                        pool.wait_ge(in_loaded[par], 16 * PER_IN * (pair + 1))
                        if seen(s, 2):
                            pool.wait_ge(y_ready, s - 1)
                        own_wait(pool, k)
                        nc.gpsimd.tensor_scalar(halfb[:, par, :], bin_[1][:, par, :], 0.5, None, ALU.mult
                                                ).then_inc(halfb_ready, 1)
                        pool.wait_ge(rows_loaded[par], 16 * (pair + 1))
                        pool.wait_ge(out_loaded[par], 16 * PER_OUT * (pair + 1))
                        own_wait(pool, k)
                        nc.gpsimd.tensor_tensor(rbias[:, par, :, :], rows[:, par, :, :],
                                                bout[:, par, :].unsqueeze(1).broadcast_to([P, SLOT // P, D]), ALU.add
                                                ).then_inc(rbias_ready, 1)
                    prepare(0, 0, 0)

                    def body(s, pair, par, has_next):
                        if has_next:
                            prepare(s + 1, pair if par == 0 else pair + 1, 1 - par)
                        pool.wait_ge(rstats_ready, s + 1)
                        own_wait(pool, k)
                        nc.gpsimd.tensor_scalar(rs[:, :], mv[:, :, 1], 1e-12, None, ALU.add).then_inc(rvar_ready, 1)
                        pool.wait_ge(rvar_ready, s + 1)
                        own_wait(pool, k)
                        nc.gpsimd.tensor_tensor(rs[:, :], rs[:, :], k.const("minus_half")[:, 0:SLOT // P], ALU.pow
                                                ).then_inc(rrstd_ready, 1)
                    per_slot(pool, body)
                for par in range(2):
                    pool.wait_ge(y_stored[par], 16 * ((SLOTS + 1 - par) // 2))
                for way, dst in enumerate((mixed1, mixed2)):
                    for t in range(NT):
                        pool.indirect_dma_start(out=dst[:, t, :], out_offset=None, in_=k.sorted_y.ap(),
                                                in_offset=bass.IndirectOffsetOnAxis(ap=row[:, way, t:t + 1], axis=0)
                                                ).then_inc(gathered[way], 16)
                if not gated:
                    norm2.gpsimd(pool)

            @block.tensor
            def _(pe):
                zT.tensor(pe)
                pe.wait_ge(route_loaded, 16 * 2)
                pe.wait_ge(zT.ready, 4)
                for t in range(NT):
                    dst = ps[:, 4, t * E:(t + 1) * E]
                    for c in range(C):
                        last = nc.tensor.matmul(dst, k.zT[:, c, t * P:(t + 1) * P], w_route[:, c, :],
                                                start=c == 0, stop=c == C - 1)
                last.then_inc(logits_done, 1)
                pe.wait_ge(both_ready, 1)
                chosen = both[:, :, :].rearrange("p t e -> p (t e)")
                nc.tensor.matmul(ps[:, 5, 0:NT * E], k.const("before"), chosen, start=True, stop=True)
                nc.tensor.matmul(ps[:, 5, NT * E:2 * NT * E], k.const("ones"), chosen, start=True, stop=True
                                 ).then_inc(counted_done, 1)

                def transpose_rows(pair, par):
                    pe.wait_ge(rows_loaded[par], 16 * (pair + 1))
                    for c in range(C):
                        for t in range(SLOT // P):
                            last = nc.tensor.transpose(ps[:, XB, (c * (SLOT // P) + t) * P:(c * (SLOT // P) + t + 1) * P],
                                                       rows[:, par, t, c * P:(c + 1) * P], k.ident)
                    last.then_inc(xt_done, 1)

                pe.wait_ge(rows_known, 1)
                transpose_rows(0, 0)

                def body(s, pair, par, has_next):
                    pe.wait_ge(xt_ready, s + 1)
                    pe.wait_ge(in_loaded[par], 16 * PER_IN * (pair + 1))
                    own_wait(pe, k)
                    for n in range(HC_N):
                        if seen(s, 1) or n >= 4:
                            pe.wait_ge(h_ready, HC_N * s + n - 3)
                        for i, w in enumerate(win):
                            for c in range(C):
                                last = nc.tensor.matmul(ps[:, HB + n % 4, i * SLOT:(i + 1) * SLOT],
                                                        w[:, par, c, n * P:(n + 1) * P], xT[:, c, :],
                                                        start=c == 0, stop=c == C - 1)
                        last.then_inc(h_done, 1)
                    if has_next:
                        transpose_rows(pair if par == 0 else pair + 1, 1 - par)
                    if seen(s, 1):
                        pe.wait_ge(y_read if gated else y_ready, s)
                    pe.wait_ge(out_loaded[par], 16 * PER_OUT * (pair + 1))
                    own_wait(pe, k)
                    for n in range(HC_N):
                        pe.wait_ge(h_ready, HC_N * s + n + 1)
                        for t in range(SLOT // P):
                            last = nc.tensor.matmul(ps[:, YB, t * D:(t + 1) * D], hT[:, par, n, t * P:(t + 1) * P],
                                                    wout[:, par, n, :], start=n == 0 and t == 0, stop=n == HC_N - 1,
                                                    skip_group_check=True)
                    last.then_inc(y_done, 1)
                per_slot(pe, body)

            @block.scalar
            def _(act):
                zT.scalar(act)
                act.wait_ge(gap_ready, 1)
                nc.scalar.activation(share2[:, :], gap[:, :], ACT.Exp).then_inc(exp_ready, 1)

                def rows_out(s):
                    act.wait_ge(xt_done, s + 1)
                    nc.scalar.copy(xT[:, :, :].rearrange("p c n -> p (c n)"), ps[:, XB, :]).then_inc(xt_ready, 1)
                rows_out(0)

                def body(s, pair, par, has_next):
                    if gated:
                        act.wait_ge(halfb_ready, s + 1)
                    elif seen(s, 2):
                        act.wait_ge(y_done, s - 1)
                    for n in range(HC_N):
                        act.wait_ge(h_done, HC_N * s + n + 1)
                        if gated:
                            if seen(s, 1) or n >= 2:
                                act.wait_ge(h_ready, HC_N * s + n - 1)
                            nc.scalar.activation(gelu[:, n % 2, :], ps[:, HB + n % 4, 0:SLOT], ACT.Gelu,
                                                 bias=bin_[0][:, par, n:n + 1])
                            nc.scalar.activation(tanh[:, n % 2, :], ps[:, HB + n % 4, SLOT:2 * SLOT], ACT.Tanh,
                                                 bias=halfb[:, par, n:n + 1], scale=0.5).then_inc(act_done, 1)
                        else:
                            nc.scalar.activation(hT[:, par, n, :], ps[:, HB + n % 4, 0:SLOT], ACT.Gelu,
                                                 bias=bin_[0][:, par, n:n + 1]).then_inc(h_ready, 1)
                    if has_next:
                        rows_out(s + 1)
                per_slot(act, body)

            @block.vector
            def _(dve):
                order = Count(dve, order_sem)
                norm.vector(dve, order)
                zT.vector(dve)
                dve.wait_ge(logits_done, 1)
                order.after(nc.vector.tensor_tensor(logits[:, :, :], ps[:, 4, 0:NT * E].rearrange("p (t e) -> p t e", e=E),
                                                    b_route[:, :].unsqueeze(1).broadcast_to([P, NT, E]), ALU.add))

                def pick(src, chosen, value, winner):
                    order.after(nc.vector.tensor_reduce(best[:, value, :], src, AX.X, ALU.max))
                    order.after(nc.vector.tensor_tensor(tie[:, :, :], src, best[:, value, :].unsqueeze(2)
                                                        .broadcast_to([P, NT, E]), ALU.is_equal))
                    order.after(nc.vector.tensor_tensor(tie[:, :, :], tie[:, :, :], k.const("prefer").unsqueeze(1)
                                                        .broadcast_to([P, NT, E]), ALU.mult))
                    order.after(nc.vector.tensor_reduce(best[:, winner, :], tie[:, :, :], AX.X, ALU.max))
                    order.after(nc.vector.tensor_tensor(chosen, tie[:, :, :], best[:, winner, :].unsqueeze(2)
                                                        .broadcast_to([P, NT, E]), ALU.is_equal))
                pick(logits[:, :, :], first[:, :, :], 0, 2)
                order.after(nc.vector.scalar_tensor_tensor(out=rest[:, :, :], in0=first[:, :, :], scalar=-3.0e38,
                                                           in1=logits[:, :, :], op0=ALU.mult, op1=ALU.add))
                pick(rest[:, :, :], second[:, :, :], 1, 3)
                nc.vector.tensor_tensor(both[:, :, :], first[:, :, :], second[:, :, :], ALU.add).then_inc(both_ready, 1)
                nc.vector.tensor_tensor(gap[:, :], best[:, 1, :], best[:, 0, :], ALU.subtract).then_inc(gap_ready, 1)
                dve.wait_ge(exp_ready, 1)
                order.after(nc.vector.tensor_scalar(gap[:, :], share2[:, :], 1.0, None, ALU.add))
                order.after(nc.vector.reciprocal(share1[:, :], gap[:, :]))
                order.after(nc.vector.tensor_tensor(share2[:, :], share2[:, :], share1[:, :], ALU.mult))
                dve.wait_ge(counted_done, 1)
                order.after(nc.vector.tensor_copy(counted[:, :, :, :].rearrange("p a t e -> p (a t e)"), ps[:, 5, 0:2 * NT * E]))
                order.after(nc.vector.memset(earlier[:, 0, :], 0.0))
                for t in range(NT):
                    order.after(nc.vector.tensor_tensor(earlier[:, t + 1, :], earlier[:, t, :], counted[:, 1, t, :], ALU.add))
                order.after(nc.vector.tensor_tensor(
                    over[:, :, :], earlier[:, NT, :].unsqueeze(2).broadcast_to([P, E, SLOTS_EACH]),
                    k.const("slot_floor").unsqueeze(1).broadcast_to([P, E, SLOTS_EACH]), ALU.is_gt))
                order.after(nc.vector.tensor_reduce(slots_of[:, :], over[:, :, :], AX.X, ALU.add))
                order.after(nc.vector.memset(start_of[:, 0:1], 0.0))
                for e in range(1, E):
                    order.after(nc.vector.tensor_tensor(start_of[:, e:e + 1], start_of[:, e - 1:e], slots_of[:, e - 1:e],
                                                        ALU.add))
                order.after(nc.vector.tensor_tensor(place[:, :, :], earlier[:, 0:NT, :], counted[:, 0, :, :], ALU.add))
                order.after(nc.vector.scalar_tensor_tensor(out=place[:, :, :], in0=start_of[:, :].unsqueeze(1)
                                                           .broadcast_to([P, NT, E]), scalar=float(SLOT),
                                                           in1=place[:, :, :], op0=ALU.mult, op1=ALU.add))
                for way, chosen in enumerate((first, second)):
                    order.after(nc.vector.tensor_tensor(tie[:, :, :], chosen[:, :, :], place[:, :, :], ALU.mult))
                    order.after(nc.vector.tensor_reduce(at[:, way, :], tie[:, :, :], AX.X, ALU.add))
                order.after(nc.vector.tensor_copy(row[:, :, :], at[:, :, :]))
                order.after(nc.vector.tensor_tensor(
                    begun[:, :, :], k.const("slot").unsqueeze(2).broadcast_to([P, SLOTS, E]),
                    start_of[:, :].unsqueeze(1).broadcast_to([P, SLOTS, E]), ALU.is_ge))
                order.after(nc.vector.tensor_reduce(expert_f[:, :], begun[:, :, :], AX.X, ALU.add))
                nc.vector.tensor_scalar(expert[:, :], expert_f[:, :], -1.0, None, ALU.add).then_inc(rows_known, 1)

                def body(s, pair, par, has_next):
                    if gated:
                        if seen(s, 2):
                            dve.wait_ge(y_done, s - 1)
                        for n in range(HC_N):
                            dve.wait_ge(act_done, HC_N * s + n + 1)
                            nc.vector.scalar_tensor_tensor(out=hT[:, par, n, :], in0=tanh[:, n % 2, :], scalar=1.0,
                                                           in1=gelu[:, n % 2, :], op0=ALU.add, op1=ALU.mult
                                                           ).then_inc(h_ready, 1)
                    dve.wait_ge(y_done, s + 1)
                    if gated:
                        dve.wait_ge(rbias_ready, s + 1)
                        nc.vector.scalar_tensor_tensor(out=resid[:, :, :].rearrange("p t d -> p (t d)"), in0=ps[:, YB, :],
                                                       scalar=0.5, in1=rbias[:, par, :, :].rearrange("p t d -> p (t d)"),
                                                       op0=ALU.mult, op1=ALU.add).then_inc(y_read, 1)
                        dve.wait_ge(y_read, s + 1)
                        for t in range(SLOT // P):
                            last = nc.vector.bn_stats(st[:, t, :], resid[:, t, :])
                        order.after(last)
                        own_wait(dve, k)
                        for t in range(SLOT // P):
                            last = nc.vector.bn_aggr(mv[:, t, :], st[:, t, :])
                        last.then_inc(rstats_ready, 1)
                        dve.wait_ge(rrstd_ready, s + 1)
                        for t in range(SLOT // P):
                            last = nc.vector.tensor_scalar(resid[:, t, :], resid[:, t, :], mv[:, t, 0:1], rs[:, t:t + 1],
                                                           ALU.subtract, ALU.mult)
                        order.after(last)
                        order.after(nc.vector.tensor_tensor(resid[:, :, :], resid[:, :, :],
                                                            g_e[:, par, :].unsqueeze(1).broadcast_to([P, SLOT // P, D]),
                                                            ALU.mult))
                        if seen(s, 2):
                            dve.wait_ge(y_stored[par], 16 * pair)
                        nc.vector.tensor_tensor(y[:, par, :, :], resid[:, :, :],
                                                b_e[:, par, :].unsqueeze(1).broadcast_to([P, SLOT // P, D]),
                                                ALU.add).then_inc(y_ready, 1)
                    else:
                        if seen(s, 2):
                            dve.wait_ge(y_stored[par], 16 * pair)
                        nc.vector.tensor_tensor(y[:, par, :, :], ps[:, YB, :].rearrange("p (t d) -> p t d", d=D),
                                                bout[:, par, :].unsqueeze(1).broadcast_to([P, SLOT // P, D]),
                                                ALU.add).then_inc(y_ready, 1)
                if gated:
                    body(0, 0, 0, True)
                    body(1, 0, 1, True)
                    with dve.Fori(1, SLOTS // 2) as pair:
                        order.enter(pair - 1, 6)
                        for par in range(2):
                            body(pair * 2 + par, pair, par, True)
                        order.leave(SLOTS // 2 - 1)
                    body(SLOTS - 1, SLOTS // 2, 0, False)
                else:
                    per_slot(dve, body)
                for way, (mixed, share) in enumerate(((mixed1, share1), (mixed2, share2))):
                    base = k.x if gated else k.z
                    dve.wait_ge(gathered[way], 16 * NT)
                    for t in range(NT):
                        src = base if way == 0 else k.x if gated else mixed1
                        dst = k.x if gated else mixed1
                        last = nc.vector.scalar_tensor_tensor(out=dst[:, t, :], in0=mixed[:, t, :], scalar=share[:, t:t + 1],
                                                              in1=src[:, t, :], op0=ALU.mult, op1=ALU.add)
                    order.after(last)
                if not gated:
                    dve.wait_ge(small_loaded, 16 * 2)
                    norm2.vector(dve, order)
                    dve.wait_ge(norm2.dst_ready, NT)
                    for op, t in ((ALU.mult, gamma), (ALU.add, beta)):
                        order.after(nc.vector.tensor_tensor(mixed1[:, :, :], mixed1[:, :, :],
                                                            t[:, :].unsqueeze(1).broadcast_to([P, NT, D]), op))
                    nc.vector.tensor_tensor(k.x[:, :, :], k.x[:, :, :], mixed1[:, :, :], ALU.add)


def experts_one(nc, k):
    experts(nc, k, "e1", False)


def experts_two(nc, k):
    experts(nc, k, "e2", True)


def constants():
    import numpy as np
    table = np.zeros((P, CONST_WIDTH), np.float32)

    def put(name, value):
        a, b = CONST_COLS[name]
        table[:, a:b] = np.broadcast_to(value, (P, b - a))
    row = np.arange(P)[:, None]
    put("ident", row == np.arange(P))
    put("ones", 1.0)
    put("before", row < np.arange(P))
    put("head_of_row", row // HD == np.arange(HC))
    put("group_of_row", row // S == np.arange(HG))
    put("query", row % S == np.arange(S))
    put("minus_half", -0.5)
    put("prefer", E - np.arange(E))
    put("slot_floor", SLOT * np.arange(SLOTS_EACH))
    put("slot", np.arange(SLOTS))
    valid = np.ones((P, B, 3), np.float32)
    valid[:, :, 2] = row == np.arange(B)
    put("last_key", valid.reshape(P, -1))
    q, key = row % S, np.arange(S)
    pair, key_pair = q // 2, key // 2
    for w in range(2):
        first = pair - w
        a = CONST_COLS["window_pen"][0] + w * S
        table[:, a:a + S] = np.where((key_pair == first) | (key_pair == first + 1), 0.0, MASKED)
        on = (first >= 0) & (first + 1 < S // 2)
        table[:, CONST_COLS["window_on"][0] + w] = on[:, 0]
    pairs = np.arange(P) % S // 2
    put("window_count", np.where((pairs == 0) | (pairs == S // 2 - 1), 1.0, 2.0))
    put("causal_pen", np.where(key <= q, 0.0, MASKED))
    theta = np.repeat((np.float32(10000.0) ** (-np.arange(0, D, 2, dtype=np.float32) / np.float32(D))), 2)
    angle = (np.arange(S, dtype=np.float32)[:, None] * theta[None, :])[np.arange(P) % S]
    put("cos", np.cos(angle))
    put("sin", np.sin(angle) * np.where(np.arange(D) % 2 == 0, -1.0, 1.0))
    return table


_DIRECT = ["x", "L0_xattn_Wq", "L0_xattn_Wk", "L0_xattn_Wv", "L0_xattn_Wo", "L0_xattn_bo",
           "L0_attn_w_qkv", "L0_attn_w_out", "L0_attn_b_out", "L1_attn_bo"] + [
    "L0_ffn_" + n for n in ("Wg", "bg", "W1", "W2", "b2", "gamma", "beta")] + [
    "L1_xattn_" + n for n in ("Wq", "Wk", "Wv", "gru_bih", "gru_bhh")] + [
    "L1_ffn_" + n for n in ("Wr", "br", "Wi", "Wg", "Wo", "bo", "gamma", "beta")]
_EXPERT_COLUMNS = ["L0_ffn_b1", "L1_ffn_bi", "L1_ffn_bg"]
_TURNED = ["L1_attn_Wq", "L1_attn_Wk", "L1_attn_Wv", "L1_attn_Wo", "L1_xattn_gru_wih", "L1_xattn_gru_whh"]
_COLUMNS = ["L0_xattn_bq", "L0_xattn_bk", "L0_xattn_bv", "L1_xattn_slot_norm_w", "L1_xattn_input_norm_w"]


def kernel(**inputs):
    import numpy as _np
    import concourse.bacc as _bacc
    from concourse import mybir as _mybir
    from concourse.bass_utils import run_bass_kernel_spmd as _run

    laid_out = {name: _np.ascontiguousarray(inputs[name]) for name in _DIRECT}
    for name in _TURNED:
        laid_out[name + "T"] = _np.ascontiguousarray(_np.asarray(inputs[name]).T)
    for name in _COLUMNS:
        laid_out[name] = _np.ascontiguousarray(_np.asarray(inputs[name]).reshape(-1, P).T)
    for name in _EXPERT_COLUMNS:
        laid_out[name] = _np.ascontiguousarray(_np.transpose(_np.asarray(inputs[name]).reshape(E, -1, P), (0, 2, 1)))
    laid_out["mask"] = _np.ascontiguousarray(inputs["mask_Bx1xSxS2_if1"])
    laid_out["ctx"] = _np.ascontiguousarray(inputs["ctx_1024"])
    laid_out["ctxT"] = _np.ascontiguousarray(_np.transpose(inputs["ctx_1024"], (2, 0, 1)))
    laid_out["ctx_lastT"] = _np.ascontiguousarray(inputs["ctx_1024"][:, KEYS - 1, :].T)
    laid_out["consts"] = constants()
    nc = _bacc.Bacc("TRN2", target_bir_lowering=False, num_devices=1)
    arrays, args = {}, {}
    for name, a in laid_out.items():
        arrays[f"in_{name}_dram"] = a
        args[name] = nc.dram_tensor(f"in_{name}_dram", a.shape, _mybir.dt.from_np(a.dtype), kind="ExternalInput").ap()
    out = nc.dram_tensor("out_0_dram", (B, S, D), _mybir.dt.float32, kind="ExternalOutput").ap()
    build(nc, args, out)
    r = _run(nc, [arrays], core_ids=[0])
    return r.results[0]["out_0_dram"]
```

```python
import concourse.bass as bass
from concourse import mybir
from contextlib import ExitStack

F32 = mybir.dt.float32
I32 = mybir.dt.int32
BF16 = mybir.dt.bfloat16
ALU = mybir.AluOpType
ACT = mybir.ActivationFunctionType
AX = mybir.AxisListType

P = 128
B, S, D = 32, 32, 256
KEYS = 257
HEADS, HD = 16, 16
C = D // P
NT = B * S // P
TB = P // S
HG = P // S
E, FF = 8, 1024
SLOT = 256
SLOTS = (2 * B * S + E * (SLOT - 1)) // SLOT
SLOTS_EACH = B * S // SLOT
NG = HEADS // HG
HC = P // HD
KT2 = KEYS // P
MASKED = -1.0e30

CONST_COLS = {}
_at = 0
for _n, _w in [("ident", P), ("ones", P), ("before", P), ("head_of_row", HC), ("group_of_row", HG), ("query", S),
               ("window_pen", 2 * S), ("window_on", 2), ("causal_pen", S), ("cos", D), ("sin", D), ("minus_half", 16),
               ("prefer", 8), ("slot_floor", 4), ("slot", 15), ("window_count", P), ("last_key", 3 * B)]:
    CONST_COLS[_n] = (_at, _at + _w)
    _at += _w
CONST_WIDTH = _at


class Count:

    def __init__(self, eng, sem):
        self.eng, self.sem, self.base, self.n = eng, sem, 0, 0

    def after(self, ins):
        self.n += 1
        ins.then_inc(self.sem, 1)
        self.eng.wait_ge(self.sem, self.base + self.n)

    def enter(self, trip, per_trip):
        self.start, self.per = self.base + self.n, per_trip
        self.base, self.n = self.start + trip * per_trip, 0

    def leave_open(self):
        assert self.n == self.per, (self.n, self.per)
        self.base, self.n = self.start, 0

    def leave(self, trips):
        assert self.n == self.per, (self.n, self.per)
        self.base, self.n = self.start + trips * self.per, 0


class Core:
    pass


def build(nc, ins, out):
    with ExitStack() as ctx:
        k = Core()
        k.nc, k.ins = nc, ins
        k.sem = nc.alloc_semaphore
        k.consts = ctx.enter_context(nc.sbuf_tensor("consts", [P, CONST_WIDTH], F32))
        k.x = ctx.enter_context(nc.sbuf_tensor("x", [P, NT, D], F32))
        k.z = ctx.enter_context(nc.sbuf_tensor("z", [P, NT, D], F32))
        k.zT = ctx.enter_context(nc.sbuf_tensor("zT", [P, C, NT * P], F32))
        k.stats = ctx.enter_context(nc.sbuf_tensor("stats", [P, NT, 6], F32))
        k.mean_var = ctx.enter_context(nc.sbuf_tensor("mean_var", [P, NT, 2], F32))
        k.rstd = ctx.enter_context(nc.sbuf_tensor("rstd", [P, NT], F32))
        k.ps = ctx.enter_context(nc.psum_tensor("ps", [P, 8, 512], F32))

        def const(name):
            a, b = CONST_COLS[name]
            return k.consts[:, a:b]
        k.const = const
        k.ident = const("ident")
        k.consts_loaded = k.sem("consts_loaded")
        k.passed = k.sem("passed")
        k.sorted_x = nc.dram_tensor("sorted_x", [SLOTS * SLOT, D], F32)
        k.sorted_y = nc.dram_tensor("sorted_y", [SLOTS * SLOT, D], F32)
        k.cleared = k.sem("sorted_x_cleared")
        for stage in (cross_attention, local_attention, experts_one, slot_attention, causal_attention,
                      experts_two):
            used = []

            def stage_sem(name):
                used.append(nc.alloc_semaphore(name))
                return used[-1]
            k.sem = stage_sem
            stage(nc, k)
            nc.clear_and_free_semaphores(used)
            nc.all_engine_barrier()
        k.sem = nc.alloc_semaphore
        x_stored = k.sem("x_stored")
        with nc.Block() as block:
            @block.sync
            def _(sp):
                sp.dma_start(out.rearrange("b s d -> (b s) d").rearrange("(t p) d -> p t d", p=P),
                             k.x[:, :, :]).then_inc(x_stored, 16)
                sp.wait_ge(x_stored, 16)


class Transpose:

    def __init__(self, nc, k, name, src, dst, bank0=0):
        self.nc, self.k, self.src, self.dst, self.bank0 = nc, k, src, dst, bank0
        self.src_ready = k.sem(name + "_rows_ready")
        self.done = k.sem(name + "_transposed")
        self.ready = k.sem(name + "_columns_ready")

    def tensor(self, pe):
        for half in range(2):
            for t in range(4 * half, 4 * half + 4):
                pe.wait_ge(self.src_ready, t + 1)
                for c in range(C):
                    last = self.nc.tensor.transpose(
                        self.k.ps[:, self.bank0 + 2 * c + half, (t % 4) * P:(t % 4 + 1) * P],
                        self.src[:, t, c * P:(c + 1) * P], self.k.ident)
            last.then_inc(self.done, 1)

    def vector(self, dve):
        for half in range(2):
            dve.wait_ge(self.done, half + 1)
            self.nc.vector.tensor_copy(self.dst[:, 1, half * 512:half * 512 + 512],
                                       self.k.ps[:, self.bank0 + 2 + half, :]).then_inc(self.ready, 1)

    def scalar(self, act):
        for half in range(2):
            act.wait_ge(self.done, half + 1)
            self.nc.scalar.copy(self.dst[:, 0, half * 512:half * 512 + 512],
                                self.k.ps[:, self.bank0 + half, :]).then_inc(self.ready, 1)


class Norm:

    def __init__(self, nc, k, name, eps, src, dst, dst_ready=None):
        self.nc, self.k, self.eps, self.src, self.dst = nc, k, eps, src, dst
        self.stats_ready = k.sem(name + "_stats_ready")
        self.var_ready = k.sem(name + "_var_ready")
        self.rstd_ready = k.sem(name + "_rstd_ready")
        self.dst_ready = dst_ready or k.sem(name + "_rows_ready")

    def vector(self, dve, order):
        nc, k = self.nc, self.k
        for t in range(NT):
            last = nc.vector.bn_stats(k.stats[:, t, :], self.src[:, t, :])
        order.after(last)
        for t in range(NT):
            last = nc.vector.bn_aggr(k.mean_var[:, t, :], k.stats[:, t, :])
        last.then_inc(self.stats_ready, 1)
        dve.wait_ge(self.rstd_ready, 1)
        for t in range(NT):
            nc.vector.tensor_scalar(self.dst[:, t, :], self.src[:, t, :], k.mean_var[:, t, 0:1], k.rstd[:, t:t + 1],
                                    ALU.subtract, ALU.mult).then_inc(self.dst_ready, 1)

    def gpsimd(self, pool):
        nc, k = self.nc, self.k
        pool.wait_ge(self.stats_ready, 1)
        nc.gpsimd.tensor_scalar(k.rstd[:, :], k.mean_var[:, :, 1], self.eps, None, ALU.add).then_inc(self.var_ready, 1)
        pool.wait_ge(self.var_ready, 1)
        nc.gpsimd.tensor_tensor(k.rstd[:, :], k.rstd[:, :], k.const("minus_half")[:, 0:NT],
                                ALU.pow).then_inc(self.rstd_ready, 1)


def seen(b, lag):
    return not isinstance(b, int) or b >= lag


def own_wait(eng, k):
    eng.sem_inc(k.passed, 1)


def exists(n, count):
    return not isinstance(n, int) or n < count


def per_batch(eng, body):
    body(0, 0, 0)
    body(1, 0, 1)
    with eng.Fori(1, B // 2 - 1) as pair:
        for par in range(2):
            body(pair * 2 + par, pair, par)
    body(B - 2, B // 2 - 1, 0)
    body(B - 1, B // 2 - 1, 1)


def cross_attention(nc, k):
    ins, ps = k.ins, k.ps
    with ExitStack() as ctx:
        def sb(name, shape, dt=F32):
            return ctx.enter_context(nc.sbuf_tensor("ca_" + name, shape, dt))

        def sem(name):
            return k.sem("ca_" + name)

        wq, wk, wv, wo = (sb(n, [P, C, D]) for n in ("wq", "wk", "wv", "wo"))
        bq, bk, bv = (sb(n, [P, C]) for n in ("bq", "bk", "bv"))
        bo = sb("bo", [1, D])
        lastT = sb("lastT", [P, C, B])
        lastV = sb("lastV", [B, D])
        lastV_by_group = sb("lastV_by_group", [NG, B, D])
        zero = sb("zero", [P, D])
        QT = sb("QT", [P, C, B * S])
        attnT = sb("attnT", [P, C, B * S])
        ctxT = sb("ctxT", [P, 2, C, KEYS])
        mask = sb("mask", [P, 2, KEYS], I32)
        hide = sb("hide", [P, 2, KEYS])
        Qblk = sb("Qblk", [P, C, HC, S])
        KT = sb("KT", [P, C, KEYS])
        V = sb("V", [P, 2, KT2, D])
        masked = sb("masked", [P, NG, KEYS])
        top = sb("top", [P, NG])
        nbias = sb("nbias", [P, NG])
        probs = sb("probs", [P, NG, KEYS])
        rowsum = sb("rowsum", [P, 2, NG])
        rinv = sb("rinv", [P, NG])
        PT = sb("PT", [P, NG, KT2, P])
        PTlast = sb("PTlast", [NG, P])
        pick = sb("pick", [P, NG, S])
        blocked = sb("blocked", [P, NG, HG * HD])

        consts_loaded = k.consts_loaded
        x_loaded, weights_loaded = sem("x_loaded"), sem("weights_loaded")
        ctxT_loaded = [sem("ctxT_loaded0"), sem("ctxT_loaded1")]
        mask_loaded = [sem("mask_loaded0"), sem("mask_loaded1")]
        zT = Transpose(nc, k, "ca_z", k.z, k.zT)
        norm = Norm(nc, k, "ca_norm", 1e-5, k.x, k.z, zT.src_ready)
        q_done, qt_ready = sem("q_done"), sem("qt_ready")
        lastv_done, lastv_ready, zeroed, lastv_placed = (
            sem(n) for n in ("lastv_done", "lastv_ready", "zeroed", "lastv_placed"))
        qblk_ready, keys_done, values_done, scores_done = (
            sem(n) for n in ("qblk_ready", "keys_done", "values_done", "scores_done"))
        kt_ready, v_ready, hide_ready, masked_ready = (
            sem(n) for n in ("kt_ready", "v_ready", "hide_ready", "masked_ready"))
        nbias_ready, probs_ready, pt_done = sem("nbias_ready"), sem("probs_ready"), sem("pt_done")
        pt_ready, ptlast_ready, av_done, blocked_ready, attn_done, attn_ready = (
            sem(n) for n in ("pt_ready", "ptlast_ready", "av_done", "blocked_ready", "attn_done", "attn_ready"))
        pick_ready, rinv_ready = sem("pick_ready"), sem("rinv_ready")
        attn_biased, proj_done, order_sem = sem("attn_biased"), sem("proj_done"), sem("vector_order")

        BK, BV, BS, BP, BM = 0, 2, 3, 5, 7
        AV = ps[:, BM, 0:D]
        BESIDE = -(-KEYS // S) * S
        PTL = ps[0:NG, BK, BESIDE:BESIDE + P]
        OT = ps[:, BS + 1, BESIDE:BESIDE + C * S]
        NWEIGHTS = 8 + C

        with nc.Block() as block:
            @block.sync
            def _(sp):
                sp.dma_start(k.x[:, :, :], ins["x"].rearrange("b s d -> (b s) d").rearrange("(t p) d -> p t d", p=P)
                             ).then_inc(x_loaded, 16)
                sp.dma_start(k.consts[:, :], ins["consts"]).then_inc(consts_loaded, 16)
                for t, n in ((wq, "Wq"), (wk, "Wk"), (wv, "Wv"), (wo, "Wo")):
                    sp.dma_start(t[:, :, :], ins["L0_xattn_" + n].rearrange("(c p) n -> p c n", p=P)
                                 ).then_inc(weights_loaded, 16)
                for t, n in ((bq, "bq"), (bk, "bk"), (bv, "bv")):
                    sp.dma_start(t[:, :], ins["L0_xattn_" + n]).then_inc(weights_loaded, 16)
                sp.dma_start(bo[:, :], ins["L0_xattn_bo"].unsqueeze(0)).then_inc(weights_loaded, 16)
                for c in range(C):
                    sp.dma_start(lastT[:, c, :], ins["ctx_lastT"][c * P:(c + 1) * P, :]).then_inc(weights_loaded, 16)

                def load(b, par):
                    sp.dma_start(ctxT[:, par, :, :],
                                 ins["ctxT"][:, bass.ds(b, 1), :].rearrange("(c p) b n -> p (c b) n", p=P)
                                 ).then_inc(ctxT_loaded[par], 16)
                    for h in range(HG):
                        sp.dma_start(mask[h * S:(h + 1) * S, par, :],
                                     ins["mask"][bass.ds(b, 1), 0].rearrange("b q n -> (b q) n")
                                     ).then_inc(mask_loaded[par], 16)
                load(0, 0)
                load(1, 1)
                sp.wait_ge(zeroed, 2)
                sp.wait_ge(lastv_ready, 1)
                for g in range(NG):
                    sp.dma_start(lastV_by_group[g:g + 1, :, g * HG * HD:(g + 1) * HG * HD],
                                 lastV[:, g * HG * HD:(g + 1) * HG * HD]).then_inc(lastv_placed, 16)
                sp.dma_start(k.sorted_x.ap().rearrange("(n p) d -> p n d", p=P),
                             zero[:, :].unsqueeze(1).broadcast_to([P, 2 * SLOTS, D])).then_inc(k.cleared, 16)
                with sp.Fori(0, B // 2 - 1) as pair:
                    for par in range(2):
                        sp.wait_ge(values_done, pair * 2 + par + 1)
                        sp.wait_ge(hide_ready, pair * 2 + par + 1)
                        load(pair * 2 + par + 2, par)

            @block.gpsimd
            def _(pool):
                nc.gpsimd.memset(zero[:, :], 0.0).then_inc(zeroed, 1)
                nc.gpsimd.memset(lastV_by_group[:, :, :], 0.0).then_inc(zeroed, 1)
                pool.wait_ge(consts_loaded, 16)
                norm.gpsimd(pool)

                def body(b, pair, par):
                    pool.wait_ge(mask_loaded[par], 16 * HG * (pair + 1))
                    if seen(b, 2):
                        pool.wait_ge(masked_ready, NG * (b - 1))
                    own_wait(pool, k)
                    nc.gpsimd.tensor_scalar(hide[:, par, :], mask[:, par, :], 0.0, MASKED,
                                            ALU.is_equal, ALU.mult).then_inc(hide_ready, 1)
                per_batch(pool, body)

            @block.tensor
            def _(pe):
                pe.wait_ge(consts_loaded, 16)
                zT.tensor(pe)
                pe.wait_ge(weights_loaded, 16 * NWEIGHTS)

                for c in range(C):
                    last = nc.tensor.matmul(ps[0:B, BM, 0:D], lastT[:, c, :], wv[:, c, :], start=c == 0, stop=c == C - 1)
                last.then_inc(lastv_done, 1)
                pe.wait_ge(zT.ready, 4)
                for m in range(C):
                    for half in range(2):
                        bank = 2 * m + half
                        for c in range(C):
                            last = nc.tensor.matmul(ps[:, bank, :], wq[:, c, m * P:(m + 1) * P],
                                                    k.zT[:, c, half * 512:(half + 1) * 512], start=c == 0, stop=c == C - 1)
                        last.then_inc(q_done, 1)

                def keys(b, pair, par):
                    pe.wait_ge(ctxT_loaded[par], 16 * (pair + 1))
                    if seen(b, 1):
                        pe.wait_ge(kt_ready, C * b)
                    for m in range(C):
                        for c in range(C):
                            last = nc.tensor.matmul(ps[:, BK + m, 0:KEYS], wk[:, c, m * P:(m + 1) * P], ctxT[:, par, c, :],
                                                    start=c == 0, stop=c == C - 1)
                        last.then_inc(keys_done, 1)

                def values(b, par):
                    if seen(b, 1):
                        pe.wait_ge(v_ready, b)
                    for t in range(KT2):
                        for c in range(C):
                            last = nc.tensor.matmul(ps[:, BV, t * D:(t + 1) * D], ctxT[:, par, c, t * P:(t + 1) * P],
                                                    wv[:, c, :], start=c == 0, stop=c == C - 1)
                    last.then_inc(values_done, 1)

                def scores(b, groups):
                    pe.wait_ge(qblk_ready, b + 1)
                    pe.wait_ge(kt_ready, C * b + C)
                    for g in groups:
                        c, j = g // 2, g % 2
                        if g == 1 and seen(b, 2):
                            pe.wait_ge(attn_ready, b - 1)
                        if g >= 2 or seen(b, 1):
                            pe.wait_ge(masked_ready, NG * b + g - 1)
                        nc.tensor.matmul(ps[:, BS + g % 2, 0:KEYS],
                                         Qblk[:, c, j * HG:(j + 1) * HG, :].rearrange("p h q -> p (h q)"),
                                         KT[:, c, :], start=True, stop=True).then_inc(scores_done, 1)

                pe.wait_ge(qt_ready, 4)
                pe.wait_ge(lastv_ready, 1)
                pe.wait_ge(lastv_placed, 16 * NG)
                keys(0, 0, 0)
                values(0, 0)
                scores(0, range(NG))
                keys(1, 0, 1)
                values(1, 1)

                def body(b, pair, par):
                    pe.wait_ge(probs_ready, NG * b + NG)
                    if seen(b, 1):
                        pe.wait_ge(pt_ready, 2 * b)
                        pe.wait_ge(ptlast_ready, b)
                    if exists(b + 1, B):
                        pe.wait_ge(kt_ready, C * b + 2 * C)
                    for g in range(NG):
                        for t in range(KT2):
                            nc.tensor.transpose(ps[:, BP + g // 2, ((g % 2) * KT2 + t) * P:((g % 2) * KT2 + t + 1) * P],
                                                probs[:, g, t * P:(t + 1) * P], k.ident)
                    nc.tensor.transpose(PTL, probs[:, :, KEYS - 1], k.ident).then_inc(pt_done, 1)
                    if exists(b + 1, B):
                        scores(b + 1, range(NG // 2))
                    pe.wait_ge(ptlast_ready, b + 1)
                    own_wait(pe, k)
                    nc.tensor.matmul(AV, PTlast[:, :], lastV_by_group[:, bass.ds(b, 1), :].rearrange("g b d -> g (b d)"),
                                     start=True, stop=False, skip_group_check=True)
                    if exists(b + 1, B):
                        scores(b + 1, range(NG // 2, NG))
                    pe.wait_ge(pt_ready, 2 * b + 2)
                    pe.wait_ge(v_ready, b + 1)
                    for g in range(NG):
                        for t in range(KT2):
                            last = nc.tensor.matmul(ps[:, BM, g * HG * HD:(g + 1) * HG * HD], PT[:, g, t, :],
                                                    V[:, par, t, g * HG * HD:(g + 1) * HG * HD],
                                                    start=False, stop=g == NG - 1 and t == KT2 - 1, skip_group_check=True)
                    last.then_inc(av_done, 1)
                    if exists(b + 2, B):
                        keys(b + 2, pair + 1, par)
                    gather_heads(b)
                    if exists(b + 2, B):
                        values(b + 2, par)

                def gather_heads(b):
                    pe.wait_ge(blocked_ready, b + 1)
                    if seen(b, 1):
                        pe.wait_ge(attn_ready, b)
                    if exists(b + 1, B):
                        pe.wait_ge(masked_ready, NG * b + 2 * NG)
                    for g in range(NG):
                        last = nc.tensor.matmul(OT[(g % 2) * 64:(g % 2) * 64 + 64, (g // 2) * S:(g // 2 + 1) * S],
                                                blocked[:, g, :], pick[:, g, :], start=True, stop=True)
                    last.then_inc(attn_done, 1)

                per_batch(pe, body)
                pe.wait_ge(attn_ready, B)

                pe.wait_ge(attn_biased, 1)
                for t in range(NT):
                    nc.tensor.matmul(ps[:, t, 0:D], k.const("ones")[0:1, :], bo[:, :], start=True, stop=False)
                    for c in range(C):
                        last = nc.tensor.matmul(ps[:, t, 0:D], attnT[:, c, t * P:(t + 1) * P], wo[:, c, :],
                                                start=False, stop=c == C - 1)
                    last.then_inc(proj_done, 1)

            @block.scalar
            def _(act):
                zT.scalar(act)
                act.wait_ge(weights_loaded, 16 * NWEIGHTS)
                act.wait_ge(lastv_done, 1)
                nc.scalar.copy(lastV[:, :], ps[0:B, BM, 0:D]).then_inc(lastv_ready, 1)
                for m in range(C):
                    for half in range(2):
                        act.wait_ge(q_done, 2 * m + half + 1)
                        nc.scalar.activation(QT[:, m, half * 512:(half + 1) * 512], ps[:, 2 * m + half, :], ACT.Identity,
                                             bias=bq[:, m:m + 1]).then_inc(qt_ready, 1)

                def keys_out(b):
                    if seen(b, 1):
                        act.wait_ge(scores_done, NG * b)
                    for m in range(C):
                        act.wait_ge(keys_done, C * b + m + 1)
                        nc.scalar.activation(KT[:, m, :], ps[:, BK + m, 0:KEYS], ACT.Identity,
                                             bias=bk[:, m:m + 1]).then_inc(kt_ready, 1)

                def values_out(b, par):
                    act.wait_ge(values_done, b + 1)
                    if seen(b, 2):
                        act.wait_ge(av_done, b - 1)
                    nc.scalar.copy(V[:, par, :, :].rearrange("p t d -> p (t d)"), ps[:, BV, :]).then_inc(v_ready, 1)

                def exponentials(b, par):
                    act.wait_ge(nbias_ready, b + 1)
                    if seen(b, 2):
                        act.wait_ge(pick_ready, b - 1)
                    for g in range(NG):
                        nc.scalar.activation(probs[:, g, :], masked[:, g, :], ACT.Exp, bias=nbias[:, g:g + 1],
                                             scale=float(HD) ** -0.5, accum_out=rowsum[:, par, g:g + 1]).then_inc(probs_ready, 1)

                keys_out(0)
                values_out(0, 0)
                exponentials(0, 0)
                keys_out(1)
                values_out(1, 1)

                def body(b, pair, par):
                    act.wait_ge(pt_done, b + 1)
                    if seen(b, 1):
                        act.wait_ge(av_done, b)
                    for half in range(2):
                        nc.scalar.copy(PT[:, 2 * half:2 * half + 2, :, :].rearrange("p g t q -> p (g t q)"),
                                       ps[:, BP + half, :]).then_inc(pt_ready, 1)
                    if exists(b + 1, B):
                        exponentials(b + 1, 1 - par)
                    if exists(b + 2, B):
                        keys_out(b + 2)
                        values_out(b + 2, par)
                per_batch(act, body)

            @block.vector
            def _(dve):
                order = Count(dve, order_sem)
                dve.wait_ge(x_loaded, 16)
                norm.vector(dve, order)
                zT.vector(dve)
                dve.wait_ge(qt_ready, 4)

                def block_queries(b):
                    if seen(b, 1):
                        dve.wait_ge(scores_done, NG * b)
                    nc.vector.tensor_tensor(
                        Qblk[:, :, :, :],
                        QT[:, :, bass.ds(b * S, S)].unsqueeze(2).broadcast_to([P, C, HC, S]),
                        k.const("head_of_row").unsqueeze(1).unsqueeze(3).broadcast_to([P, C, HC, S]),
                        ALU.mult).then_inc(qblk_ready, 1)

                def attention_out(b):
                    dve.wait_ge(attn_done, b + 1)
                    nc.vector.tensor_copy(attnT[:, :, bass.ds(b * S, S)],
                                          OT.rearrange("p (c q) -> p c q", c=C)).then_inc(attn_ready, 1)

                def mask_scores(b, par):
                    dve.wait_ge(hide_ready, b + 1)
                    if seen(b, 1):
                        dve.wait_ge(probs_ready, NG * b)
                    for g in range(NG):
                        dve.wait_ge(scores_done, NG * b + g + 1)
                        own_wait(dve, k)
                        nc.vector.tensor_tensor_reduce(out=masked[:, g, :], in0=ps[:, BS + g % 2, 0:KEYS], in1=hide[:, par, :],
                                                       scale=1.0, scalar=-3.0e38, op0=ALU.add, op1=ALU.max,
                                                       accum_out=top[:, g:g + 1]).then_inc(masked_ready, 1)
                    dve.wait_ge(masked_ready, NG * b + NG)
                    nc.vector.tensor_scalar(nbias[:, :], top[:, :], -float(HD) ** -0.5, None, ALU.mult).then_inc(nbias_ready, 1)

                block_queries(0)
                mask_scores(0, 0)
                block_queries(1)

                def body(b, pair, par):
                    dve.wait_ge(pt_done, b + 1)
                    if seen(b, 1):
                        dve.wait_ge(av_done, b)
                    nc.vector.tensor_copy(PTlast[:, :], PTL).then_inc(ptlast_ready, 1)
                    if exists(b + 1, B):
                        mask_scores(b + 1, 1 - par)
                    nc.vector.reciprocal(rinv[:, :], rowsum[:, par, :]).then_inc(rinv_ready, 1)
                    dve.wait_ge(rinv_ready, b + 1)
                    if seen(b, 1):
                        dve.wait_ge(attn_done, b)
                    own_wait(dve, k)
                    nc.vector.tensor_tensor(pick[:, :, :], k.const("query").unsqueeze(1).broadcast_to([P, NG, S]),
                                            rinv[:, :].unsqueeze(2).broadcast_to([P, NG, S]), ALU.mult).then_inc(pick_ready, 1)
                    dve.wait_ge(av_done, b + 1)
                    nc.vector.tensor_tensor(
                        blocked[:, :, :].rearrange("p g (h d) -> p g h d", h=HG),
                        AV.rearrange("p (g h d) -> p g h d", g=NG, h=HG),
                        k.const("group_of_row").unsqueeze(1).unsqueeze(3).broadcast_to([P, NG, HG, HD]),
                        ALU.mult).then_inc(blocked_ready, 1)
                    if exists(b + 2, B):
                        block_queries(b + 2)
                    attention_out(b)
                per_batch(dve, body)
                dve.wait_ge(attn_ready, B)
                for c in range(C):
                    last = nc.vector.tensor_scalar(attnT[:, c, :], attnT[:, c, :], bv[:, c:c + 1], None, ALU.add)
                last.then_inc(attn_biased, 1)
                add_projection(nc, k, dve, proj_done)


def add_projection(nc, k, dve, proj_done):
    for t in range(NT):
        dve.wait_ge(proj_done, t + 1)
        nc.vector.tensor_tensor(k.x[:, t, :], k.ps[:, t, 0:D], k.x[:, t, :], ALU.add)


def self_attention(nc, k, name, weights, scale, windows, rope, bias_name, bias_weight):
    ins, ps = k.ins, k.ps
    W = len(windows)
    with ExitStack() as ctx:
        def sb(n, shape, dt=F32):
            return ctx.enter_context(nc.sbuf_tensor(name + "_" + n, shape, dt))

        def sem(n):
            return k.sem(name + "_" + n)

        wq, wk, wv, wo = (sb(n, [P, C, D]) for n in ("wq", "wk", "wv", "wo"))
        bo = sb("bo", [1, D])
        QT, KT, attnT = (sb(n, [P, C, B * S]) for n in ("QT", "KT", "attnT"))
        V = sb("V", [P, NT, D])
        Qblk = sb("Qblk", [P, C, TB, HC, S])
        Vblk = sb("Vblk", [P, NG, TB, HG * HD])
        shifted = sb("shifted", [P, W, NG * TB, S])
        top = sb("top", [P, W * NG * TB])
        weight = sb("weight", [P, W, NG * TB, S])
        rowsum = sb("rowsum", [P, W * NG * TB])
        rinv = sb("rinv", [P, W, NG * TB])
        probs = sb("probs", [P, NG * TB, S])
        PT = sb("PT", [P, NG, P])
        blocked = sb("blocked", [P, 2, TB, NG, HG * HD])

        zT = Transpose(nc, k, name + "_z", k.z, k.zT)
        norm = Norm(nc, k, name + "_norm", 1e-5, k.x, k.z, zT.src_ready)
        if rope:
            rx, rxT = sb("rx", [P, NT, D]), sb("rxT", [P, C, B * S])
            turned = sb("turned", [P, NT, D])
            rT = Transpose(nc, k, name + "_rope", rx, rxT, bank0=4)
        else:
            rxT, rT = k.zT, zT
        weights_loaded, proj_in_done, proj_in_ready = sem("weights_loaded"), sem("proj_in_done"), sem("proj_in_ready")
        qblk_ready, vblk_ready, scores_done, shifted_ready, centred, weight_ready = (
            sem(n) for n in ("qblk_ready", "vblk_ready", "scores_done", "shifted_ready", "centred", "weight_ready"))
        probs_ready, pt_done, pt_ready, av_done, blocked_ready, attn_done, attn_ready, proj_done = (
            sem(n) for n in ("probs_ready", "pt_done", "pt_ready", "av_done", "blocked_ready", "attn_done",
                             "attn_ready", "proj_done"))
        order_sem = sem("vector_order")
        BS, BP, BA, BO = 0, 2, 3, 7
        GB = NG * TB

        def each_tile(eng, body, order=None, per_tile=0):
            body(0, 0)
            body(1, 1)
            with eng.Fori(1, NT // 2 - 1) as pair:
                if order:
                    order.enter(pair - 1, 2 * per_tile)
                for par in range(2):
                    body(pair * 2 + par, par)
                if order:
                    order.leave(NT // 2 - 2)
            body(NT - 2, 0)
            body(NT - 1, 1)

        with nc.Block() as block:
            @block.sync
            def _(sp):
                for t, src in zip((wq, wk, wv, wo), weights):
                    sp.dma_start(t[:, :, :], src.rearrange("(c p) n -> p c n", p=P)).then_inc(weights_loaded, 16)
                sp.dma_start(bo[:, :], ins[bias_name].unsqueeze(0)).then_inc(weights_loaded, 16)

            @block.gpsimd
            def _(pool):
                norm.gpsimd(pool)

                def block_queries(t):
                    if seen(t, 1):
                        pool.wait_ge(scores_done, t)
                        own_wait(pool, k)
                    for c in range(C):
                        last = nc.gpsimd.tensor_tensor(
                            Qblk[:, c, :, :, :],
                            QT[:, c, bass.ds(t * P, P)].rearrange("p (b q) -> p b q", b=TB).unsqueeze(2)
                            .broadcast_to([P, TB, HC, S]),
                            k.const("head_of_row").unsqueeze(1).unsqueeze(3).broadcast_to([P, TB, HC, S]), ALU.mult)
                    last.then_inc(qblk_ready, 1)

                pool.wait_ge(proj_in_ready, 4)
                block_queries(0)
                block_queries(1)
                pool.wait_ge(proj_in_ready, 16)

                def step(t, par):
                    if seen(t, 1):
                        pool.wait_ge(av_done, t)
                        own_wait(pool, k)
                    nc.gpsimd.tensor_tensor(
                        Vblk[:, :, :, :],
                        V[:, bass.ds(t, 1), :].rearrange("p t (g e) -> p (t g) e", g=NG).unsqueeze(2)
                        .broadcast_to([P, NG, TB, HG * HD]),
                        k.const("group_of_row").unsqueeze(1).unsqueeze(3).broadcast_to([P, NG, TB, HG * HD]),
                        ALU.mult).then_inc(vblk_ready, 1)
                    if exists(t + 2, NT):
                        block_queries(t + 2)
                each_tile(pool, step)

            @block.tensor
            def _(pe):
                zT.tensor(pe)
                if rope:
                    rT.tensor(pe)
                pe.wait_ge(weights_loaded, 16 * 5)
                pe.wait_ge(zT.ready, 4)
                pe.wait_ge(rT.ready, 4)
                for n, w in enumerate((wq, wk)):
                    for m in range(C):
                        for half in range(2):
                            for c in range(C):
                                last = nc.tensor.matmul(ps[:, 4 * n + 2 * m + half, :], w[:, c, m * P:(m + 1) * P],
                                                        rxT[:, c, half * 512:(half + 1) * 512],
                                                        start=c == 0, stop=c == C - 1)
                            last.then_inc(proj_in_done, 1)
                for t in range(NT):
                    pe.wait_ge(proj_in_ready, t + 1)
                    for c in range(C):
                        last = nc.tensor.matmul(ps[:, t, 0:D], k.zT[:, c, t * P:(t + 1) * P], wv[:, c, :],
                                                start=c == 0, stop=c == C - 1)
                    last.then_inc(proj_in_done, 1)
                pe.wait_ge(proj_in_ready, 16)

                def scores(t, par):
                    pe.wait_ge(qblk_ready, t + 1)
                    if seen(t, 2):
                        pe.wait_ge(shifted_ready, W * (t - 1))
                    for g in range(NG):
                        c, j = g // 2, g % 2
                        for b in range(TB):
                            last = nc.tensor.matmul(ps[:, BS + par, (g * TB + b) * S:(g * TB + b + 1) * S],
                                                    Qblk[:, c, b, j * HG:(j + 1) * HG, :].rearrange("p h q -> p (h q)"),
                                                    KT[:, c, bass.ds(t * P + b * S, S)], start=True, stop=True)
                    last.then_inc(scores_done, 1)

                def gather_heads(t, par):
                    pe.wait_ge(blocked_ready, NG * t + NG)
                    if isinstance(t, int) and t:
                        pe.wait_ge(attn_ready, t)
                    for c in range(C):
                        for b in range(TB):
                            last = nc.tensor.matmul(ps[:, BO, (c * TB + b) * S:(c * TB + b + 1) * S],
                                                    blocked[:, par, b, 2 * c:2 * c + 2, :].rearrange("p g e -> p (g e)"),
                                                    k.const("query"), start=True, stop=True)
                    last.then_inc(attn_done, 1)

                def step(t, par):
                    pe.wait_ge(probs_ready, t + 1)
                    if seen(t, 1):
                        pe.wait_ge(pt_ready, t)
                    for g in range(NG):
                        last = nc.tensor.transpose(ps[:, BP, g * P:(g + 1) * P],
                                                   probs[:, g * TB:(g + 1) * TB, :].rearrange("p b s -> p (b s)"), k.ident)
                    last.then_inc(pt_done, 1)
                    if seen(t, 2):
                        gather_heads(t - 2, par)
                    pe.wait_ge(pt_ready, t + 1)
                    pe.wait_ge(vblk_ready, t + 1)
                    if seen(t, 2):
                        pe.wait_ge(blocked_ready, NG * (t - 1))
                    for g in range(NG):
                        last = nc.tensor.matmul(ps[:, BA + 2 * par + g // 2, (g % 2) * D:(g % 2 + 1) * D], PT[:, g, :],
                                                Vblk[:, g, :, :].rearrange("p b e -> p (b e)"), start=True, stop=True)
                    last.then_inc(av_done, 1)
                    if exists(t + 2, NT):
                        scores(t + 2, par)

                scores(0, 0)
                scores(1, 1)
                each_tile(pe, step)
                gather_heads(NT - 2, 0)
                gather_heads(NT - 1, 1)
                pe.wait_ge(attn_ready, NT)
                for t in range(NT):
                    nc.tensor.matmul(ps[:, t, 0:D], bias_weight[0:1, :], bo[:, :], start=True, stop=False)
                    for c in range(C):
                        last = nc.tensor.matmul(ps[:, t, 0:D], attnT[:, c, t * P:(t + 1) * P], wo[:, c, :],
                                                start=False, stop=c == C - 1)
                    last.then_inc(proj_done, 1)

            @block.scalar
            def _(act):
                zT.scalar(act)
                if rope:
                    rT.scalar(act)
                for n, dst in enumerate((QT, KT)):
                    for m in range(C):
                        for half in range(2):
                            act.wait_ge(proj_in_done, 4 * n + 2 * m + half + 1)
                            nc.scalar.copy(dst[:, m, half * 512:(half + 1) * 512],
                                           ps[:, 4 * n + 2 * m + half, :]).then_inc(proj_in_ready, 1)
                for t in range(NT):
                    act.wait_ge(proj_in_done, 8 + t + 1)
                    nc.scalar.copy(V[:, t, :], ps[:, t, 0:D]).then_inc(proj_in_ready, 1)

                def exponentials(t):
                    act.wait_ge(centred, t + 1)
                    nc.scalar.activation(weight[:, :, :, :], shifted[:, :, :, :], ACT.Exp, scale=scale
                                         ).then_inc(weight_ready, 1)

                def attention_out(t):
                    act.wait_ge(attn_done, t + 1)
                    own_wait(act, k)
                    nc.scalar.copy(attnT[:, :, bass.ds(t * P, P)],
                                   ps[:, BO, 0:C * P].rearrange("p (c r) -> p c r", c=C)).then_inc(attn_ready, 1)

                def step(t, par):
                    act.wait_ge(pt_done, t + 1)
                    if seen(t, 1):
                        act.wait_ge(av_done, t)
                    nc.scalar.copy(PT[:, :, :].rearrange("p g r -> p (g r)"), ps[:, BP, :]).then_inc(pt_ready, 1)
                    if seen(t, 2):
                        attention_out(t - 2)
                    if exists(t + 1, NT):
                        exponentials(t + 1)
                exponentials(0)
                each_tile(act, step)
                attention_out(NT - 2)
                attention_out(NT - 1)

            @block.vector
            def _(dve):
                order = Count(dve, order_sem)
                norm.vector(dve, order)
                if rope:
                    dve.wait_ge(zT.src_ready, NT)
                    cos = k.const("cos").unsqueeze(1).broadcast_to([P, NT, D])
                    sin = k.const("sin").rearrange("p (i two) -> p i two", two=2)
                    zp = k.z[:, :, :].rearrange("p t (i two) -> p t i two", two=2)
                    tp = turned[:, :, :].rearrange("p t (i two) -> p t i two", two=2)
                    for side in range(2):
                        last = nc.vector.tensor_tensor(
                            tp[:, :, :, side], zp[:, :, :, 1 - side],
                            sin[:, :, side].unsqueeze(1).broadcast_to([P, NT, D // 2]), ALU.mult)
                    order.after(last)
                    order.after(nc.vector.tensor_tensor(rx[:, :, :], k.z[:, :, :], cos, ALU.mult))
                    for t in range(NT):
                        nc.vector.tensor_tensor(rx[:, t, :], rx[:, t, :], turned[:, t, :], ALU.add
                                                ).then_inc(rT.src_ready, 1)
                zT.vector(dve)
                if rope:
                    rT.vector(dve)

                def centre(t, par):
                    dve.wait_ge(scores_done, t + 1)
                    for w, pen in enumerate(windows):
                        nc.vector.tensor_tensor(shifted[:, w, :, :], ps[:, BS + par, :].rearrange("p (n s) -> p n s", s=S),
                                                pen.unsqueeze(1).broadcast_to([P, GB, S]), ALU.add
                                                ).then_inc(shifted_ready, 1)
                    dve.wait_ge(shifted_ready, W * t + W)
                    flat = shifted[:, :, :, :].rearrange("p w n s -> p (w n) s")
                    order.after(nc.vector.tensor_reduce(top[:, :], flat, AX.X, ALU.max))
                    nc.vector.tensor_tensor(flat, flat, top[:, :].unsqueeze(2).broadcast_to([P, W * GB, S]), ALU.subtract
                                            ).then_inc(centred, 1)

                def probabilities(t):
                    dve.wait_ge(weight_ready, t + 1)
                    order.after(nc.vector.tensor_reduce(rowsum[:, :], weight[:, :, :, :].rearrange("p w n s -> p (w n) s"),
                                                        AX.X, ALU.add))
                    order.after(nc.vector.reciprocal(rinv[:, :, :].rearrange("p w n -> p (w n)"), rowsum[:, :]))
                    if W == 2:
                        order.after(nc.vector.tensor_tensor(rinv[:, :, :], rinv[:, :, :],
                                                            k.const("window_on").unsqueeze(2).broadcast_to([P, W, GB]),
                                                            ALU.mult))
                    if seen(t, 1):
                        dve.wait_ge(pt_done, t)
                    if W == 1:
                        nc.vector.tensor_tensor(probs[:, :, :], weight[:, 0, :, :],
                                                rinv[:, 0, :].unsqueeze(2).broadcast_to([P, GB, S]), ALU.mult
                                                ).then_inc(probs_ready, 1)
                    else:
                        order.after(nc.vector.tensor_tensor(weight[:, :, :, :], weight[:, :, :, :],
                                                            rinv[:, :, :].unsqueeze(3).broadcast_to([P, W, GB, S]), ALU.mult))
                        nc.vector.tensor_tensor(probs[:, :, :], weight[:, 0, :, :], weight[:, 1, :, :], ALU.add
                                                ).then_inc(probs_ready, 1)

                def block_attention(t, par):
                    dve.wait_ge(av_done, t + 1)
                    for g in range(NG):
                        nc.vector.tensor_tensor(
                            blocked[:, par, :, g, :].rearrange("p b (h d) -> p b h d", h=HG),
                            ps[:, BA + 2 * par + g // 2, (g % 2) * D:(g % 2 + 1) * D]
                            .rearrange("p (b h d) -> p b h d", h=HG, d=HD),
                            k.const("group_of_row").unsqueeze(1).unsqueeze(3).broadcast_to([P, TB, HG, HD]),
                            ALU.mult).then_inc(blocked_ready, 1)

                def step(t, par):
                    probabilities(t)
                    if exists(t + 1, NT):
                        centre(t + 1, 1 - par)
                    if seen(t, 1):
                        block_attention(t - 1, 1 - par)
                centre(0, 0)
                each_tile(dve, step, order, 3 if W == 1 else 5)
                block_attention(NT - 1, 1)
                add_projection(nc, k, dve, proj_done)


def local_attention(nc, k):
    w = k.ins["L0_attn_w_qkv"]
    pen = k.const("window_pen").rearrange("p (w s) -> p w s", w=2)
    self_attention(nc, k, "la", [w[:, 0:D], w[:, D:2 * D], w[:, 2 * D:3 * D], k.ins["L0_attn_w_out"]], float(D) ** -0.5,
                   [pen[:, 0, :], pen[:, 1, :]], False, "L0_attn_b_out", k.const("window_count"))


def slot_attention(nc, k):
    ins, ps = k.ins, k.ps
    with ExitStack() as ctx:
        def sb(n, shape, dt=F32):
            return ctx.enter_context(nc.sbuf_tensor("sa_" + n, shape, dt))

        def sem(n):
            return k.sem("sa_" + n)

        def pair_of(f, n, *more):
            return [f(n + str(i), *more) for i in range(2)]

        G = 3 * D
        PARTS = 3
        wq, wk, wv = (sb(n, [P, C, D]) for n in ("wq", "wk", "wv"))
        wihT, whhT, wvi = (sb(n, [P, C, G]) for n in ("wihT", "whhT", "wvi"))
        wqk = sb("wqk", [P, C, D])
        bih, bhh = sb("bih", [PARTS, G]), sb("bhh", [PARTS, G])
        bias, kept, parts = sb("bias", [PARTS, 4 * D]), sb("kept", [PARTS, 4 * D]), sb("parts", [PARTS, 4 * D])
        high = sb("high", [PARTS, 4 * D], BF16)
        bias_parts = sb("bias_parts", [PARTS, 4 * D], BF16)
        ones_parts = sb("ones_parts", [PARTS, P], BF16)
        w_slot, w_in = sb("w_slot", [P, C]), sb("w_in", [P, C])
        last_rows = sb("last_rows", [P, D])
        lastT = sb("lastT", [P, C, P])
        last_st, last_mv, last_ms = sb("last_st", [P, 6]), sb("last_mv", [P, 2]), sb("last_ms", [P, 1])
        rows = pair_of(sb, "rows", [P, TB * KT2, D])
        ctxT = pair_of(sb, "ctxT", [P, C, TB, KEYS])
        cst = pair_of(sb, "cst", [P, TB * KT2, 6])
        cmv = pair_of(sb, "cmv", [P, TB * KT2, 2])
        rms = pair_of(sb, "rms", [P, TB, 3])
        slots = pair_of(sb, "slots", [P, D])
        squares, total_sq, srs = pair_of(sb, "squares", [P, D]), pair_of(sb, "total_sq", [P, 1]), pair_of(sb, "srs", [P, 1])
        srs_diag = pair_of(sb, "srs_diag", [P, P])
        slotsT = pair_of(sb, "slotsT", [P, C, P])
        qT = pair_of(sb, "qT", [P, C, P])
        top, total, inv, invr = (pair_of(sb, n, [P, TB * 3]) for n in ("top", "total", "inv", "invr"))
        e, share, weight = (pair_of(sb, n, [P, TB * 3, S]) for n in ("e", "share", "weight"))
        shifted = pair_of(sb, "shifted", [P, TB * 3, S])
        colinv = pair_of(sb, "colinv", [P, P])
        uT = pair_of(sb, "uT", [P, C, P])
        trz = pair_of(sb, "trz", [P, 2 * D])
        pre, cand, diff = (pair_of(sb, n, [P, D]) for n in ("pre", "cand", "diff"))
        srsR = pair_of(sb, "srsR", [P, P])

        norm = Norm(nc, k, "sa_norm", 1e-5, k.x, k.z)
        weights_loaded, zeroed, last_loaded, fold_done, fold_ready, bias_ready = (
            sem(n) for n in ("weights_loaded", "zeroed", "last_loaded", "fold_done", "fold_ready", "bias_ready"))
        ctxT_loaded, rows_loaded = pair_of(sem, "ctxT_loaded"), pair_of(sem, "rows_loaded")
        (ms_ready, mse_ready, rms_ready, slots_ready, sq_ready, srs_ready, diag_ready, turn_done, turn_ready, q_done,
         q_ready, scores_done, centred, e_ready, inv_ready, share_ready, weight_ready, u_done, uT_ready, gates_done,
         trz_ready, pre_ready, cand_ready) = (
            pair_of(sem, n) for n in (
                "ms_ready", "mse_ready", "rms_ready", "slots_ready", "sq_ready", "srs_ready", "diag_ready", "turn_done",
                "turn_ready", "q_done", "q_ready", "scores_done", "centred", "e_ready", "inv_ready", "share_ready",
                "weight_ready", "u_done", "uT_ready", "gates_done", "trz_ready", "pre_ready", "cand_ready"))
        order_sem = sem("vector_order")
        ROUNDS, PAIRS = 3, NT // 2
        BA, BB, BR, BN = 0, 1, 2, 3

        def bank(par, n):
            return ps[:, 4 * par + n, :]

        def all_rounds(eng, round_, order=None, per_pair=0):
            with eng.Fori(0, PAIRS - 1) as pair:
                if order:
                    order.enter(pair, per_pair)
                for r in range(ROUNDS):
                    round_(pair, r, pair * ROUNDS + r, True)
                if order:
                    order.leave(PAIRS - 1)
            for r in range(ROUNDS):
                round_(PAIRS - 1, r, (PAIRS - 1) * ROUNDS + r, r < ROUNDS - 1)

        with nc.Block() as block:
            @block.sync
            def _(sp):
                for t, n in ((wq, "Wq"), (wk, "Wk"), (wv, "Wv"), (wihT, "gru_wihT"), (whhT, "gru_whhT")):
                    sp.dma_start(t[:, :, :], ins["L1_xattn_" + n].rearrange("(c p) n -> p c n", p=P)
                                 ).then_inc(weights_loaded, 16)
                for t, n in ((bih, "gru_bih"), (bhh, "gru_bhh")):
                    sp.dma_start(t[:, :], ins["L1_xattn_" + n].partition_broadcast(PARTS)).then_inc(weights_loaded, 16)
                for t, n in ((w_slot, "slot_norm_w"), (w_in, "input_norm_w")):
                    sp.dma_start(t[:, :], ins["L1_xattn_" + n]).then_inc(weights_loaded, 16)
                sp.wait_ge(zeroed, 2)
                sp.dma_start(last_rows[0:B, :], ins["ctx"][:, KEYS - 1, :]).then_inc(last_loaded, 16)
                for c in range(C):
                    sp.dma_start(lastT[:, c, 0:B], ins["ctx_lastT"][c * P:(c + 1) * P, :]).then_inc(last_loaded, 16)

                def load_ctxT(pair, par):
                    for c in range(C):
                        sp.dma_start(ctxT[par][:, c, :, :],
                                     ins["ctxT"][c * P:(c + 1) * P, bass.ds((pair * 2 + par) * TB, TB), :]
                                     ).then_inc(ctxT_loaded[par], 16)

                def load_rows(pair, par):
                    for b in range(TB):
                        sp.dma_start(rows[par][:, b * KT2:(b + 1) * KT2, :],
                                     ins["ctx"][bass.ds((pair * 2 + par) * TB + b, 1), 0:KT2 * P, :]
                                     .rearrange("b (t p) d -> p (b t) d", p=P)).then_inc(rows_loaded[par], 16)
                for par in range(2):
                    load_rows(0, par)
                    load_ctxT(0, par)
                with sp.Fori(1, PAIRS) as pair:
                    for par in range(2):
                        sp.wait_ge(scores_done[par], pair * ROUNDS)
                        load_ctxT(pair, par)
                        sp.wait_ge(u_done[par], pair * ROUNDS)
                        load_rows(pair, par)

            @block.gpsimd
            def _(pool):
                nc.gpsimd.memset(last_rows[:, :], 0.0).then_inc(zeroed, 1)
                nc.gpsimd.memset(lastT[:, :, :], 0.0).then_inc(zeroed, 1)
                norm.gpsimd(pool)

                def context_rms(pair, par):
                    pool.wait_ge(ms_ready[par], pair + 1)
                    own_wait(pool, k)
                    nc.gpsimd.tensor_scalar(rms[par][:, :, :], rms[par][:, :, :], 1e-6, None, ALU.add
                                            ).then_inc(mse_ready[par], 1)
                    pool.wait_ge(mse_ready[par], pair + 1)
                    own_wait(pool, k)
                    nc.gpsimd.tensor_tensor(rms[par][:, :, :].rearrange("p b t -> p (b t)"),
                                            rms[par][:, :, :].rearrange("p b t -> p (b t)"),
                                            k.const("minus_half")[:, 0:TB * 3], ALU.pow).then_inc(rms_ready[par], 1)

                def slot_rms(n, par):
                    pool.wait_ge(sq_ready[par], n + 1)
                    own_wait(pool, k)
                    nc.gpsimd.tensor_tensor(srs[par][:, :], total_sq[par][:, :], k.const("minus_half")[:, 0:1], ALU.pow
                                            ).then_inc(srs_ready[par], 1)
                    pool.wait_ge(srs_ready[par], n + 1)
                    own_wait(pool, k)
                    nc.gpsimd.tensor_tensor(srs_diag[par][:, :], k.ident, srs[par][:, :].broadcast_to([P, P]), ALU.mult
                                            ).then_inc(diag_ready[par], 1)

                def weights(n, par):
                    pool.wait_ge(inv_ready[par], n + 1)
                    own_wait(pool, k)
                    nc.gpsimd.tensor_tensor(weight[par][:, :, :], e[par][:, :, :],
                                            invr[par][:, :].unsqueeze(2).broadcast_to([P, TB * 3, S]), ALU.mult
                                            ).then_inc(weight_ready[par], 1)
                slot_rms(0, 0)
                context_rms(0, 0)
                weights(0, 0)

                def round_(pair, r, n, follows):
                    slot_rms(n, 1)
                    if r == 0:
                        context_rms(pair, 1)
                    if follows:
                        slot_rms(n + 1, 0)
                    weights(n, 1)
                    if follows:
                        if r == ROUNDS - 1:
                            context_rms(pair + 1, 0)
                        weights(n + 1, 0)
                all_rounds(pool, round_)

            @block.tensor
            def _(pe):
                pe.wait_ge(weights_loaded, 16 * 9)
                for m in range(C):
                    for c in range(C):
                        last = nc.tensor.matmul(ps[:, m, 0:D], wq[:, c, m * P:(m + 1) * P], wk[:, c, :],
                                                start=c == 0, stop=c == C - 1)
                    last.then_inc(fold_done, 1)
                for m in range(C):
                    for j, (lo, hi) in enumerate(((0, 2 * D), (2 * D, 3 * D))):
                        for c in range(C):
                            last = nc.tensor.matmul(ps[:, 2 + 2 * m + j, 0:hi - lo], wv[:, c, m * P:(m + 1) * P],
                                                    wihT[:, c, lo:hi], start=c == 0, stop=c == C - 1)
                        last.then_inc(fold_done, 1)
                pe.wait_ge(fold_ready, 6)
                pe.wait_ge(bias_ready, 2)
                pe.wait_ge(last_loaded, 16 * 3)

                def turn(n, par):
                    pe.wait_ge(slots_ready[par], n + 1)
                    for c in range(C):
                        last = nc.tensor.transpose(bank(par, BA)[:, c * P:(c + 1) * P], slots[par][:, c * P:(c + 1) * P],
                                                   k.ident)
                    last.then_inc(turn_done[par], 1)

                def queries(n, par):
                    pe.wait_ge(turn_ready[par], n + 1)
                    for m in range(C):
                        for c in range(C):
                            nc.tensor.matmul(bank(par, BB)[:, m * P:(m + 1) * P], wqk[:, c, m * P:(m + 1) * P],
                                             slotsT[par][:, c, :], start=c == 0, stop=c == C - 1)
                    pe.wait_ge(diag_ready[par], n + 1)
                    nc.tensor.matmul(bank(par, BB)[:, 2 * P:3 * P], k.const("ones"), srs_diag[par][:, :],
                                     start=True, stop=True).then_inc(q_done[par], 1)

                def scores(pair, n, par):
                    pe.wait_ge(ctxT_loaded[par], 16 * C * (pair + 1))
                    pe.wait_ge(q_ready[par], C * n + C)
                    for b in range(TB):
                        for t in range(KT2):
                            for c in range(C):
                                nc.tensor.matmul(bank(par, BA)[:, (b * 3 + t) * S:(b * 3 + t + 1) * S],
                                                 ctxT[par][:, c, b, t * P:(t + 1) * P],
                                                 qT[par][:, c, b * S:(b + 1) * S], start=c == 0, stop=c == C - 1)
                    lastcol = bank(par, BA)[:, 0:TB * 3 * S].rearrange("p (b t s) -> p b t s", b=TB, t=3)[:, :, 2, :]
                    for c in range(C):
                        last = nc.tensor.matmul(lastcol, lastT[:, c, :], qT[par][:, c, :].rearrange("p (b s) -> p b s", b=TB),
                                                start=c == 0, stop=c == C - 1)
                    last.then_inc(scores_done[par], 1)

                def hidden_rz(par):
                    nc.tensor.matmul(bank(par, BR), ones_parts[:, :], bias_parts[:, 0:2 * D], start=True, stop=False,
                                     skip_group_check=True)
                    for c in range(C):
                        nc.tensor.matmul(bank(par, BR), slotsT[par][:, c, :], whhT[:, c, 0:2 * D], start=False, stop=False,
                                         skip_group_check=True)

                def hidden_n(par):
                    nc.tensor.matmul(bank(par, BN), ones_parts[:, :], bias_parts[:, 2 * D:4 * D], start=True, stop=False,
                                     skip_group_check=True)
                    for c in range(C):
                        nc.tensor.matmul(bank(par, BN)[:, D:2 * D], slotsT[par][:, c, :], whhT[:, c, 2 * D:3 * D],
                                         start=False, stop=c == C - 1, skip_group_check=True)

                def totals(n, par):
                    pe.wait_ge(share_ready[par], n + 1)
                    grid = share[par][:, :, :].rearrange("p (b t) s -> p b t s", t=3)
                    for t in range(3):
                        nc.tensor.matmul(bank(par, BB)[:, 2 * P:3 * P], k.const("ones"), grid[:, :, t, :],
                                         start=t == 0, stop=t == 2)

                def updates(pair, n, par):
                    pe.wait_ge(rows_loaded[par], 16 * TB * (pair + 1))
                    pe.wait_ge(weight_ready[par], n + 1)
                    grid = weight[par][:, :, :].rearrange("p (b t) s -> p b t s", t=3)
                    for c in range(C):
                        nc.tensor.matmul(bank(par, BB)[:, c * P:(c + 1) * P], last_rows[:, c * P:(c + 1) * P],
                                         grid[:, :, 2, :], start=True, stop=False, skip_group_check=True)
                        for b in range(TB):
                            for t in range(KT2):
                                last = nc.tensor.matmul(
                                    bank(par, BB)[:, c * P + b * S:c * P + (b + 1) * S],
                                    rows[par][:, b * KT2 + t, c * P:(c + 1) * P], weight[par][:, b * 3 + t, :],
                                    start=False, stop=b == TB - 1 and t == KT2 - 1, skip_group_check=True)
                    last.then_inc(u_done[par], 1)

                def gates(n, par):
                    pe.wait_ge(uT_ready[par], n + 1)
                    for c in range(C):
                        nc.tensor.matmul(bank(par, BR), uT[par][:, c, :], wvi[:, c, 0:2 * D],
                                         start=False, stop=c == C - 1, skip_group_check=True)
                    for c in range(C):
                        last = nc.tensor.matmul(bank(par, BN)[:, 0:D], uT[par][:, c, :], wvi[:, c, 2 * D:3 * D],
                                                start=False, stop=c == C - 1, skip_group_check=True)
                    last.then_inc(gates_done[par], 1)

                turn(0, 0)
                queries(0, 0)
                scores(0, 0, 0)
                hidden_rz(0)
                hidden_n(0)

                def round_(pair, r, n, follows):
                    totals(n, 0)
                    updates(pair, n, 0)
                    turn(n, 1)
                    queries(n, 1)
                    gates(n, 0)
                    scores(pair, n, 1)
                    hidden_rz(1)
                    if follows:
                        turn(n + 1, 0)
                    hidden_n(1)
                    if follows:
                        queries(n + 1, 0)
                    totals(n, 1)
                    if follows:
                        scores(pair + 1 if r == ROUNDS - 1 else pair, n + 1, 0)
                    updates(pair, n, 1)
                    if follows:
                        hidden_rz(0)
                        hidden_n(0)
                    gates(n, 1)
                all_rounds(pe, round_)

            @block.scalar
            def _(act):
                act.wait_ge(weights_loaded, 16 * 9)
                for m in range(C):
                    act.wait_ge(fold_done, m + 1)
                    nc.scalar.activation(wqk[:, m, :], ps[:, m, 0:D], ACT.Copy, scale=w_slot[:, m:m + 1]
                                         ).then_inc(fold_ready, 1)
                for m in range(C):
                    for j, (lo, hi) in enumerate(((0, 2 * D), (2 * D, 3 * D))):
                        act.wait_ge(fold_done, 2 + 2 * m + j + 1)
                        nc.scalar.activation(wvi[:, m, lo:hi], ps[:, 2 + 2 * m + j, 0:hi - lo], ACT.Copy,
                                             scale=w_in[:, m:m + 1]).then_inc(fold_ready, 1)

                def turned(n, par):
                    act.wait_ge(turn_done[par], n + 1)
                    nc.scalar.copy(slotsT[par][:, :, :].rearrange("p c n -> p (c n)"), bank(par, BA)[:, 0:C * P]
                                   ).then_inc(turn_ready[par], 1)

                def exponentials(n, par):
                    act.wait_ge(centred[par], n + 1)
                    nc.scalar.activation(e[par][:, :, :], shifted[par][:, :, :], ACT.Exp).then_inc(e_ready[par], 1)

                def tanhs(n, par):
                    act.wait_ge(gates_done[par], n + 1)
                    nc.scalar.activation(trz[par][:, :], bank(par, BR), ACT.Tanh, scale=0.5).then_inc(trz_ready[par], 1)
                    act.wait_ge(pre_ready[par], n + 1)
                    nc.scalar.activation(cand[par][:, :], pre[par][:, :], ACT.Tanh).then_inc(cand_ready[par], 1)
                turned(0, 0)
                exponentials(0, 0)

                def round_(pair, r, n, follows):
                    turned(n, 1)
                    tanhs(n, 0)
                    exponentials(n, 1)
                    if follows:
                        turned(n + 1, 0)
                        exponentials(n + 1, 0)
                    tanhs(n, 1)
                all_rounds(act, round_)

            @block.vector
            def _(dve):
                order = Count(dve, order_sem)
                norm.vector(dve, order)
                dve.wait_ge(norm.dst_ready, NT)
                wide = [P, TB * 3, S]

                def square(par):
                    own_wait(dve, k)
                    nc.vector.tensor_tensor_reduce(out=squares[par][:, :], in0=slots[par][:, :], in1=slots[par][:, :],
                                                   scale=1.0, scalar=D * 1e-6, op0=ALU.mult, op1=ALU.add,
                                                   accum_out=total_sq[par][:, :]).then_inc(sq_ready[par], 1)

                def context_squares(pair, par):
                    dve.wait_ge(rows_loaded[par], 16 * TB * (pair + 1))
                    own_wait(dve, k)
                    for i in range(TB * KT2):
                        last = nc.vector.bn_stats(cst[par][:, i, :], rows[par][:, i, :])
                    order.after(last)
                    own_wait(dve, k)
                    for i in range(TB * KT2):
                        last = nc.vector.bn_aggr(cmv[par][:, i, :], cst[par][:, i, :])
                    order.after(last)
                    mean = cmv[par][:, :, 0].rearrange("p (b t) -> p b t", b=TB)
                    order.after(nc.vector.tensor_tensor(rms[par][:, :, 0:KT2], mean, mean, ALU.mult))
                    nc.vector.tensor_tensor(rms[par][:, :, 0:KT2], rms[par][:, :, 0:KT2],
                                            cmv[par][:, :, 1].rearrange("p (b t) -> p b t", b=TB), ALU.add)
                    nc.vector.tensor_copy(rms[par][:, :, 2], last_ms[:, :].broadcast_to([P, TB])
                                          ).then_inc(ms_ready[par], 1)

                def queries_out(n, par):
                    dve.wait_ge(q_done[par], n + 1)
                    order.after(nc.vector.tensor_copy(srsR[par][:, :], bank(par, BB)[:, 2 * P:3 * P]))
                    for m in range(C):
                        nc.vector.scalar_tensor_tensor(out=qT[par][:, m, :], in0=bank(par, BB)[:, m * P:(m + 1) * P],
                                                       scalar=w_in[:, m:m + 1], in1=srsR[par][:, :],
                                                       op0=ALU.mult, op1=ALU.mult).then_inc(q_ready[par], 1)

                def centre(pair, n, par):
                    dve.wait_ge(scores_done[par], n + 1)
                    sc = bank(par, BA)[:, 0:TB * 3 * S].rearrange("p (n s) -> p n s", s=S)
                    order.after(nc.vector.tensor_reduce(top[par][:, :], sc, AX.X, ALU.max))
                    order.after(nc.vector.tensor_tensor(shifted[par][:, :, :], sc, top[par][:, :].unsqueeze(2)
                                                        .broadcast_to(wide), ALU.subtract))
                    dve.wait_ge(rms_ready[par], pair + 1)
                    nc.vector.tensor_tensor(shifted[par][:, :, :], shifted[par][:, :, :],
                                            rms[par][:, :, :].rearrange("p b t -> p (b t)").unsqueeze(2)
                                            .broadcast_to(wide), ALU.mult).then_inc(centred[par], 1)

                def shares(pair, n, par):
                    dve.wait_ge(e_ready[par], n + 1)
                    order.after(nc.vector.tensor_reduce(total[par][:, :], e[par][:, :, :], AX.X, ALU.add))
                    order.after(nc.vector.reciprocal(inv[par][:, :], total[par][:, :]))
                    order.after(nc.vector.tensor_tensor(inv[par][:, :], inv[par][:, :],
                                                        k.const("last_key")[:, bass.ds((pair * 2 + par) * TB * 3, TB * 3)],
                                                        ALU.mult))
                    nc.vector.tensor_tensor(invr[par][:, :], inv[par][:, :],
                                            rms[par][:, :, :].rearrange("p b t -> p (b t)"), ALU.mult
                                            ).then_inc(inv_ready[par], 1)
                    nc.vector.tensor_tensor(share[par][:, :, :], e[par][:, :, :],
                                            inv[par][:, :].unsqueeze(2).broadcast_to(wide), ALU.mult
                                            ).then_inc(share_ready[par], 1)

                def updates_out(n, par):
                    dve.wait_ge(u_done[par], n + 1)
                    order.after(nc.vector.tensor_scalar(colinv[par][:, :], bank(par, BB)[:, 2 * P:3 * P], 1e-6, None,
                                                        ALU.add))
                    order.after(nc.vector.reciprocal(colinv[par][:, :], colinv[par][:, :]))
                    nc.vector.tensor_tensor(uT[par][:, :, :], bank(par, BB)[:, 0:2 * P].rearrange("p (c n) -> p c n", c=C),
                                            colinv[par][:, :].unsqueeze(1).broadcast_to([P, C, P]), ALU.mult
                                            ).then_inc(uT_ready[par], 1)

                def new_slots(pair, r, n, par, follows):
                    dve.wait_ge(trz_ready[par], n + 1)
                    order.after(nc.vector.scalar_tensor_tensor(out=pre[par][:, :], in0=trz[par][:, 0:D], scalar=1.0,
                                                               in1=bank(par, BN)[:, D:2 * D], op0=ALU.add, op1=ALU.mult))
                    nc.vector.scalar_tensor_tensor(out=pre[par][:, :], in0=pre[par][:, :], scalar=0.5,
                                                   in1=bank(par, BN)[:, 0:D], op0=ALU.mult, op1=ALU.add
                                                   ).then_inc(pre_ready[par], 1)
                    dve.wait_ge(cand_ready[par], n + 1)
                    order.after(nc.vector.tensor_tensor(diff[par][:, :], slots[par][:, :], cand[par][:, :], ALU.subtract))
                    order.after(nc.vector.scalar_tensor_tensor(out=diff[par][:, :], in0=trz[par][:, D:2 * D], scalar=1.0,
                                                               in1=diff[par][:, :], op0=ALU.add, op1=ALU.mult))
                    last = nc.vector.scalar_tensor_tensor(out=slots[par][:, :], in0=diff[par][:, :], scalar=0.5,
                                                          in1=cand[par][:, :], op0=ALU.mult, op1=ALU.add)
                    if r < ROUNDS - 1:
                        last.then_inc(slots_ready[par], 1)
                        dve.wait_ge(slots_ready[par], n + 2)
                        square(par)
                        return
                    order.after(last)
                    tile = bass.ds(pair * 2 + par, 1)
                    last = nc.vector.tensor_tensor(k.x[:, tile, :].rearrange("p t d -> p (t d)"),
                                                   k.x[:, tile, :].rearrange("p t d -> p (t d)"), slots[par][:, :], ALU.add)
                    if follows:
                        order.after(last)
                        nc.vector.tensor_copy(slots[par][:, :], k.z[:, bass.ds(pair * 2 + 2 + par, 1), :]
                                              .rearrange("p t d -> p (t d)")).then_inc(slots_ready[par], 1)
                        dve.wait_ge(slots_ready[par], n + 2)
                        square(par)

                for par in range(2):
                    nc.vector.tensor_copy(slots[par][:, :], k.z[:, par, :]).then_inc(slots_ready[par], 1)
                for par in range(2):
                    dve.wait_ge(slots_ready[par], 1)
                    square(par)
                dve.wait_ge(weights_loaded, 16 * 9)
                nc.vector.tensor_tensor(bias[:, 0:2 * D], bih[:, 0:2 * D], bhh[:, 0:2 * D], ALU.add)
                nc.vector.tensor_copy(bias[:, 2 * D:3 * D], bih[:, 2 * D:3 * D])
                order.after(nc.vector.tensor_copy(bias[:, 3 * D:4 * D], bhh[:, 2 * D:3 * D]))
                nc.vector.tensor_copy(ones_parts[:, :], k.const("ones")[0:PARTS, :]).then_inc(bias_ready, 1)
                own = [k.ident[0:PARTS, i:i + 1] for i in range(PARTS)]
                order.after(nc.vector.tensor_copy(high[:, :], bias[:, :]))
                order.after(nc.vector.tensor_scalar(parts[:, :], high[:, :], own[0], None, ALU.mult))
                order.after(nc.vector.tensor_tensor(bias[:, :], bias[:, :], high[:, :], ALU.subtract))
                order.after(nc.vector.tensor_copy(high[:, :], bias[:, :]))
                order.after(nc.vector.scalar_tensor_tensor(out=parts[:, :], in0=high[:, :], scalar=own[1], in1=parts[:, :],
                                                           op0=ALU.mult, op1=ALU.add))
                order.after(nc.vector.tensor_tensor(bias[:, :], bias[:, :], high[:, :], ALU.subtract))
                nc.vector.scalar_tensor_tensor(out=bias_parts[:, :], in0=bias[:, :], scalar=own[2], in1=parts[:, :],
                                               op0=ALU.mult, op1=ALU.add).then_inc(bias_ready, 1)
                dve.wait_ge(last_loaded, 16 * 3)
                order.after(nc.vector.bn_stats(last_st[:, :], last_rows[:, :]))
                order.after(nc.vector.bn_aggr(last_mv[:, :], last_st[:, :]))
                order.after(nc.vector.scalar_tensor_tensor(out=last_ms[:, :], in0=last_mv[:, 0:1], scalar=last_mv[:, 0:1],
                                                           in1=last_mv[:, 1:2], op0=ALU.mult, op1=ALU.add))
                queries_out(0, 0)
                context_squares(0, 0)
                centre(0, 0, 0)
                shares(0, 0, 0)

                def round_(pair, r, n, follows):
                    updates_out(n, 0)
                    queries_out(n, 1)
                    if r == 0:
                        context_squares(pair, 1)
                    new_slots(pair, r, n, 0, follows)
                    centre(pair, n, 1)
                    shares(pair, n, 1)
                    if follows:
                        next_pair = pair + 1 if r == ROUNDS - 1 else pair
                        queries_out(n + 1, 0)
                        if r == ROUNDS - 1:
                            context_squares(pair + 1, 0)
                        centre(next_pair, n + 1, 0)
                        shares(next_pair, n + 1, 0)
                    updates_out(n, 1)
                    new_slots(pair, r, n, 1, follows)
                all_rounds(dve, round_, order, 2 * (ROUNDS * (1 + 2 + 3 + 2 + 3) + 3 + 2))


def causal_attention(nc, k):
    self_attention(nc, k, "ra", [k.ins["L1_attn_" + n] for n in ("WqT", "WkT", "WvT", "WoT")], float(HD) ** -0.5,
                   [k.const("causal_pen")], True, "L1_attn_bo", k.const("ones"))


def per_slot(eng, body):
    body(0, 0, 0, True)
    body(1, 0, 1, True)
    with eng.Fori(1, SLOTS // 2) as pair:
        for par in range(2):
            body(pair * 2 + par, pair, par, True)
    body(SLOTS - 1, SLOTS // 2, 0, False)


def experts(nc, k, name, gated):
    ins, ps = k.ins, k.ps
    pre = "L1_ffn_" if gated else "L0_ffn_"
    with ExitStack() as ctx:
        def sb(n, shape, dt=F32):
            return ctx.enter_context(nc.sbuf_tensor(name + "_" + n, shape, dt))

        def sem(n):
            return k.sem(name + "_" + n)

        w_route = sb("w_route", [P, C, E])
        b_route = sb("b_route", [P, E])
        logits, rest, tie, first, second, both = (
            sb(n, [P, NT, E]) for n in ("logits", "rest", "tie", "first", "second", "both"))
        best = sb("best", [P, 4, NT])
        gap, share1, share2 = (sb(n, [P, NT]) for n in ("gap", "share1", "share2"))
        counted = sb("counted", [P, 2, NT, E])
        earlier = sb("earlier", [P, NT + 1, E])
        over = sb("over", [P, E, SLOTS_EACH])
        slots_of = sb("slots_of", [P, E])
        start_of = sb("start_of", [P, E])
        place = sb("place", [P, NT, E])
        at = sb("at", [P, 2, NT])
        row = sb("row", [P, 2, NT], I32)
        begun = sb("begun", [P, SLOTS, E])
        expert_f = sb("expert_f", [P, SLOTS])
        expert = sb("expert", [P, SLOTS], I32)

        win = [sb("win%d" % i, [P, 2, C, FF]) for i in range(1 + gated)]
        bin_ = [sb("bin%d" % i, [P, 2, FF // P]) for i in range(1 + gated)]
        wout = sb("wout", [P, 2, FF // P, D])
        bout = sb("bout", [P, 2, D])
        rows = sb("rows", [P, 2, SLOT // P, D])
        xT = sb("xT", [P, C, SLOT])
        hT = sb("hT", [P, 2, FF // P, SLOT])
        y = sb("y", [P, 2, SLOT // P, D])
        mixed1, mixed2 = sb("mixed1", [P, NT, D]), sb("mixed2", [P, NT, D])
        if gated:
            halfb = sb("halfb", [P, 2, FF // P])
            gelu, tanh = (sb(n, [P, 2, SLOT]) for n in ("gelu", "tanh"))
            g_e, b_e = sb("g_e", [P, 2, D]), sb("b_e", [P, 2, D])
            rbias = sb("rbias", [P, 2, SLOT // P, D])
            resid = sb("resid", [P, SLOT // P, D])
            st = sb("st", [P, SLOT // P, 6])
            mv = sb("mv", [P, SLOT // P, 2])
            rs = sb("rs", [P, SLOT // P])
        else:
            gamma, beta = sb("gamma", [P, D]), sb("beta", [P, D])

        zT = Transpose(nc, k, name + "_z", k.z, k.zT)
        norm = Norm(nc, k, name + "_norm", 1e-5, k.x, k.z, zT.src_ready)
        norm2 = None if gated else Norm(nc, k, name + "_norm2", 1e-5, mixed1, mixed1)
        route_loaded = sem("route_loaded")
        small_loaded, logits_done, gap_ready, exp_ready, both_ready, counted_done, rows_known, scattered = (
            sem(n) for n in ("small_loaded", "logits_done", "gap_ready", "exp_ready", "both_ready", "counted_done",
                             "rows_known", "scattered"))
        rows_loaded, in_loaded, out_loaded = (
            [sem(n + "0"), sem(n + "1")] for n in ("rows_loaded", "in_loaded", "out_loaded"))
        xt_done, xt_ready, h_done, h_ready, y_done, y_read, y_ready = (
            sem(n) for n in ("xt_done", "xt_ready", "h_done", "h_ready", "y_done", "y_read", "y_ready"))
        y_stored = [sem("y_stored0"), sem("y_stored1")]
        gathered = [sem("gathered0"), sem("gathered1")]
        order_sem = sem("vector_order")
        if gated:
            halfb_ready, act_done, rbias_ready = (
                sem(n) for n in ("halfb_ready", "act_done", "rbias_ready"))
            rstats_ready, rvar_ready, rrstd_ready = (sem(n) for n in ("rstats_ready", "rvar_ready", "rrstd_ready"))
        HB, XB, YB = 0, 4, 5
        HC_N = FF // P
        PER_IN, PER_OUT = (4, 4) if gated else (2, 2)
        ff_names = ("Wi", "Wg") if gated else ("W1",)
        fb_names = ("bi", "bg") if gated else ("b1",)
        out_w, out_b = ("Wo", "bo") if gated else ("W2", "b2")

        with nc.Block() as block:
            @block.sync
            def _(sp):
                sp.dma_start(w_route[:, :, :], ins[pre + ("Wr" if gated else "Wg")].rearrange("(c p) n -> p c n", p=P)
                             ).then_inc(route_loaded, 16)
                sp.dma_start(b_route[:, :], ins[pre + ("br" if gated else "bg")].partition_broadcast(P)).then_inc(route_loaded, 16)
                if not gated:
                    sp.dma_start(gamma[:, :], ins[pre + "gamma"].partition_broadcast(P)).then_inc(small_loaded, 16)
                    sp.dma_start(beta[:, :], ins[pre + "beta"].partition_broadcast(P)).then_inc(small_loaded, 16)
                sp.wait_ge(rows_known, 1)

                def load_in(s, par):
                    one = bass.ds(sp.value_load(expert[0:1, bass.ds(s, 1)], min_val=0, max_val=E - 1), 1)
                    for n, t in zip(ff_names, win):
                        sp.dma_start(t[:, par, :, :], ins[pre + n][one, :, :].rearrange("e (c p) h -> p (e c) h", p=P)
                                     ).then_inc(in_loaded[par], 16)
                    for n, t in zip(fb_names, bin_):
                        sp.dma_start(t[:, par, :], ins[pre + n][one, :, :].rearrange("e p n -> p (e n)")
                                     ).then_inc(in_loaded[par], 16)

                def load_out(s, par):
                    one = bass.ds(sp.value_load(expert[0:1, bass.ds(s, 1)], min_val=0, max_val=E - 1), 1)
                    sp.dma_start(wout[:, par, :, :], ins[pre + out_w][one, :, :].rearrange("e (c p) d -> p (e c) d", p=P)
                                 ).then_inc(out_loaded[par], 16)
                    for n, t in [(out_b, bout)] + ([("gamma", g_e), ("beta", b_e)] if gated else []):
                        sp.dma_start(t[:, par, :], ins[pre + n][one, :].rearrange("e d -> (e d)").partition_broadcast(P)
                                     ).then_inc(out_loaded[par], 16)

                def load_rows(s, par):
                    sp.dma_start(rows[:, par, :, :], k.sorted_x.ap()[bass.ds(s * SLOT, SLOT), :]
                                 .rearrange("(t p) d -> p t d", p=P)).then_inc(rows_loaded[par], 16)

                def load_ahead(s, par):
                    sp.wait_ge(h_ready, HC_N * s + HC_N)
                    own_wait(sp, k)
                    if gated:
                        sp.wait_ge(rbias_ready, s + 1)
                        own_wait(sp, k)
                    load_rows(s + 2, par)
                    load_in(s + 2, par)

                def store(s, par):
                    sp.wait_ge(y_ready, s + 1)
                    sp.dma_start(k.sorted_y.ap()[bass.ds(s * SLOT, SLOT), :].rearrange("(t p) d -> p t d", p=P),
                                 y[:, par, :, :]).then_inc(y_stored[par], 16)
                load_in(0, 0)
                load_out(0, 0)
                load_in(1, 1)
                sp.wait_ge(scattered, 16 * 2 * NT)
                for par in range(2):
                    load_rows(par, par)
                load_out(1, 1)
                with sp.Fori(0, SLOTS // 2 - 1) as pair:
                    for par in range(2):
                        load_ahead(pair * 2 + par, par)
                        store(pair * 2 + par, par)
                        load_out(pair * 2 + par + 2, par)
                load_ahead(SLOTS - 3, 0)
                store(SLOTS - 3, 0)
                load_out(SLOTS - 1, 0)
                store(SLOTS - 2, 1)
                store(SLOTS - 1, 0)
                for par in range(2):
                    sp.wait_ge(y_stored[par], 16 * ((SLOTS + 1 - par) // 2))

            @block.gpsimd
            def _(pool):
                norm.gpsimd(pool)
                pool.wait_ge(k.cleared, 16)
                pool.wait_ge(rows_known, 1)
                for t in range(NT):
                    for way in range(2):
                        pool.indirect_dma_start(out=k.sorted_x.ap(), in_=k.z[:, t, :], in_offset=None,
                                                out_offset=bass.IndirectOffsetOnAxis(ap=row[:, way, t:t + 1], axis=0)
                                                ).then_inc(scattered, 16)
                if gated:
                    def prepare(s, pair, par):
                        pool.wait_ge(in_loaded[par], 16 * PER_IN * (pair + 1))
                        if seen(s, 2):
                            pool.wait_ge(y_ready, s - 1)
                        own_wait(pool, k)
                        nc.gpsimd.tensor_scalar(halfb[:, par, :], bin_[1][:, par, :], 0.5, None, ALU.mult
                                                ).then_inc(halfb_ready, 1)
                        pool.wait_ge(rows_loaded[par], 16 * (pair + 1))
                        pool.wait_ge(out_loaded[par], 16 * PER_OUT * (pair + 1))
                        own_wait(pool, k)
                        nc.gpsimd.tensor_tensor(rbias[:, par, :, :], rows[:, par, :, :],
                                                bout[:, par, :].unsqueeze(1).broadcast_to([P, SLOT // P, D]), ALU.add
                                                ).then_inc(rbias_ready, 1)
                    prepare(0, 0, 0)

                    def body(s, pair, par, has_next):
                        if has_next:
                            prepare(s + 1, pair if par == 0 else pair + 1, 1 - par)
                        pool.wait_ge(rstats_ready, s + 1)
                        own_wait(pool, k)
                        nc.gpsimd.tensor_scalar(rs[:, :], mv[:, :, 1], 1e-12, None, ALU.add).then_inc(rvar_ready, 1)
                        pool.wait_ge(rvar_ready, s + 1)
                        own_wait(pool, k)
                        nc.gpsimd.tensor_tensor(rs[:, :], rs[:, :], k.const("minus_half")[:, 0:SLOT // P], ALU.pow
                                                ).then_inc(rrstd_ready, 1)
                    per_slot(pool, body)
                for par in range(2):
                    pool.wait_ge(y_stored[par], 16 * ((SLOTS + 1 - par) // 2))
                for way, dst in enumerate((mixed1, mixed2)):
                    for t in range(NT):
                        pool.indirect_dma_start(out=dst[:, t, :], out_offset=None, in_=k.sorted_y.ap(),
                                                in_offset=bass.IndirectOffsetOnAxis(ap=row[:, way, t:t + 1], axis=0)
                                                ).then_inc(gathered[way], 16)
                if not gated:
                    norm2.gpsimd(pool)

            @block.tensor
            def _(pe):
                zT.tensor(pe)
                pe.wait_ge(route_loaded, 16 * 2)
                pe.wait_ge(zT.ready, 4)
                for t in range(NT):
                    dst = ps[:, 4, t * E:(t + 1) * E]
                    for c in range(C):
                        last = nc.tensor.matmul(dst, k.zT[:, c, t * P:(t + 1) * P], w_route[:, c, :],
                                                start=c == 0, stop=c == C - 1)
                last.then_inc(logits_done, 1)
                pe.wait_ge(both_ready, 1)
                chosen = both[:, :, :].rearrange("p t e -> p (t e)")
                nc.tensor.matmul(ps[:, 5, 0:NT * E], k.const("before"), chosen, start=True, stop=True)
                nc.tensor.matmul(ps[:, 5, NT * E:2 * NT * E], k.const("ones"), chosen, start=True, stop=True
                                 ).then_inc(counted_done, 1)

                def transpose_rows(pair, par):
                    pe.wait_ge(rows_loaded[par], 16 * (pair + 1))
                    for c in range(C):
                        for t in range(SLOT // P):
                            last = nc.tensor.transpose(ps[:, XB, (c * (SLOT // P) + t) * P:(c * (SLOT // P) + t + 1) * P],
                                                       rows[:, par, t, c * P:(c + 1) * P], k.ident)
                    last.then_inc(xt_done, 1)

                pe.wait_ge(rows_known, 1)
                transpose_rows(0, 0)

                def body(s, pair, par, has_next):
                    pe.wait_ge(xt_ready, s + 1)
                    pe.wait_ge(in_loaded[par], 16 * PER_IN * (pair + 1))
                    own_wait(pe, k)
                    for n in range(HC_N):
                        if seen(s, 1) or n >= 4:
                            pe.wait_ge(h_ready, HC_N * s + n - 3)
                        for i, w in enumerate(win):
                            for c in range(C):
                                last = nc.tensor.matmul(ps[:, HB + n % 4, i * SLOT:(i + 1) * SLOT],
                                                        w[:, par, c, n * P:(n + 1) * P], xT[:, c, :],
                                                        start=c == 0, stop=c == C - 1)
                        last.then_inc(h_done, 1)
                    if has_next:
                        transpose_rows(pair if par == 0 else pair + 1, 1 - par)
                    if seen(s, 1):
                        pe.wait_ge(y_read if gated else y_ready, s)
                    pe.wait_ge(out_loaded[par], 16 * PER_OUT * (pair + 1))
                    own_wait(pe, k)
                    for n in range(HC_N):
                        pe.wait_ge(h_ready, HC_N * s + n + 1)
                        for t in range(SLOT // P):
                            last = nc.tensor.matmul(ps[:, YB, t * D:(t + 1) * D], hT[:, par, n, t * P:(t + 1) * P],
                                                    wout[:, par, n, :], start=n == 0 and t == 0, stop=n == HC_N - 1,
                                                    skip_group_check=True)
                    last.then_inc(y_done, 1)
                per_slot(pe, body)

            @block.scalar
            def _(act):
                zT.scalar(act)
                act.wait_ge(gap_ready, 1)
                nc.scalar.activation(share2[:, :], gap[:, :], ACT.Exp).then_inc(exp_ready, 1)

                def rows_out(s):
                    act.wait_ge(xt_done, s + 1)
                    nc.scalar.copy(xT[:, :, :].rearrange("p c n -> p (c n)"), ps[:, XB, :]).then_inc(xt_ready, 1)
                rows_out(0)

                def body(s, pair, par, has_next):
                    if gated:
                        act.wait_ge(halfb_ready, s + 1)
                    elif seen(s, 2):
                        act.wait_ge(y_done, s - 1)
                    for n in range(HC_N):
                        act.wait_ge(h_done, HC_N * s + n + 1)
                        if gated:
                            if seen(s, 1) or n >= 2:
                                act.wait_ge(h_ready, HC_N * s + n - 1)
                            nc.scalar.activation(gelu[:, n % 2, :], ps[:, HB + n % 4, 0:SLOT], ACT.Gelu,
                                                 bias=bin_[0][:, par, n:n + 1])
                            nc.scalar.activation(tanh[:, n % 2, :], ps[:, HB + n % 4, SLOT:2 * SLOT], ACT.Tanh,
                                                 bias=halfb[:, par, n:n + 1], scale=0.5).then_inc(act_done, 1)
                        else:
                            nc.scalar.activation(hT[:, par, n, :], ps[:, HB + n % 4, 0:SLOT], ACT.Gelu,
                                                 bias=bin_[0][:, par, n:n + 1]).then_inc(h_ready, 1)
                    if has_next:
                        rows_out(s + 1)
                per_slot(act, body)

            @block.vector
            def _(dve):
                order = Count(dve, order_sem)
                norm.vector(dve, order)
                zT.vector(dve)
                dve.wait_ge(logits_done, 1)
                order.after(nc.vector.tensor_tensor(logits[:, :, :], ps[:, 4, 0:NT * E].rearrange("p (t e) -> p t e", e=E),
                                                    b_route[:, :].unsqueeze(1).broadcast_to([P, NT, E]), ALU.add))

                def pick(src, chosen, value, winner):
                    order.after(nc.vector.tensor_reduce(best[:, value, :], src, AX.X, ALU.max))
                    order.after(nc.vector.tensor_tensor(tie[:, :, :], src, best[:, value, :].unsqueeze(2)
                                                        .broadcast_to([P, NT, E]), ALU.is_equal))
                    order.after(nc.vector.tensor_tensor(tie[:, :, :], tie[:, :, :], k.const("prefer").unsqueeze(1)
                                                        .broadcast_to([P, NT, E]), ALU.mult))
                    order.after(nc.vector.tensor_reduce(best[:, winner, :], tie[:, :, :], AX.X, ALU.max))
                    order.after(nc.vector.tensor_tensor(chosen, tie[:, :, :], best[:, winner, :].unsqueeze(2)
                                                        .broadcast_to([P, NT, E]), ALU.is_equal))
                pick(logits[:, :, :], first[:, :, :], 0, 2)
                order.after(nc.vector.scalar_tensor_tensor(out=rest[:, :, :], in0=first[:, :, :], scalar=-3.0e38,
                                                           in1=logits[:, :, :], op0=ALU.mult, op1=ALU.add))
                pick(rest[:, :, :], second[:, :, :], 1, 3)
                nc.vector.tensor_tensor(both[:, :, :], first[:, :, :], second[:, :, :], ALU.add).then_inc(both_ready, 1)
                nc.vector.tensor_tensor(gap[:, :], best[:, 1, :], best[:, 0, :], ALU.subtract).then_inc(gap_ready, 1)
                dve.wait_ge(exp_ready, 1)
                order.after(nc.vector.tensor_scalar(gap[:, :], share2[:, :], 1.0, None, ALU.add))
                order.after(nc.vector.reciprocal(share1[:, :], gap[:, :]))
                order.after(nc.vector.tensor_tensor(share2[:, :], share2[:, :], share1[:, :], ALU.mult))
                dve.wait_ge(counted_done, 1)
                order.after(nc.vector.tensor_copy(counted[:, :, :, :].rearrange("p a t e -> p (a t e)"), ps[:, 5, 0:2 * NT * E]))
                order.after(nc.vector.memset(earlier[:, 0, :], 0.0))
                for t in range(NT):
                    order.after(nc.vector.tensor_tensor(earlier[:, t + 1, :], earlier[:, t, :], counted[:, 1, t, :], ALU.add))
                order.after(nc.vector.tensor_tensor(
                    over[:, :, :], earlier[:, NT, :].unsqueeze(2).broadcast_to([P, E, SLOTS_EACH]),
                    k.const("slot_floor").unsqueeze(1).broadcast_to([P, E, SLOTS_EACH]), ALU.is_gt))
                order.after(nc.vector.tensor_reduce(slots_of[:, :], over[:, :, :], AX.X, ALU.add))
                order.after(nc.vector.memset(start_of[:, 0:1], 0.0))
                for e in range(1, E):
                    order.after(nc.vector.tensor_tensor(start_of[:, e:e + 1], start_of[:, e - 1:e], slots_of[:, e - 1:e],
                                                        ALU.add))
                order.after(nc.vector.tensor_tensor(place[:, :, :], earlier[:, 0:NT, :], counted[:, 0, :, :], ALU.add))
                order.after(nc.vector.scalar_tensor_tensor(out=place[:, :, :], in0=start_of[:, :].unsqueeze(1)
                                                           .broadcast_to([P, NT, E]), scalar=float(SLOT),
                                                           in1=place[:, :, :], op0=ALU.mult, op1=ALU.add))
                for way, chosen in enumerate((first, second)):
                    order.after(nc.vector.tensor_tensor(tie[:, :, :], chosen[:, :, :], place[:, :, :], ALU.mult))
                    order.after(nc.vector.tensor_reduce(at[:, way, :], tie[:, :, :], AX.X, ALU.add))
                order.after(nc.vector.tensor_copy(row[:, :, :], at[:, :, :]))
                order.after(nc.vector.tensor_tensor(
                    begun[:, :, :], k.const("slot").unsqueeze(2).broadcast_to([P, SLOTS, E]),
                    start_of[:, :].unsqueeze(1).broadcast_to([P, SLOTS, E]), ALU.is_ge))
                order.after(nc.vector.tensor_reduce(expert_f[:, :], begun[:, :, :], AX.X, ALU.add))
                nc.vector.tensor_scalar(expert[:, :], expert_f[:, :], -1.0, None, ALU.add).then_inc(rows_known, 1)

                def body(s, pair, par, has_next):
                    if gated:
                        if seen(s, 2):
                            dve.wait_ge(y_done, s - 1)
                        for n in range(HC_N):
                            dve.wait_ge(act_done, HC_N * s + n + 1)
                            nc.vector.scalar_tensor_tensor(out=hT[:, par, n, :], in0=tanh[:, n % 2, :], scalar=1.0,
                                                           in1=gelu[:, n % 2, :], op0=ALU.add, op1=ALU.mult
                                                           ).then_inc(h_ready, 1)
                    dve.wait_ge(y_done, s + 1)
                    if gated:
                        dve.wait_ge(rbias_ready, s + 1)
                        nc.vector.scalar_tensor_tensor(out=resid[:, :, :].rearrange("p t d -> p (t d)"), in0=ps[:, YB, :],
                                                       scalar=0.5, in1=rbias[:, par, :, :].rearrange("p t d -> p (t d)"),
                                                       op0=ALU.mult, op1=ALU.add).then_inc(y_read, 1)
                        dve.wait_ge(y_read, s + 1)
                        for t in range(SLOT // P):
                            last = nc.vector.bn_stats(st[:, t, :], resid[:, t, :])
                        order.after(last)
                        own_wait(dve, k)
                        for t in range(SLOT // P):
                            last = nc.vector.bn_aggr(mv[:, t, :], st[:, t, :])
                        last.then_inc(rstats_ready, 1)
                        dve.wait_ge(rrstd_ready, s + 1)
                        for t in range(SLOT // P):
                            last = nc.vector.tensor_scalar(resid[:, t, :], resid[:, t, :], mv[:, t, 0:1], rs[:, t:t + 1],
                                                           ALU.subtract, ALU.mult)
                        order.after(last)
                        order.after(nc.vector.tensor_tensor(resid[:, :, :], resid[:, :, :],
                                                            g_e[:, par, :].unsqueeze(1).broadcast_to([P, SLOT // P, D]),
                                                            ALU.mult))
                        if seen(s, 2):
                            dve.wait_ge(y_stored[par], 16 * pair)
                        nc.vector.tensor_tensor(y[:, par, :, :], resid[:, :, :],
                                                b_e[:, par, :].unsqueeze(1).broadcast_to([P, SLOT // P, D]),
                                                ALU.add).then_inc(y_ready, 1)
                    else:
                        if seen(s, 2):
                            dve.wait_ge(y_stored[par], 16 * pair)
                        nc.vector.tensor_tensor(y[:, par, :, :], ps[:, YB, :].rearrange("p (t d) -> p t d", d=D),
                                                bout[:, par, :].unsqueeze(1).broadcast_to([P, SLOT // P, D]),
                                                ALU.add).then_inc(y_ready, 1)
                if gated:
                    body(0, 0, 0, True)
                    body(1, 0, 1, True)
                    with dve.Fori(1, SLOTS // 2) as pair:
                        order.enter(pair - 1, 6)
                        for par in range(2):
                            body(pair * 2 + par, pair, par, True)
                        order.leave(SLOTS // 2 - 1)
                    body(SLOTS - 1, SLOTS // 2, 0, False)
                else:
                    per_slot(dve, body)
                for way, (mixed, share) in enumerate(((mixed1, share1), (mixed2, share2))):
                    base = k.x if gated else k.z
                    dve.wait_ge(gathered[way], 16 * NT)
                    for t in range(NT):
                        src = base if way == 0 else k.x if gated else mixed1
                        dst = k.x if gated else mixed1
                        last = nc.vector.scalar_tensor_tensor(out=dst[:, t, :], in0=mixed[:, t, :], scalar=share[:, t:t + 1],
                                                              in1=src[:, t, :], op0=ALU.mult, op1=ALU.add)
                    order.after(last)
                if not gated:
                    dve.wait_ge(small_loaded, 16 * 2)
                    norm2.vector(dve, order)
                    dve.wait_ge(norm2.dst_ready, NT)
                    for op, t in ((ALU.mult, gamma), (ALU.add, beta)):
                        order.after(nc.vector.tensor_tensor(mixed1[:, :, :], mixed1[:, :, :],
                                                            t[:, :].unsqueeze(1).broadcast_to([P, NT, D]), op))
                    nc.vector.tensor_tensor(k.x[:, :, :], k.x[:, :, :], mixed1[:, :, :], ALU.add)


def experts_one(nc, k):
    experts(nc, k, "e1", False)


def experts_two(nc, k):
    experts(nc, k, "e2", True)


def constants():
    import numpy as np
    table = np.zeros((P, CONST_WIDTH), np.float32)

    def put(name, value):
        a, b = CONST_COLS[name]
        table[:, a:b] = np.broadcast_to(value, (P, b - a))
    row = np.arange(P)[:, None]
    put("ident", row == np.arange(P))
    put("ones", 1.0)
    put("before", row < np.arange(P))
    put("head_of_row", row // HD == np.arange(HC))
    put("group_of_row", row // S == np.arange(HG))
    put("query", row % S == np.arange(S))
    put("minus_half", -0.5)
    put("prefer", E - np.arange(E))
    put("slot_floor", SLOT * np.arange(SLOTS_EACH))
    put("slot", np.arange(SLOTS))
    valid = np.ones((P, B, 3), np.float32)
    valid[:, :, 2] = row == np.arange(B)
    put("last_key", valid.reshape(P, -1))
    q, key = row % S, np.arange(S)
    pair, key_pair = q // 2, key // 2
    for w in range(2):
        first = pair - w
        a = CONST_COLS["window_pen"][0] + w * S
        table[:, a:a + S] = np.where((key_pair == first) | (key_pair == first + 1), 0.0, MASKED)
        on = (first >= 0) & (first + 1 < S // 2)
        table[:, CONST_COLS["window_on"][0] + w] = on[:, 0]
    pairs = np.arange(P) % S // 2
    put("window_count", np.where((pairs == 0) | (pairs == S // 2 - 1), 1.0, 2.0))
    put("causal_pen", np.where(key <= q, 0.0, MASKED))
    theta = np.repeat((np.float32(10000.0) ** (-np.arange(0, D, 2, dtype=np.float32) / np.float32(D))), 2)
    angle = (np.arange(S, dtype=np.float32)[:, None] * theta[None, :])[np.arange(P) % S]
    put("cos", np.cos(angle))
    put("sin", np.sin(angle) * np.where(np.arange(D) % 2 == 0, -1.0, 1.0))
    return table


_DIRECT = ["x", "L0_xattn_Wq", "L0_xattn_Wk", "L0_xattn_Wv", "L0_xattn_Wo", "L0_xattn_bo",
           "L0_attn_w_qkv", "L0_attn_w_out", "L0_attn_b_out", "L1_attn_bo"] + [
    "L0_ffn_" + n for n in ("Wg", "bg", "W1", "W2", "b2", "gamma", "beta")] + [
    "L1_xattn_" + n for n in ("Wq", "Wk", "Wv", "gru_bih", "gru_bhh")] + [
    "L1_ffn_" + n for n in ("Wr", "br", "Wi", "Wg", "Wo", "bo", "gamma", "beta")]
_EXPERT_COLUMNS = ["L0_ffn_b1", "L1_ffn_bi", "L1_ffn_bg"]
_TURNED = ["L1_attn_Wq", "L1_attn_Wk", "L1_attn_Wv", "L1_attn_Wo", "L1_xattn_gru_wih", "L1_xattn_gru_whh"]
_COLUMNS = ["L0_xattn_bq", "L0_xattn_bk", "L0_xattn_bv", "L1_xattn_slot_norm_w", "L1_xattn_input_norm_w"]


def kernel(**inputs):
    import numpy as _np
    import concourse.bacc as _bacc
    from concourse import mybir as _mybir
    from concourse.bass_utils import run_bass_kernel_spmd as _run

    laid_out = {name: _np.ascontiguousarray(inputs[name]) for name in _DIRECT}
    for name in _TURNED:
        laid_out[name + "T"] = _np.ascontiguousarray(_np.asarray(inputs[name]).T)
    for name in _COLUMNS:
        laid_out[name] = _np.ascontiguousarray(_np.asarray(inputs[name]).reshape(-1, P).T)
    for name in _EXPERT_COLUMNS:
        laid_out[name] = _np.ascontiguousarray(_np.transpose(_np.asarray(inputs[name]).reshape(E, -1, P), (0, 2, 1)))
    laid_out["mask"] = _np.ascontiguousarray(inputs["mask_Bx1xSxS2_if1"])
    laid_out["ctx"] = _np.ascontiguousarray(inputs["ctx_1024"])
    laid_out["ctxT"] = _np.ascontiguousarray(_np.transpose(inputs["ctx_1024"], (2, 0, 1)))
    laid_out["ctx_lastT"] = _np.ascontiguousarray(inputs["ctx_1024"][:, KEYS - 1, :].T)
    laid_out["consts"] = constants()
    nc = _bacc.Bacc("TRN2", target_bir_lowering=False, num_devices=1)
    arrays, args = {}, {}
    for name, a in laid_out.items():
        arrays[f"in_{name}_dram"] = a
        args[name] = nc.dram_tensor(f"in_{name}_dram", a.shape, _mybir.dt.from_np(a.dtype), kind="ExternalInput").ap()
    out = nc.dram_tensor("out_0_dram", (B, S, D), _mybir.dt.float32, kind="ExternalOutput").ap()
    build(nc, args, out)
    r = _run(nc, [arrays], core_ids=[0])
    return r.results[0]["out_0_dram"]
```

```python
import concourse.bass as bass
from concourse import mybir
from contextlib import ExitStack

F32 = mybir.dt.float32
I32 = mybir.dt.int32
BF16 = mybir.dt.bfloat16
ALU = mybir.AluOpType
ACT = mybir.ActivationFunctionType
AX = mybir.AxisListType

P = 128
B, S, D = 32, 32, 256
KEYS = 257
HEADS, HD = 16, 16
C = D // P
NT = B * S // P
TB = P // S
HG = P // S
E, FF = 8, 1024
SLOT = 256
SLOTS = (2 * B * S + E * (SLOT - 1)) // SLOT
SLOTS_EACH = B * S // SLOT
NG = HEADS // HG
HC = P // HD
KT2 = KEYS // P
MASKED = -1.0e30

CONST_COLS = {}
_at = 0
for _n, _w in [("ident", P), ("ones", P), ("before", P), ("head_of_row", HC), ("group_of_row", HG), ("query", P),
               ("window_pen", 2 * S), ("window_on", 2), ("causal_pen", S), ("cos", D), ("sin", D), ("minus_half", 16),
               ("prefer", 8), ("slot_floor", 4), ("slot", 15), ("window_count", 1), ("last_key", 3 * B)]:
    CONST_COLS[_n] = (_at, _at + _w)
    _at += _w
CONST_WIDTH = _at


class Count:

    def __init__(self, eng, sem):
        self.eng, self.sem, self.base, self.n = eng, sem, 0, 0

    def after(self, ins):
        self.n += 1
        ins.then_inc(self.sem, 1)
        self.eng.wait_ge(self.sem, self.base + self.n)

    def enter(self, trip, per_trip):
        self.start, self.per = self.base + self.n, per_trip
        self.base, self.n = self.start + trip * per_trip, 0

    def leave_open(self):
        assert self.n == self.per, (self.n, self.per)
        self.base, self.n = self.start, 0

    def leave(self, trips):
        assert self.n == self.per, (self.n, self.per)
        self.base, self.n = self.start + trips * self.per, 0


PARTS = 3


class Core:
    pass


def build(nc, ins, out):
    with ExitStack() as ctx:
        k = Core()
        k.nc, k.ins, k.out = nc, ins, out
        k.sem = nc.alloc_semaphore
        k.consts = ctx.enter_context(nc.sbuf_tensor("consts", [P, CONST_WIDTH], F32))
        k.x = ctx.enter_context(nc.sbuf_tensor("x", [P, NT, D], F32))
        k.z = ctx.enter_context(nc.sbuf_tensor("z", [P, NT, D], F32))
        k.zT = ctx.enter_context(nc.sbuf_tensor("zT", [P, C, NT * P], F32))
        k.stats = ctx.enter_context(nc.sbuf_tensor("stats", [P, NT, 6], F32))
        k.mean_var = ctx.enter_context(nc.sbuf_tensor("mean_var", [P, NT, 2], F32))
        k.rstd = ctx.enter_context(nc.sbuf_tensor("rstd", [P, NT], F32))
        k.attention = [ctx.enter_context(nc.sbuf_tensor("attention_" + n, [P, C, D], F32)) for n in ("wq", "wk", "wv", "wo")]
        k.attention_bias = ctx.enter_context(nc.sbuf_tensor("attention_bias", [P, D], F32))
        k.slot_weights = [ctx.enter_context(nc.sbuf_tensor("slot_" + n, [P, C, w], F32))
                          for n, w in (("wq", D), ("wk", D), ("wv", D), ("wihT", 3 * D), ("whhT", 3 * D))]
        k.slot_scales = [ctx.enter_context(nc.sbuf_tensor("slot_" + n, [P, C], F32)) for n in ("w_slot", "w_in")]
        k.wqk = ctx.enter_context(nc.sbuf_tensor("slot_wqk", [P, C, D], F32))
        k.wvi = ctx.enter_context(nc.sbuf_tensor("slot_wvi", [P, C, 3 * D], F32))
        k.bias_parts = ctx.enter_context(nc.sbuf_tensor("slot_bias_parts", [PARTS, 4 * D], BF16))
        k.ones_parts = ctx.enter_context(nc.sbuf_tensor("slot_ones_parts", [PARTS, P], BF16))
        k.route = {n: (ctx.enter_context(nc.sbuf_tensor(n + "_w_route", [P, C, E], F32)),
                       ctx.enter_context(nc.sbuf_tensor(n + "_b_route", [P, E], F32))) for n in ("e1", "e2")}
        k.loaded = {n: k.sem(n + "_weights_ahead") for n in ("la", "ra", "sa", "e1", "e2")}
        k.ps = ctx.enter_context(nc.psum_tensor("ps", [P, 8, 512], F32))

        def const(name):
            a, b = CONST_COLS[name]
            return k.consts[:, a:b]
        k.const = const
        k.ident = const("ident")
        k.consts_loaded = k.sem("consts_loaded")
        k.passed = k.sem("passed")
        k.sorted_x = nc.dram_tensor("sorted_x", [SLOTS * SLOT, D], F32)
        k.sorted_y = nc.dram_tensor("sorted_y", [SLOTS * SLOT, D], F32)
        k.cleared = k.sem("sorted_x_cleared")
        for stage in (cross_attention, local_attention, experts_one, slot_attention, causal_attention,
                      experts_two):
            used = []

            def stage_sem(name):
                used.append(nc.alloc_semaphore(name))
                return used[-1]
            k.sem = stage_sem
            stage(nc, k)
            nc.clear_and_free_semaphores(used)
            nc.all_engine_barrier()


def load_attention(k, sp, name):
    if name == "la":
        w, bias = k.ins["L0_attn_w_qkv"], k.ins["L0_attn_b_out"]
        sources = [w[:, 0:D], w[:, D:2 * D], w[:, 2 * D:3 * D], k.ins["L0_attn_w_out"]]
    else:
        sources, bias = [k.ins["L1_attn_" + n] for n in ("WqT", "WkT", "WvT", "WoT")], k.ins["L1_attn_bo"]
    for t, src in zip(k.attention, sources):
        sp.dma_start(t[:, :, :], src.rearrange("(c p) n -> p c n", p=P)).then_inc(k.loaded[name], 16)
    sp.dma_start(k.attention_bias[:, :], bias.partition_broadcast(P)).then_inc(k.loaded[name], 16)


def load_slot_weights(k, sp):
    for t, n in zip(k.slot_weights, ("Wq", "Wk", "Wv", "gru_wihT", "gru_whhT")):
        sp.dma_start(t[:, :, :], k.ins["L1_xattn_" + n].rearrange("(c p) n -> p c n", p=P)).then_inc(k.loaded["sa"], 16)
    for t, n in zip(k.slot_scales, ("slot_norm_w", "input_norm_w")):
        sp.dma_start(t[:, :], k.ins["L1_xattn_" + n]).then_inc(k.loaded["sa"], 16)


def load_route(k, sp, name):
    w, bias = ("L0_ffn_Wg", "L0_ffn_bg") if name == "e1" else ("L1_ffn_Wr", "L1_ffn_br")
    sp.dma_start(k.route[name][0][:, :, :], k.ins[w].rearrange("(c p) n -> p c n", p=P)).then_inc(k.loaded[name], 16)
    sp.dma_start(k.route[name][1][:, :], k.ins[bias].partition_broadcast(P)).then_inc(k.loaded[name], 16)


class Fold:

    def __init__(self, nc, k, sb):
        self.nc, self.k = nc, k
        self.done, self.ready, self.loaded = k.sem("fold_done"), k.sem("fold_ready"), k.sem("fold_biases_loaded")
        self.bih, self.bhh = sb("bih", [PARTS, 3 * D]), sb("bhh", [PARTS, 3 * D])
        self.bias, self.parts = sb("bias", [PARTS, 4 * D]), sb("bias_sum", [PARTS, 4 * D])
        self.high = sb("bias_high", [PARTS, 4 * D], BF16)

    def tensor(self, pe, banks):
        nc, ps = self.nc, self.k.ps
        wq, wk, wv, wihT, _ = self.k.slot_weights
        pe.wait_ge(self.k.loaded["sa"], 16 * 7)
        for m in range(C):
            for c in range(C):
                last = nc.tensor.matmul(ps[:, banks[m], 0:D], wq[:, c, m * P:(m + 1) * P], wk[:, c, :],
                                        start=c == 0, stop=c == C - 1)
            last.then_inc(self.done, 1)
        for m in range(C):
            for j, (lo, hi) in enumerate(((0, 2 * D), (2 * D, 3 * D))):
                for c in range(C):
                    last = nc.tensor.matmul(ps[:, banks[2 + 2 * m + j], 0:hi - lo], wv[:, c, m * P:(m + 1) * P],
                                            wihT[:, c, lo:hi], start=c == 0, stop=c == C - 1)
                last.then_inc(self.done, 1)

    def scalar(self, act, banks):
        nc, k = self.nc, self.k
        w_slot, w_in = k.slot_scales
        for m in range(C):
            act.wait_ge(self.done, m + 1)
            nc.scalar.activation(k.wqk[:, m, :], k.ps[:, banks[m], 0:D], ACT.Copy, scale=w_slot[:, m:m + 1]
                                 ).then_inc(self.ready, 1)
        for m in range(C):
            for j, (lo, hi) in enumerate(((0, 2 * D), (2 * D, 3 * D))):
                act.wait_ge(self.done, 2 + 2 * m + j + 1)
                nc.scalar.activation(k.wvi[:, m, lo:hi], k.ps[:, banks[2 + 2 * m + j], 0:hi - lo], ACT.Copy,
                                     scale=w_in[:, m:m + 1]).then_inc(self.ready, 1)

    def sync(self, sp):
        for t, n in ((self.bih, "gru_bih"), (self.bhh, "gru_bhh")):
            sp.dma_start(t[:, :], self.k.ins["L1_xattn_" + n].partition_broadcast(PARTS)).then_inc(self.loaded, 16)

    def vector(self, dve, order):
        nc, k, bih, bhh, bias, high, parts = self.nc, self.k, self.bih, self.bhh, self.bias, self.high, self.parts
        dve.wait_ge(self.loaded, 16 * 2)
        nc.vector.tensor_tensor(bias[:, 0:2 * D], bih[:, 0:2 * D], bhh[:, 0:2 * D], ALU.add)
        nc.vector.tensor_copy(bias[:, 2 * D:3 * D], bih[:, 2 * D:3 * D])
        order.after(nc.vector.tensor_copy(bias[:, 3 * D:4 * D], bhh[:, 2 * D:3 * D]))
        nc.vector.tensor_copy(k.ones_parts[:, :], k.const("ones")[0:PARTS, :])
        own = [k.ident[0:PARTS, i:i + 1] for i in range(PARTS)]
        order.after(nc.vector.tensor_copy(high[:, :], bias[:, :]))
        order.after(nc.vector.tensor_scalar(parts[:, :], high[:, :], own[0], None, ALU.mult))
        order.after(nc.vector.tensor_tensor(bias[:, :], bias[:, :], high[:, :], ALU.subtract))
        order.after(nc.vector.tensor_copy(high[:, :], bias[:, :]))
        order.after(nc.vector.scalar_tensor_tensor(out=parts[:, :], in0=high[:, :], scalar=own[1], in1=parts[:, :],
                                                   op0=ALU.mult, op1=ALU.add))
        order.after(nc.vector.tensor_tensor(bias[:, :], bias[:, :], high[:, :], ALU.subtract))
        order.after(nc.vector.scalar_tensor_tensor(out=k.bias_parts[:, :], in0=bias[:, :], scalar=own[2], in1=parts[:, :],
                                                   op0=ALU.mult, op1=ALU.add))


class Transpose:

    def __init__(self, nc, k, name, src, dst, bank0=0):
        self.nc, self.k, self.src, self.dst, self.bank0 = nc, k, src, dst, bank0
        self.src_ready = k.sem(name + "_rows_ready")
        self.done = k.sem(name + "_transposed")
        self.ready = k.sem(name + "_columns_ready")

    def tensor(self, pe):
        for half in range(2):
            for t in range(4 * half, 4 * half + 4):
                pe.wait_ge(self.src_ready, t + 1)
                for c in range(C):
                    last = self.nc.tensor.transpose(
                        self.k.ps[:, self.bank0 + 2 * c + half, (t % 4) * P:(t % 4 + 1) * P],
                        self.src[:, t, c * P:(c + 1) * P], self.k.ident)
            last.then_inc(self.done, 1)

    def vector(self, dve):
        for half in range(2):
            dve.wait_ge(self.done, half + 1)
            self.nc.vector.tensor_copy(self.dst[:, 1, half * 512:half * 512 + 512],
                                       self.k.ps[:, self.bank0 + 2 + half, :]).then_inc(self.ready, 1)

    def scalar(self, act):
        for half in range(2):
            act.wait_ge(self.done, half + 1)
            self.nc.scalar.copy(self.dst[:, 0, half * 512:half * 512 + 512],
                                self.k.ps[:, self.bank0 + half, :]).then_inc(self.ready, 1)


class Norm:

    def __init__(self, nc, k, name, eps, src, dst, dst_ready=None):
        self.nc, self.k, self.eps, self.src, self.dst = nc, k, eps, src, dst
        self.stats_ready = k.sem(name + "_stats_ready")
        self.var_ready = k.sem(name + "_var_ready")
        self.rstd_ready = k.sem(name + "_rstd_ready")
        self.dst_ready = dst_ready or k.sem(name + "_rows_ready")

    def vector(self, dve, order):
        nc, k = self.nc, self.k
        for t in range(NT):
            last = nc.vector.bn_stats(k.stats[:, t, :], self.src[:, t, :])
        order.after(last)
        for t in range(NT):
            last = nc.vector.bn_aggr(k.mean_var[:, t, :], k.stats[:, t, :])
        last.then_inc(self.stats_ready, 1)
        dve.wait_ge(self.rstd_ready, 1)
        for t in range(NT):
            nc.vector.tensor_scalar(self.dst[:, t, :], self.src[:, t, :], k.mean_var[:, t, 0:1], k.rstd[:, t:t + 1],
                                    ALU.subtract, ALU.mult).then_inc(self.dst_ready, 1)

    def gpsimd(self, pool):
        nc, k = self.nc, self.k
        pool.wait_ge(self.stats_ready, 1)
        nc.gpsimd.tensor_scalar(k.rstd[:, :], k.mean_var[:, :, 1], self.eps, None, ALU.add).then_inc(self.var_ready, 1)
        pool.wait_ge(self.var_ready, 1)
        nc.gpsimd.tensor_tensor(k.rstd[:, :], k.rstd[:, :], k.const("minus_half")[:, 0:NT],
                                ALU.pow).then_inc(self.rstd_ready, 1)


class Residual:

    def __init__(self, nc, k, name, eps=1e-5):
        self.nc, self.k, self.eps = nc, k, eps
        self.x_ready, self.stats_ready, self.mean_ready, self.var_ready, self.rstd_ready = (
            k.sem(name + "_" + n) for n in ("x_ready", "stats_ready", "mean_ready", "var_ready", "rstd_ready"))
        self.zT = Transpose(nc, k, name + "_next", k.z, k.zT)

    def stats(self, dve, t):
        dve.wait_ge(self.x_ready, t + 1)
        self.nc.vector.bn_stats(self.k.stats[:, t, :], self.k.x[:, t, :]).then_inc(self.stats_ready, 1)

    def mean(self, dve, t):
        dve.wait_ge(self.stats_ready, t + 1)
        self.nc.vector.bn_aggr(self.k.mean_var[:, t, :], self.k.stats[:, t, :]).then_inc(self.mean_ready, 1)

    def normalise(self, dve, t):
        dve.wait_ge(self.rstd_ready, t + 1)
        self.nc.vector.tensor_scalar(self.k.z[:, t, :], self.k.x[:, t, :], self.k.mean_var[:, t, 0:1],
                                     self.k.rstd[:, t:t + 1], ALU.subtract, ALU.mult).then_inc(self.zT.src_ready, 1)

    def vector(self, dve, add):
        for n in range(NT + 4):
            for lag, step in ((1, self.stats), (2, self.mean), (4, self.normalise)):
                if lag == 1 and n < NT:
                    add(n).then_inc(self.x_ready, 1)
                if 0 <= n - lag < NT:
                    step(dve, n - lag)
        self.zT.vector(dve)

    def rstd(self, pool, t):
        nc, k = self.nc, self.k
        pool.wait_ge(self.mean_ready, t + 1)
        nc.gpsimd.tensor_scalar(k.rstd[:, t:t + 1], k.mean_var[:, t, 1:2], self.eps, None, ALU.add
                                ).then_inc(self.var_ready, 1)
        pool.wait_ge(self.var_ready, t + 1)
        nc.gpsimd.tensor_tensor(k.rstd[:, t:t + 1], k.rstd[:, t:t + 1], k.const("minus_half")[:, 0:1],
                                ALU.pow).then_inc(self.rstd_ready, 1)

    def gpsimd(self, pool):
        for t in range(NT):
            self.rstd(pool, t)

    def tensor(self, pe):
        self.zT.tensor(pe)

    def scalar(self, act):
        self.zT.scalar(act)


def seen(b, lag):
    return not isinstance(b, int) or b >= lag


def own_wait(eng, k):
    eng.sem_inc(k.passed, 1)


def exists(n, count):
    return not isinstance(n, int) or n < count


def per_batch(eng, body):
    body(0, 0, 0)
    body(1, 0, 1)
    with eng.Fori(1, B // 2 - 1) as pair:
        for par in range(2):
            body(pair * 2 + par, pair, par)
    body(B - 2, B // 2 - 1, 0)
    body(B - 1, B // 2 - 1, 1)


def cross_attention(nc, k):
    ins, ps = k.ins, k.ps
    with ExitStack() as ctx:
        def sb(name, shape, dt=F32):
            return ctx.enter_context(nc.sbuf_tensor("ca_" + name, shape, dt))

        def sem(name):
            return k.sem("ca_" + name)

        wq, wk, wv, wo = (sb(n, [P, C, D]) for n in ("wq", "wk", "wv", "wo"))
        bq, bk, bv = (sb(n, [P, C]) for n in ("bq", "bk", "bv"))
        bo = sb("bo", [P, D])
        lastT = sb("lastT", [P, C, B])
        lastV = sb("lastV", [B, D])
        lastV_by_group = sb("lastV_by_group", [NG, B, D])
        zero = sb("zero", [P, D])
        QT = sb("QT", [P, C, B * S])
        attnT = sb("attnT", [P, C, B * S])
        ctxT = sb("ctxT", [P, 2, C, KEYS])
        mask = sb("mask", [P, 2, KEYS], I32)
        hide = sb("hide", [P, 2, KEYS])
        Qblk = sb("Qblk", [P, C, HC, S])
        KT = sb("KT", [P, C, KEYS])
        V = sb("V", [P, 2, KT2, D])
        masked = sb("masked", [P, NG, KEYS])
        top = sb("top", [P, NG])
        nbias = sb("nbias", [P, NG])
        probs = sb("probs", [P, NG, KEYS])
        rowsum = sb("rowsum", [P, 2, NG])
        rinv = sb("rinv", [P, NG])
        PT = sb("PT", [P, NG, KT2, P])
        PTlast = sb("PTlast", [NG, P])
        pick = sb("pick", [P, NG, S])
        blocked = sb("blocked", [P, NG, HG * HD])

        consts_loaded = k.consts_loaded
        x_loaded, weights_loaded = sem("x_loaded"), sem("weights_loaded")
        ctxT_loaded = [sem("ctxT_loaded0"), sem("ctxT_loaded1")]
        mask_loaded = [sem("mask_loaded0"), sem("mask_loaded1")]
        zT = Transpose(nc, k, "ca_z", k.z, k.zT)
        norm = Norm(nc, k, "ca_norm", 1e-5, k.x, k.z, zT.src_ready)
        residual = Residual(nc, k, "ca")
        q_done, qt_ready = sem("q_done"), sem("qt_ready")
        lastv_done, lastv_ready, zeroed, lastv_placed = (
            sem(n) for n in ("lastv_done", "lastv_ready", "zeroed", "lastv_placed"))
        qblk_ready, keys_done, values_done, scores_done = (
            sem(n) for n in ("qblk_ready", "keys_done", "values_done", "scores_done"))
        kt_ready, v_ready, hide_ready, masked_ready = (
            sem(n) for n in ("kt_ready", "v_ready", "hide_ready", "masked_ready"))
        nbias_ready, probs_ready, pt_done = sem("nbias_ready"), sem("probs_ready"), sem("pt_done")
        pt_ready, ptlast_ready, av_done, blocked_ready, attn_done, attn_ready = (
            sem(n) for n in ("pt_ready", "ptlast_ready", "av_done", "blocked_ready", "attn_done", "attn_ready"))
        pick_ready, rinv_ready = sem("pick_ready"), sem("rinv_ready")
        attn_biased, proj_done, order_sem = sem("attn_biased"), sem("proj_done"), sem("vector_order")

        BK, BV, BS, BP, BM = 0, 2, 3, 5, 7
        AV = ps[:, BM, 0:D]
        BESIDE = -(-KEYS // S) * S
        PTL = ps[0:NG, BK, BESIDE:BESIDE + P]
        OT = ps[:, BS + 1, BESIDE:BESIDE + C * S]
        NWEIGHTS = 8 + C

        with nc.Block() as block:
            @block.sync
            def _(sp):
                sp.dma_start(k.x[:, :, :], ins["x"].rearrange("b s d -> (b s) d").rearrange("(t p) d -> p t d", p=P)
                             ).then_inc(x_loaded, 16)
                sp.dma_start(k.consts[:, :], ins["consts"]).then_inc(consts_loaded, 16)
                for t, n in ((wq, "Wq"), (wk, "Wk"), (wv, "Wv"), (wo, "Wo")):
                    sp.dma_start(t[:, :, :], ins["L0_xattn_" + n].rearrange("(c p) n -> p c n", p=P)
                                 ).then_inc(weights_loaded, 16)
                for t, n in ((bq, "bq"), (bk, "bk"), (bv, "bv")):
                    sp.dma_start(t[:, :], ins["L0_xattn_" + n]).then_inc(weights_loaded, 16)
                sp.dma_start(bo[:, :], ins["L0_xattn_bo"].partition_broadcast(P)).then_inc(weights_loaded, 16)
                for c in range(C):
                    sp.dma_start(lastT[:, c, :], ins["ctx_lastT"][c * P:(c + 1) * P, :]).then_inc(weights_loaded, 16)

                def load(b, par):
                    sp.dma_start(ctxT[:, par, :, :],
                                 ins["ctxT"][:, bass.ds(b, 1), :].rearrange("(c p) b n -> p (c b) n", p=P)
                                 ).then_inc(ctxT_loaded[par], 16)
                    for h in range(HG):
                        sp.dma_start(mask[h * S:(h + 1) * S, par, :],
                                     ins["mask"][bass.ds(b, 1), 0].rearrange("b q n -> (b q) n")
                                     ).then_inc(mask_loaded[par], 16)
                load(0, 0)
                load(1, 1)
                sp.wait_ge(zeroed, 2)
                sp.wait_ge(lastv_ready, 1)
                for g in range(NG):
                    sp.dma_start(lastV_by_group[g:g + 1, :, g * HG * HD:(g + 1) * HG * HD],
                                 lastV[:, g * HG * HD:(g + 1) * HG * HD]).then_inc(lastv_placed, 16)
                load_attention(k, sp, "la")
                load_route(k, sp, "e1")
                sp.dma_start(k.sorted_x.ap().rearrange("(n p) d -> p n d", p=P),
                             zero[:, :].unsqueeze(1).broadcast_to([P, 2 * SLOTS, D])).then_inc(k.cleared, 16)
                with sp.Fori(0, B // 2 - 1) as pair:
                    for par in range(2):
                        sp.wait_ge(values_done, pair * 2 + par + 1)
                        sp.wait_ge(hide_ready, pair * 2 + par + 1)
                        load(pair * 2 + par + 2, par)

            @block.gpsimd
            def _(pool):
                nc.gpsimd.memset(zero[:, :], 0.0).then_inc(zeroed, 1)
                nc.gpsimd.memset(lastV_by_group[:, :, :], 0.0).then_inc(zeroed, 1)
                pool.wait_ge(consts_loaded, 16)
                norm.gpsimd(pool)

                def body(b, pair, par):
                    pool.wait_ge(mask_loaded[par], 16 * HG * (pair + 1))
                    if seen(b, 2):
                        pool.wait_ge(masked_ready, NG * (b - 1))
                    own_wait(pool, k)
                    nc.gpsimd.tensor_scalar(hide[:, par, :], mask[:, par, :], 0.0, MASKED,
                                            ALU.is_equal, ALU.mult).then_inc(hide_ready, 1)
                per_batch(pool, body)
                residual.gpsimd(pool)

            @block.tensor
            def _(pe):
                pe.wait_ge(consts_loaded, 16)
                zT.tensor(pe)
                pe.wait_ge(weights_loaded, 16 * NWEIGHTS)

                for c in range(C):
                    last = nc.tensor.matmul(ps[0:B, BM, 0:D], lastT[:, c, :], wv[:, c, :], start=c == 0, stop=c == C - 1)
                last.then_inc(lastv_done, 1)
                pe.wait_ge(zT.ready, 4)
                for m in range(C):
                    for half in range(2):
                        bank = 2 * m + half
                        for c in range(C):
                            last = nc.tensor.matmul(ps[:, bank, :], wq[:, c, m * P:(m + 1) * P],
                                                    k.zT[:, c, half * 512:(half + 1) * 512], start=c == 0, stop=c == C - 1)
                        last.then_inc(q_done, 1)

                def keys(b, pair, par):
                    pe.wait_ge(ctxT_loaded[par], 16 * (pair + 1))
                    if seen(b, 1):
                        pe.wait_ge(kt_ready, C * b)
                    for m in range(C):
                        for c in range(C):
                            last = nc.tensor.matmul(ps[:, BK + m, 0:KEYS], wk[:, c, m * P:(m + 1) * P], ctxT[:, par, c, :],
                                                    start=c == 0, stop=c == C - 1)
                        last.then_inc(keys_done, 1)

                def values(b, par):
                    if seen(b, 1):
                        pe.wait_ge(v_ready, b)
                    for t in range(KT2):
                        for c in range(C):
                            last = nc.tensor.matmul(ps[:, BV, t * D:(t + 1) * D], ctxT[:, par, c, t * P:(t + 1) * P],
                                                    wv[:, c, :], start=c == 0, stop=c == C - 1)
                    last.then_inc(values_done, 1)

                def scores(b, groups):
                    pe.wait_ge(qblk_ready, b + 1)
                    pe.wait_ge(kt_ready, C * b + C)
                    for g in groups:
                        c, j = g // 2, g % 2
                        if g == 1 and seen(b, 2):
                            pe.wait_ge(attn_ready, b - 1)
                        if g >= 2 or seen(b, 1):
                            pe.wait_ge(masked_ready, NG * b + g - 1)
                        nc.tensor.matmul(ps[:, BS + g % 2, 0:KEYS],
                                         Qblk[:, c, j * HG:(j + 1) * HG, :].rearrange("p h q -> p (h q)"),
                                         KT[:, c, :], start=True, stop=True).then_inc(scores_done, 1)

                pe.wait_ge(qt_ready, 4)
                pe.wait_ge(lastv_ready, 1)
                pe.wait_ge(lastv_placed, 16 * NG)
                keys(0, 0, 0)
                values(0, 0)
                scores(0, range(NG))
                keys(1, 0, 1)
                values(1, 1)

                def body(b, pair, par):
                    pe.wait_ge(probs_ready, NG * b + NG)
                    if seen(b, 1):
                        pe.wait_ge(pt_ready, 2 * b)
                        pe.wait_ge(ptlast_ready, b)
                    if exists(b + 1, B):
                        pe.wait_ge(kt_ready, C * b + 2 * C)
                    for g in range(NG):
                        for t in range(KT2):
                            nc.tensor.transpose(ps[:, BP + g // 2, ((g % 2) * KT2 + t) * P:((g % 2) * KT2 + t + 1) * P],
                                                probs[:, g, t * P:(t + 1) * P], k.ident)
                    nc.tensor.transpose(PTL, probs[:, :, KEYS - 1], k.ident).then_inc(pt_done, 1)
                    if exists(b + 1, B):
                        scores(b + 1, range(NG // 2))
                    pe.wait_ge(ptlast_ready, b + 1)
                    own_wait(pe, k)
                    nc.tensor.matmul(AV, PTlast[:, :], lastV_by_group[:, bass.ds(b, 1), :].rearrange("g b d -> g (b d)"),
                                     start=True, stop=False, skip_group_check=True)
                    if exists(b + 1, B):
                        scores(b + 1, range(NG // 2, NG))
                    pe.wait_ge(pt_ready, 2 * b + 2)
                    pe.wait_ge(v_ready, b + 1)
                    for g in range(NG):
                        for t in range(KT2):
                            last = nc.tensor.matmul(ps[:, BM, g * HG * HD:(g + 1) * HG * HD], PT[:, g, t, :],
                                                    V[:, par, t, g * HG * HD:(g + 1) * HG * HD],
                                                    start=False, stop=g == NG - 1 and t == KT2 - 1, skip_group_check=True)
                    last.then_inc(av_done, 1)
                    if exists(b + 2, B):
                        keys(b + 2, pair + 1, par)
                    gather_heads(b)
                    if exists(b + 2, B):
                        values(b + 2, par)

                def gather_heads(b):
                    pe.wait_ge(blocked_ready, b + 1)
                    if seen(b, 1):
                        pe.wait_ge(attn_ready, b)
                    if exists(b + 1, B):
                        pe.wait_ge(masked_ready, NG * b + 2 * NG)
                    for g in range(NG):
                        last = nc.tensor.matmul(OT[(g % 2) * 64:(g % 2) * 64 + 64, (g // 2) * S:(g // 2 + 1) * S],
                                                blocked[:, g, :], pick[:, g, :], start=True, stop=True)
                    last.then_inc(attn_done, 1)

                per_batch(pe, body)
                pe.wait_ge(attn_ready, B)

                pe.wait_ge(attn_biased, 1)
                for t in range(NT):
                    for c in range(C):
                        last = nc.tensor.matmul(ps[:, t, 0:D], attnT[:, c, t * P:(t + 1) * P], wo[:, c, :],
                                                start=c == 0, stop=c == C - 1)
                    last.then_inc(proj_done, 1)
                residual.tensor(pe)

            @block.scalar
            def _(act):
                zT.scalar(act)
                act.wait_ge(weights_loaded, 16 * NWEIGHTS)
                act.wait_ge(lastv_done, 1)
                nc.scalar.copy(lastV[:, :], ps[0:B, BM, 0:D]).then_inc(lastv_ready, 1)
                for m in range(C):
                    for half in range(2):
                        act.wait_ge(q_done, 2 * m + half + 1)
                        nc.scalar.activation(QT[:, m, half * 512:(half + 1) * 512], ps[:, 2 * m + half, :], ACT.Identity,
                                             bias=bq[:, m:m + 1]).then_inc(qt_ready, 1)

                def keys_out(b):
                    if seen(b, 1):
                        act.wait_ge(scores_done, NG * b)
                    for m in range(C):
                        act.wait_ge(keys_done, C * b + m + 1)
                        nc.scalar.activation(KT[:, m, :], ps[:, BK + m, 0:KEYS], ACT.Identity,
                                             bias=bk[:, m:m + 1]).then_inc(kt_ready, 1)

                def values_out(b, par):
                    act.wait_ge(values_done, b + 1)
                    if seen(b, 2):
                        act.wait_ge(av_done, b - 1)
                    nc.scalar.copy(V[:, par, :, :].rearrange("p t d -> p (t d)"), ps[:, BV, :]).then_inc(v_ready, 1)

                def exponentials(b, par):
                    act.wait_ge(nbias_ready, b + 1)
                    if seen(b, 2):
                        act.wait_ge(pick_ready, b - 1)
                    for g in range(NG):
                        nc.scalar.activation(probs[:, g, :], masked[:, g, :], ACT.Exp, bias=nbias[:, g:g + 1],
                                             scale=float(HD) ** -0.5, accum_out=rowsum[:, par, g:g + 1]).then_inc(probs_ready, 1)

                keys_out(0)
                values_out(0, 0)
                exponentials(0, 0)
                keys_out(1)
                values_out(1, 1)

                def body(b, pair, par):
                    act.wait_ge(pt_done, b + 1)
                    if seen(b, 1):
                        act.wait_ge(av_done, b)
                    for half in range(2):
                        nc.scalar.copy(PT[:, 2 * half:2 * half + 2, :, :].rearrange("p g t q -> p (g t q)"),
                                       ps[:, BP + half, :]).then_inc(pt_ready, 1)
                    if exists(b + 1, B):
                        exponentials(b + 1, 1 - par)
                    if exists(b + 2, B):
                        keys_out(b + 2)
                        values_out(b + 2, par)
                per_batch(act, body)
                residual.scalar(act)

            @block.vector
            def _(dve):
                order = Count(dve, order_sem)
                dve.wait_ge(x_loaded, 16)
                norm.vector(dve, order)
                zT.vector(dve)
                dve.wait_ge(weights_loaded, 16 * NWEIGHTS)
                nc.vector.tensor_tensor(k.x[:, :, :], k.x[:, :, :], bo[:, :].unsqueeze(1).broadcast_to([P, NT, D]), ALU.add)
                dve.wait_ge(qt_ready, 4)

                def block_queries(b):
                    if seen(b, 1):
                        dve.wait_ge(scores_done, NG * b)
                    nc.vector.tensor_tensor(
                        Qblk[:, :, :, :],
                        QT[:, :, bass.ds(b * S, S)].unsqueeze(2).broadcast_to([P, C, HC, S]),
                        k.const("head_of_row").unsqueeze(1).unsqueeze(3).broadcast_to([P, C, HC, S]),
                        ALU.mult).then_inc(qblk_ready, 1)

                def attention_out(b):
                    dve.wait_ge(attn_done, b + 1)
                    nc.vector.tensor_copy(attnT[:, :, bass.ds(b * S, S)],
                                          OT.rearrange("p (c q) -> p c q", c=C)).then_inc(attn_ready, 1)

                def mask_scores(b, par):
                    dve.wait_ge(hide_ready, b + 1)
                    if seen(b, 1):
                        dve.wait_ge(probs_ready, NG * b)
                    for g in range(NG):
                        dve.wait_ge(scores_done, NG * b + g + 1)
                        own_wait(dve, k)
                        nc.vector.tensor_tensor_reduce(out=masked[:, g, :], in0=ps[:, BS + g % 2, 0:KEYS], in1=hide[:, par, :],
                                                       scale=1.0, scalar=-3.0e38, op0=ALU.add, op1=ALU.max,
                                                       accum_out=top[:, g:g + 1]).then_inc(masked_ready, 1)
                    dve.wait_ge(masked_ready, NG * b + NG)
                    nc.vector.tensor_scalar(nbias[:, :], top[:, :], -float(HD) ** -0.5, None, ALU.mult).then_inc(nbias_ready, 1)

                block_queries(0)
                mask_scores(0, 0)
                block_queries(1)

                def body(b, pair, par):
                    dve.wait_ge(pt_done, b + 1)
                    if seen(b, 1):
                        dve.wait_ge(av_done, b)
                    nc.vector.tensor_copy(PTlast[:, :], PTL).then_inc(ptlast_ready, 1)
                    if exists(b + 1, B):
                        mask_scores(b + 1, 1 - par)
                    nc.vector.reciprocal(rinv[:, :], rowsum[:, par, :]).then_inc(rinv_ready, 1)
                    dve.wait_ge(rinv_ready, b + 1)
                    if seen(b, 1):
                        dve.wait_ge(attn_done, b)
                    own_wait(dve, k)
                    nc.vector.tensor_tensor(pick[:, :, :], k.const("query")[:, 0:S].unsqueeze(1).broadcast_to([P, NG, S]),
                                            rinv[:, :].unsqueeze(2).broadcast_to([P, NG, S]), ALU.mult).then_inc(pick_ready, 1)
                    dve.wait_ge(av_done, b + 1)
                    nc.vector.tensor_tensor(
                        blocked[:, :, :].rearrange("p g (h d) -> p g h d", h=HG),
                        AV.rearrange("p (g h d) -> p g h d", g=NG, h=HG),
                        k.const("group_of_row").unsqueeze(1).unsqueeze(3).broadcast_to([P, NG, HG, HD]),
                        ALU.mult).then_inc(blocked_ready, 1)
                    if exists(b + 2, B):
                        block_queries(b + 2)
                    attention_out(b)
                per_batch(dve, body)
                dve.wait_ge(attn_ready, B)
                for c in range(C):
                    last = nc.vector.tensor_scalar(attnT[:, c, :], attnT[:, c, :], bv[:, c:c + 1], None, ALU.add)
                last.then_inc(attn_biased, 1)
                residual.vector(dve, add_projection(nc, k, dve, proj_done))


def add_projection(nc, k, dve, proj_done):
    def add(t):
        dve.wait_ge(proj_done, t + 1)
        return nc.vector.tensor_tensor(k.x[:, t, :], k.ps[:, t, 0:D], k.x[:, t, :], ALU.add)
    return add


def self_attention(nc, k, name, scale, windows, rope, bias_weight):
    ins, ps = k.ins, k.ps
    W = len(windows)
    with ExitStack() as ctx:
        def sb(n, shape, dt=F32):
            return ctx.enter_context(nc.sbuf_tensor(name + "_" + n, shape, dt))

        def sem(n):
            return k.sem(name + "_" + n)

        wq, wk, wv, wo = k.attention
        bo, weights_loaded = k.attention_bias, k.loaded[name]
        QT, attnT = (sb(n, [P, C, B * S]) for n in ("QT", "attnT"))
        KT = sb("KT", [P, C, B * S + P - S])
        V = sb("V", [P, NT, D])
        Qblk = sb("Qblk", [P, 2, C, TB, HC, S])
        Vblk = sb("Vblk", [P, NG, TB, HG * HD])
        shifted = sb("shifted", [P, W, NG * TB, S])
        top = sb("top", [P, W * NG * TB])
        weight = sb("weight", [P, W, NG * TB, S])
        rowsum = sb("rowsum", [P, W * NG * TB])
        rinv = sb("rinv", [P, W, NG * TB])
        probs = sb("probs", [P, NG * TB, S])
        PT = sb("PT", [P, NG, P])
        blocked = sb("blocked", [P, 2, TB, NG, HG * HD])

        residual = Residual(nc, k, name)
        if rope:
            rx, rxT = sb("rx", [P, NT, D]), sb("rxT", [P, C, B * S])
            turned = sb("turned", [P, NT, D])
            rT = Transpose(nc, k, name + "_rope", rx, rxT, bank0=4)
        else:
            rxT = k.zT
        proj_in_done, proj_in_ready = sem("proj_in_done"), sem("proj_in_ready")
        qblk_ready, vblk_ready, scores_done, shifted_ready, centred, weight_ready = (
            sem(n) for n in ("qblk_ready", "vblk_ready", "scores_done", "shifted_ready", "centred", "weight_ready"))
        probs_ready, pt_done, pt_ready, av_done, blocked_ready, attn_done, attn_ready, proj_done = (
            sem(n) for n in ("probs_ready", "pt_done", "pt_ready", "av_done", "blocked_ready", "attn_done",
                             "attn_ready", "proj_done"))
        order_sem, padded = sem("vector_order"), sem("padded")
        BS, BP, BA, BO = 0, 2, 3, 7
        GB = NG * TB

        def each_tile(eng, body, order=None, per_tile=0):
            body(0, 0)
            body(1, 1)
            with eng.Fori(1, NT // 2 - 1) as pair:
                if order:
                    order.enter(pair - 1, 2 * per_tile)
                for par in range(2):
                    body(pair * 2 + par, par)
                if order:
                    order.leave(NT // 2 - 2)
            body(NT - 2, 0)
            body(NT - 1, 1)

        with nc.Block() as block:
            @block.gpsimd
            def _(pool):
                def block_queries(t, par):
                    if seen(t, 2):
                        pool.wait_ge(scores_done, t - 1)
                        own_wait(pool, k)
                    for c in range(C):
                        last = nc.gpsimd.tensor_tensor(
                            Qblk[:, par, c, :, :, :],
                            QT[:, c, bass.ds(t * P, P)].rearrange("p (b q) -> p b q", b=TB).unsqueeze(2)
                            .broadcast_to([P, TB, HC, S]),
                            k.const("head_of_row").unsqueeze(1).unsqueeze(3).broadcast_to([P, TB, HC, S]), ALU.mult)
                    last.then_inc(qblk_ready, 1)

                nc.gpsimd.memset(KT[:, :, B * S:], 0.0).then_inc(padded, 1)
                pool.wait_ge(proj_in_ready, 4)
                block_queries(0, 0)
                block_queries(1, 1)
                pool.wait_ge(proj_in_ready, 16)

                def step(t, par):
                    if seen(t, 1):
                        pool.wait_ge(av_done, t)
                        own_wait(pool, k)
                    nc.gpsimd.tensor_tensor(
                        Vblk[:, :, :, :],
                        V[:, bass.ds(t, 1), :].rearrange("p t (g e) -> p (t g) e", g=NG).unsqueeze(2)
                        .broadcast_to([P, NG, TB, HG * HD]),
                        k.const("group_of_row").unsqueeze(1).unsqueeze(3).broadcast_to([P, NG, TB, HG * HD]),
                        ALU.mult).then_inc(vblk_ready, 1)
                    if exists(t + 2, NT):
                        block_queries(t + 2, par)
                each_tile(pool, step)
                residual.gpsimd(pool)

            @block.tensor
            def _(pe):
                if rope:
                    rT.tensor(pe)
                    pe.wait_ge(rT.ready, 4)
                pe.wait_ge(weights_loaded, 16 * 5)
                for n, w in enumerate((wq, wk)):
                    for m in range(C):
                        for half in range(2):
                            for c in range(C):
                                last = nc.tensor.matmul(ps[:, 4 * n + 2 * m + half, :], w[:, c, m * P:(m + 1) * P],
                                                        rxT[:, c, half * 512:(half + 1) * 512],
                                                        start=c == 0, stop=c == C - 1)
                            last.then_inc(proj_in_done, 1)
                for t in range(NT):
                    pe.wait_ge(proj_in_ready, t + 1)
                    for c in range(C):
                        last = nc.tensor.matmul(ps[:, t, 0:D], k.zT[:, c, t * P:(t + 1) * P], wv[:, c, :],
                                                start=c == 0, stop=c == C - 1)
                    last.then_inc(proj_in_done, 1)
                pe.wait_ge(proj_in_ready, 16)

                def scores(t, par):
                    pe.wait_ge(qblk_ready, t + 1)
                    if seen(t, 2):
                        pe.wait_ge(shifted_ready, W * (t - 1))
                    for g in range(NG):
                        for b in range(TB):
                            first = (g * TB + b) * S
                            width = min(P, NG * TB * S - first)
                            last = nc.tensor.matmul(ps[:, BS + par, first:first + width],
                                                    Qblk[:, par, g // 2, b, (g % 2) * HG:(g % 2 + 1) * HG, :]
                                                    .rearrange("p h q -> p (h q)"),
                                                    KT[:, g // 2, bass.ds(t * P + b * S, width)], start=True, stop=True)
                    last.then_inc(scores_done, 1)

                def gather_heads(t, par):
                    pe.wait_ge(blocked_ready, HG * t + HG)
                    if isinstance(t, int) and t:
                        pe.wait_ge(attn_ready, t)
                    for c in range(C):
                        for b in range(TB):
                            last = nc.tensor.matmul(ps[:, BO, (c * TB + b) * S:(c * TB + b) * S + P],
                                                    blocked[:, par, b, 2 * c:2 * c + 2, :].rearrange("p g e -> p (g e)"),
                                                    k.const("query"), start=True, stop=True)
                    last.then_inc(attn_done, 1)

                def step(t, par):
                    pe.wait_ge(probs_ready, t + 1)
                    if seen(t, 1):
                        pe.wait_ge(pt_ready, t)
                    for g in range(NG):
                        last = nc.tensor.transpose(ps[:, BP, g * P:(g + 1) * P],
                                                   probs[:, g * TB:(g + 1) * TB, :].rearrange("p b s -> p (b s)"), k.ident)
                    last.then_inc(pt_done, 1)
                    if seen(t, 2):
                        gather_heads(t - 2, par)
                    pe.wait_ge(pt_ready, t + 1)
                    pe.wait_ge(vblk_ready, t + 1)
                    if seen(t, 2):
                        pe.wait_ge(blocked_ready, HG * (t - 1))
                    for g in range(NG):
                        last = nc.tensor.matmul(ps[:, BA + 2 * par + g // 2, (g % 2) * D:(g % 2 + 1) * D], PT[:, g, :],
                                                Vblk[:, g, :, :].rearrange("p b e -> p (b e)"), start=True, stop=True)
                    last.then_inc(av_done, 1)
                    if exists(t + 2, NT):
                        scores(t + 2, par)

                pe.wait_ge(padded, 1)
                scores(0, 0)
                scores(1, 1)
                each_tile(pe, step)
                gather_heads(NT - 2, 0)
                gather_heads(NT - 1, 1)
                pe.wait_ge(attn_ready, NT)
                for t in range(NT):
                    for c in range(C):
                        last = nc.tensor.matmul(ps[:, t, 0:D], attnT[:, c, t * P:(t + 1) * P], wo[:, c, :],
                                                start=c == 0, stop=c == C - 1)
                    last.then_inc(proj_done, 1)
                residual.tensor(pe)

            @block.scalar
            def _(act):
                if rope:
                    rT.scalar(act)
                for n, dst in enumerate((QT, KT)):
                    for m in range(C):
                        for half in range(2):
                            act.wait_ge(proj_in_done, 4 * n + 2 * m + half + 1)
                            nc.scalar.copy(dst[:, m, half * 512:(half + 1) * 512],
                                           ps[:, 4 * n + 2 * m + half, :]).then_inc(proj_in_ready, 1)
                for t in range(NT):
                    act.wait_ge(proj_in_done, 8 + t + 1)
                    nc.scalar.copy(V[:, t, :], ps[:, t, 0:D]).then_inc(proj_in_ready, 1)

                def exponentials(t):
                    for w in range(W):
                        act.wait_ge(centred, W * t + w + 1)
                        nc.scalar.activation(weight[:, w, :, :], shifted[:, w, :, :], ACT.Exp, scale=scale
                                             ).then_inc(weight_ready, 1)

                def block_attention(t, par):
                    act.wait_ge(av_done, t + 1)
                    for h in range(HG):
                        nc.scalar.activation(
                            blocked[:, par, :, :, h * HD:(h + 1) * HD],
                            ps[:, BA + 2 * par:BA + 2 * par + 2, :].rearrange("p k n -> p (k n)")
                            .rearrange("p (g b h d) -> p h b g d", g=NG, b=TB, h=HG)[:, h],
                            ACT.Copy, scale=k.const("group_of_row")[:, h:h + 1]).then_inc(blocked_ready, 1)

                def attention_out(t):
                    act.wait_ge(attn_done, t + 1)
                    own_wait(act, k)
                    nc.scalar.copy(attnT[:, :, bass.ds(t * P, P)],
                                   ps[:, BO, 0:C * P].rearrange("p (c r) -> p c r", c=C)).then_inc(attn_ready, 1)

                def step(t, par):
                    act.wait_ge(pt_done, t + 1)
                    if seen(t, 1):
                        act.wait_ge(av_done, t)
                    nc.scalar.copy(PT[:, :, :].rearrange("p g r -> p (g r)"), ps[:, BP, :]).then_inc(pt_ready, 1)
                    if seen(t, 2):
                        attention_out(t - 2)
                    if exists(t + 1, NT):
                        exponentials(t + 1)
                    block_attention(t, par)
                exponentials(0)
                each_tile(act, step)
                attention_out(NT - 2)
                attention_out(NT - 1)
                residual.scalar(act)

            @block.vector
            def _(dve):
                order = Count(dve, order_sem)
                if rope:
                    cos = k.const("cos").unsqueeze(1).broadcast_to([P, NT // 4, D])
                    sin = k.const("sin").rearrange("p (i two) -> p i two", two=2)
                    zp = k.z[:, :, :].rearrange("p t (i two) -> p t i two", two=2)
                    tp = turned[:, :, :].rearrange("p t (i two) -> p t i two", two=2)
                    for quarter in range(4):
                        own = slice(quarter * NT // 4, (quarter + 1) * NT // 4)
                        for side in range(2):
                            last = nc.vector.tensor_tensor(
                                tp[:, own, :, side], zp[:, own, :, 1 - side],
                                sin[:, :, side].unsqueeze(1).broadcast_to([P, NT // 4, D // 2]), ALU.mult)
                        order.after(last)
                        order.after(nc.vector.tensor_tensor(rx[:, own, :], k.z[:, own, :], cos, ALU.mult))
                        for t in range(own.start, own.stop):
                            nc.vector.tensor_tensor(rx[:, t, :], rx[:, t, :], turned[:, t, :], ALU.add
                                                    ).then_inc(rT.src_ready, 1)
                    rT.vector(dve)
                dve.wait_ge(weights_loaded, 16 * 5)
                for t in range(NT):
                    nc.vector.scalar_tensor_tensor(out=k.x[:, t, :], in0=bo[:, :], scalar=bias_weight[:, 0:1],
                                                   in1=k.x[:, t, :], op0=ALU.mult, op1=ALU.add)

                def centre(t, par):
                    dve.wait_ge(scores_done, t + 1)
                    for w, pen in enumerate(windows):
                        nc.vector.tensor_tensor(shifted[:, w, :, :], ps[:, BS + par, :].rearrange("p (n s) -> p n s", s=S),
                                                pen.unsqueeze(1).broadcast_to([P, GB, S]), ALU.add
                                                ).then_inc(shifted_ready, 1)
                    dve.wait_ge(shifted_ready, W * t + W)
                    flat = shifted[:, :, :, :].rearrange("p w n s -> p (w n) s")
                    order.after(nc.vector.tensor_reduce(top[:, :], flat, AX.X, ALU.max))
                    for w in range(W):
                        nc.vector.tensor_tensor(shifted[:, w, :, :], shifted[:, w, :, :],
                                                top[:, w * GB:(w + 1) * GB].unsqueeze(2).broadcast_to([P, GB, S]),
                                                ALU.subtract).then_inc(centred, 1)

                def probabilities(t):
                    for w in range(W):
                        dve.wait_ge(weight_ready, W * t + w + 1)
                        last = nc.vector.tensor_reduce(rowsum[:, w * GB:(w + 1) * GB], weight[:, w, :, :], AX.X, ALU.add)
                    order.after(last)
                    order.after(nc.vector.reciprocal(rinv[:, :, :].rearrange("p w n -> p (w n)"), rowsum[:, :]))
                    if W == 2:
                        order.after(nc.vector.tensor_tensor(rinv[:, :, :], rinv[:, :, :],
                                                            k.const("window_on").unsqueeze(2).broadcast_to([P, W, GB]),
                                                            ALU.mult))
                    if seen(t, 1):
                        dve.wait_ge(pt_done, t)
                    if W == 1:
                        nc.vector.tensor_tensor(probs[:, :, :], weight[:, 0, :, :],
                                                rinv[:, 0, :].unsqueeze(2).broadcast_to([P, GB, S]), ALU.mult
                                                ).then_inc(probs_ready, 1)
                    else:
                        order.after(nc.vector.tensor_tensor(weight[:, :, :, :], weight[:, :, :, :],
                                                            rinv[:, :, :].unsqueeze(3).broadcast_to([P, W, GB, S]), ALU.mult))
                        nc.vector.tensor_tensor(probs[:, :, :], weight[:, 0, :, :], weight[:, 1, :, :], ALU.add
                                                ).then_inc(probs_ready, 1)

                def step(t, par):
                    probabilities(t)
                    if exists(t + 1, NT):
                        centre(t + 1, 1 - par)
                centre(0, 0)
                each_tile(dve, step, order, 3 if W == 1 else 5)
                residual.vector(dve, add_projection(nc, k, dve, proj_done))


def local_attention(nc, k):
    pen = k.const("window_pen").rearrange("p (w s) -> p w s", w=2)
    self_attention(nc, k, "la", float(D) ** -0.5, [pen[:, 0, :], pen[:, 1, :]], False, k.const("window_count"))


def slot_attention(nc, k):
    ins, ps = k.ins, k.ps
    with ExitStack() as ctx:
        def sb(n, shape, dt=F32):
            return ctx.enter_context(nc.sbuf_tensor("sa_" + n, shape, dt))

        def sem(n):
            return k.sem("sa_" + n)

        def pair_of(f, n, *more):
            return [f(n + str(i), *more) for i in range(2)]

        whhT, wqk, wvi = k.slot_weights[-1], k.wqk, k.wvi
        w_in = k.slot_scales[1]
        last_rows = sb("last_rows", [P, D])
        lastT = sb("lastT", [P, C, P])
        last_st, last_mv, last_ms = sb("last_st", [P, 6]), sb("last_mv", [P, 2]), sb("last_ms", [P, 1])
        rows = pair_of(sb, "rows", [P, TB * KT2, D])
        ctxT = pair_of(sb, "ctxT", [P, C, TB, KEYS])
        cst = pair_of(sb, "cst", [P, TB * KT2, 6])
        cmv = pair_of(sb, "cmv", [P, TB * KT2, 2])
        rms = pair_of(sb, "rms", [P, TB, 3])
        slots = pair_of(sb, "slots", [P, D])
        squares, total_sq, srs = pair_of(sb, "squares", [P, D]), pair_of(sb, "total_sq", [P, 1]), pair_of(sb, "srs", [P, 1])
        srs_diag = pair_of(sb, "srs_diag", [P, P])
        slotsT = pair_of(sb, "slotsT", [P, C, P])
        qT = pair_of(sb, "qT", [P, C, 2 * P - S])
        top, total, inv, invr = (pair_of(sb, n, [P, TB * 3]) for n in ("top", "total", "inv", "invr"))
        e, share = (pair_of(sb, n, [P, TB * 3, S]) for n in ("e", "share"))
        weight = pair_of(sb, "weight", [P, TB * (3 * P + S)])
        shifted = pair_of(sb, "shifted", [P, TB * 3, S])
        colinv = pair_of(sb, "colinv", [P, P])
        uT = pair_of(sb, "uT", [P, C, P])
        trz = pair_of(sb, "trz", [P, 2 * D])
        pre, cand, diff = (pair_of(sb, n, [P, D]) for n in ("pre", "cand", "diff"))
        srs_rows = pair_of(sb, "srs_rows", [P, P])

        residual = Residual(nc, k, "sa")
        zeroed, padded, blank, last_loaded = sem("zeroed"), sem("padded"), sem("blank"), sem("last_loaded")
        ctxT_loaded, rows_loaded = pair_of(sem, "ctxT_loaded"), pair_of(sem, "rows_loaded")
        srs_done, totals_done = pair_of(sem, "srs_done"), pair_of(sem, "totals_done")
        (ms_ready, mse_ready, rms_ready, slots_ready, sq_ready, srs_ready, diag_ready, turn_done, turn_ready, q_done,
         q_ready, scores_done, centred, e_ready, inv_ready, share_ready, weight_ready, u_done, uT_ready, gates_done,
         trz_ready, pre_ready, cand_ready) = (
            pair_of(sem, n) for n in (
                "ms_ready", "mse_ready", "rms_ready", "slots_ready", "sq_ready", "srs_ready", "diag_ready", "turn_done",
                "turn_ready", "q_done", "q_ready", "scores_done", "centred", "e_ready", "inv_ready", "share_ready",
                "weight_ready", "u_done", "uT_ready", "gates_done", "trz_ready", "pre_ready", "cand_ready"))
        order_sem = sem("vector_order")
        ROUNDS, PAIRS = 3, NT // 2
        BA, BB, BR, BN = 0, 1, 2, 3

        def bank(par, n):
            return ps[:, 4 * par + n, :]

        def own_weights(par):
            return (weight[par][:, :].rearrange("p (b n) -> p b n", b=TB)[:, :, 0:3 * P]
                    .rearrange("p b (t n) -> p b t n", t=3)[:, :, :, 0:S])

        def all_rounds(eng, round_, order=None, per_pair=0):
            with eng.Fori(0, PAIRS - 1) as pair:
                if order:
                    order.enter(pair, per_pair)
                for r in range(ROUNDS):
                    round_(pair, r, pair * ROUNDS + r, True)
                if order:
                    order.leave(PAIRS - 1)
            for r in range(ROUNDS):
                round_(PAIRS - 1, r, (PAIRS - 1) * ROUNDS + r, r < ROUNDS - 1)

        def complete(pair, r):
            if not isinstance(pair, int):
                return []
            return [NT - 2] if r == ROUNDS - 1 else range(r * (NT - 2) // 2, (r + 1) * (NT - 2) // 2)

        with nc.Block() as block:
            @block.sync
            def _(sp):
                sp.wait_ge(zeroed, 2)
                sp.dma_start(last_rows[0:B, :], ins["ctx"][:, KEYS - 1, :]).then_inc(last_loaded, 16)
                for c in range(C):
                    sp.dma_start(lastT[:, c, 0:B], ins["ctx_lastT"][c * P:(c + 1) * P, :]).then_inc(last_loaded, 16)

                def load_ctxT(pair, par):
                    for c in range(C):
                        sp.dma_start(ctxT[par][:, c, :, :],
                                     ins["ctxT"][c * P:(c + 1) * P, bass.ds((pair * 2 + par) * TB, TB), :]
                                     ).then_inc(ctxT_loaded[par], 16)

                def load_rows(pair, par):
                    for b in range(TB):
                        sp.dma_start(rows[par][:, b * KT2:(b + 1) * KT2, :],
                                     ins["ctx"][bass.ds((pair * 2 + par) * TB + b, 1), 0:KT2 * P, :]
                                     .rearrange("b (t p) d -> p (b t) d", p=P)).then_inc(rows_loaded[par], 16)
                for par in range(2):
                    load_ctxT(0, par)
                    load_rows(0, par)
                with sp.Fori(1, PAIRS) as pair:
                    for par in range(2):
                        sp.wait_ge(scores_done[par], pair * ROUNDS)
                        load_ctxT(pair, par)
                        sp.wait_ge(u_done[par], pair * ROUNDS)
                        load_rows(pair, par)

            @block.gpsimd
            def _(pool):
                nc.gpsimd.memset(last_rows[:, :], 0.0).then_inc(zeroed, 1)
                nc.gpsimd.memset(lastT[:, :, :], 0.0).then_inc(zeroed, 1)

                def context_rms(pair, par):
                    pool.wait_ge(ms_ready[par], pair + 1)
                    own_wait(pool, k)
                    nc.gpsimd.tensor_scalar(rms[par][:, :, :], rms[par][:, :, :], 1e-6, None, ALU.add
                                            ).then_inc(mse_ready[par], 1)
                    pool.wait_ge(mse_ready[par], pair + 1)
                    own_wait(pool, k)
                    nc.gpsimd.tensor_tensor(rms[par][:, :, :].rearrange("p b t -> p (b t)"),
                                            rms[par][:, :, :].rearrange("p b t -> p (b t)"),
                                            k.const("minus_half")[:, 0:TB * 3], ALU.pow).then_inc(rms_ready[par], 1)

                def slot_rms(n, par):
                    pool.wait_ge(sq_ready[par], n + 1)
                    own_wait(pool, k)
                    nc.gpsimd.tensor_tensor(srs[par][:, :], total_sq[par][:, :], k.const("minus_half")[:, 0:1], ALU.pow
                                            ).then_inc(srs_ready[par], 1)
                    pool.wait_ge(srs_ready[par], n + 1)
                    own_wait(pool, k)
                    nc.gpsimd.tensor_tensor(srs_diag[par][:, :], k.ident, srs[par][:, :].broadcast_to([P, P]), ALU.mult
                                            ).then_inc(diag_ready[par], 1)

                def weights(n, par):
                    pool.wait_ge(inv_ready[par], n + 1)
                    own_wait(pool, k)
                    nc.gpsimd.tensor_tensor(own_weights(par), e[par][:, :, :].rearrange("p (b t) s -> p b t s", t=3),
                                            invr[par][:, :].rearrange("p (b t) -> p b t", t=3).unsqueeze(3)
                                            .broadcast_to([P, TB, 3, S]), ALU.mult).then_inc(weight_ready[par], 1)
                slot_rms(0, 0)
                for par in range(2):
                    nc.gpsimd.memset(qT[par][:, :, P:], 0.0).then_inc(padded, 1)
                for par in range(2):
                    nc.gpsimd.memset(weight[par][:, :], 0.0).then_inc(blank, 1)
                pool.wait_ge(blank, 2)
                context_rms(0, 0)
                weights(0, 0)

                def round_(pair, r, n, follows):
                    slot_rms(n, 1)
                    if r == 0:
                        context_rms(pair, 1)
                    if follows:
                        slot_rms(n + 1, 0)
                    weights(n, 1)
                    for t in complete(pair, r):
                        residual.rstd(pool, t)
                    if follows:
                        if r == ROUNDS - 1:
                            context_rms(pair + 1, 0)
                        weights(n + 1, 0)
                all_rounds(pool, round_)
                residual.rstd(pool, NT - 1)

            @block.tensor
            def _(pe):
                pe.wait_ge(k.loaded["sa"], 16 * 7)

                def turn(n, par):
                    pe.wait_ge(slots_ready[par], n + 1)
                    for c in range(C):
                        last = nc.tensor.transpose(bank(par, BA)[:, c * P:(c + 1) * P], slots[par][:, c * P:(c + 1) * P],
                                                   k.ident)
                    last.then_inc(turn_done[par], 1)

                def queries(n, par):
                    pe.wait_ge(diag_ready[par], n + 1)
                    pe.wait_ge(turn_ready[par], n + 1)
                    nc.tensor.matmul(bank(par, BA)[:, 2 * P:3 * P], k.const("ones"), srs_diag[par][:, :],
                                     start=True, stop=True).then_inc(srs_done[par], 1)
                    for m in range(C):
                        for c in range(C):
                            last = nc.tensor.matmul(bank(par, BB)[:, m * P:(m + 1) * P], wqk[:, c, m * P:(m + 1) * P],
                                                    slotsT[par][:, c, :], start=c == 0, stop=c == C - 1)
                    last.then_inc(q_done[par], 1)

                def scores(pair, n, par):
                    pe.wait_ge(ctxT_loaded[par], 16 * C * (pair + 1))
                    pe.wait_ge(q_ready[par], C * n + C)
                    for b in range(TB):
                        for t in range(KT2):
                            for c in range(C):
                                nc.tensor.matmul(bank(par, BA)[:, (b * 3 + t) * S:(b * 3 + t) * S + P],
                                                 ctxT[par][:, c, b, t * P:(t + 1) * P],
                                                 qT[par][:, c, b * S:b * S + P], start=c == 0, stop=c == C - 1)
                    lastcol = bank(par, BA)[:, 0:TB * 3 * S].rearrange("p (b t s) -> p b t s", b=TB, t=3)[:, :, 2, :]
                    for c in range(C):
                        last = nc.tensor.matmul(lastcol, lastT[:, c, :], qT[par][:, c, 0:P].rearrange("p (b s) -> p b s", b=TB),
                                                start=c == 0, stop=c == C - 1)
                    last.then_inc(scores_done[par], 1)

                def hidden_rz(par):
                    nc.tensor.matmul(bank(par, BR), k.ones_parts[:, :], k.bias_parts[:, 0:2 * D], start=True, stop=False,
                                     skip_group_check=True)
                    for c in range(C):
                        nc.tensor.matmul(bank(par, BR), slotsT[par][:, c, :], whhT[:, c, 0:2 * D], start=False, stop=False,
                                         skip_group_check=True)

                def hidden_n(par, chunks=range(C)):
                    if 0 in chunks:
                        nc.tensor.matmul(bank(par, BN), k.ones_parts[:, :], k.bias_parts[:, 2 * D:4 * D], start=True,
                                         stop=False, skip_group_check=True)
                    for c in chunks:
                        nc.tensor.matmul(bank(par, BN)[:, D:2 * D], slotsT[par][:, c, :], whhT[:, c, 2 * D:3 * D],
                                         start=False, stop=c == C - 1, skip_group_check=True)

                def updates(pair, n, par):
                    pe.wait_ge(rows_loaded[par], 16 * TB * (pair + 1))
                    pe.wait_ge(share_ready[par], n + 1)
                    pe.wait_ge(weight_ready[par], n + 1)
                    shares = share[par][:, :, :].rearrange("p (b t) s -> p b t s", t=3)
                    for c in range(C):
                        nc.tensor.matmul(bank(par, BB)[:, c * P:(c + 1) * P], last_rows[:, c * P:(c + 1) * P],
                                         own_weights(par)[:, :, 2, :], start=True, stop=False, skip_group_check=True)
                        for b in range(TB):
                            for t in range(KT2):
                                last = nc.tensor.matmul(
                                    bank(par, BB)[:, c * P:(c + 1) * P], rows[par][:, b * KT2 + t, c * P:(c + 1) * P],
                                    weight[par][:, (b * 3 + t) * P:(b * 3 + t + 1) * P],
                                    start=False, stop=b == TB - 1 and t == KT2 - 1, skip_group_check=True)
                        if c == 0:
                            for t in range(3):
                                total = nc.tensor.matmul(bank(par, BA)[:, 3 * P:4 * P], k.const("ones"), shares[:, :, t, :],
                                                         start=t == 0, stop=t == 2)
                            total.then_inc(totals_done[par], 1)
                    last.then_inc(u_done[par], 1)

                def gates(n, par):
                    pe.wait_ge(uT_ready[par], n + 1)
                    for c in range(C):
                        nc.tensor.matmul(bank(par, BR), uT[par][:, c, :], wvi[:, c, 0:2 * D],
                                         start=False, stop=c == C - 1, skip_group_check=True)
                    for c in range(C):
                        last = nc.tensor.matmul(bank(par, BN)[:, 0:D], uT[par][:, c, :], wvi[:, c, 2 * D:3 * D],
                                                start=False, stop=c == C - 1, skip_group_check=True)
                    last.then_inc(gates_done[par], 1)

                turn(0, 0)
                queries(0, 0)
                pe.wait_ge(padded, 2)
                pe.wait_ge(last_loaded, 16 * 3)
                scores(0, 0, 0)
                hidden_rz(0)
                hidden_n(0)

                def round_(pair, r, n, follows):
                    updates(pair, n, 0)
                    turn(n, 1)
                    queries(n, 1)
                    gates(n, 0)
                    scores(pair, n, 1)
                    hidden_rz(1)
                    if follows:
                        turn(n + 1, 0)
                    hidden_n(1, [0])
                    if follows:
                        queries(n + 1, 0)
                    hidden_n(1, range(1, C))
                    if follows:
                        scores(pair + 1 if r == ROUNDS - 1 else pair, n + 1, 0)
                        hidden_rz(0)
                    updates(pair, n, 1)
                    if follows:
                        hidden_n(0)
                    gates(n, 1)
                all_rounds(pe, round_)
                pe.wait_ge(residual.mean_ready, NT - 1)
                residual.tensor(pe)

            @block.scalar
            def _(act):

                def turned(n, par):
                    act.wait_ge(turn_done[par], n + 1)
                    nc.scalar.copy(slotsT[par][:, :, :].rearrange("p c n -> p (c n)"), bank(par, BA)[:, 0:C * P]
                                   ).then_inc(turn_ready[par], 1)

                def exponentials(n, par):
                    act.wait_ge(centred[par], n + 1)
                    nc.scalar.activation(e[par][:, :, :], shifted[par][:, :, :], ACT.Exp).then_inc(e_ready[par], 1)

                def tanhs(n, par):
                    act.wait_ge(gates_done[par], n + 1)
                    nc.scalar.activation(trz[par][:, :], bank(par, BR), ACT.Tanh, scale=0.5).then_inc(trz_ready[par], 1)
                    act.wait_ge(pre_ready[par], n + 1)
                    nc.scalar.activation(cand[par][:, :], pre[par][:, :], ACT.Tanh).then_inc(cand_ready[par], 1)
                turned(0, 0)
                exponentials(0, 0)

                def round_(pair, r, n, follows):
                    turned(n, 1)
                    tanhs(n, 0)
                    if follows:
                        turned(n + 1, 0)
                    exponentials(n, 1)
                    if follows:
                        exponentials(n + 1, 0)
                    tanhs(n, 1)
                all_rounds(act, round_)
                residual.scalar(act)

            @block.vector
            def _(dve):
                order = Count(dve, order_sem)
                wide = [P, TB * 3, S]

                def square(par):
                    own_wait(dve, k)
                    nc.vector.tensor_tensor_reduce(out=squares[par][:, :], in0=slots[par][:, :], in1=slots[par][:, :],
                                                   scale=1.0, scalar=D * 1e-6, op0=ALU.mult, op1=ALU.add,
                                                   accum_out=total_sq[par][:, :]).then_inc(sq_ready[par], 1)

                def context_squares(pair, par):
                    dve.wait_ge(rows_loaded[par], 16 * TB * (pair + 1))
                    own_wait(dve, k)
                    for i in range(TB * KT2):
                        last = nc.vector.bn_stats(cst[par][:, i, :], rows[par][:, i, :])
                    order.after(last)
                    own_wait(dve, k)
                    for i in range(TB * KT2):
                        last = nc.vector.bn_aggr(cmv[par][:, i, :], cst[par][:, i, :])
                    order.after(last)
                    mean = cmv[par][:, :, 0].rearrange("p (b t) -> p b t", b=TB)
                    order.after(nc.vector.tensor_tensor(rms[par][:, :, 0:KT2], mean, mean, ALU.mult))
                    nc.vector.tensor_tensor(rms[par][:, :, 0:KT2], rms[par][:, :, 0:KT2],
                                            cmv[par][:, :, 1].rearrange("p (b t) -> p b t", b=TB), ALU.add)
                    nc.vector.tensor_copy(rms[par][:, :, 2], last_ms[:, :].broadcast_to([P, TB])
                                          ).then_inc(ms_ready[par], 1)

                def queries_out(n, par):
                    dve.wait_ge(srs_done[par], n + 1)
                    order.after(nc.vector.tensor_copy(srs_rows[par][:, :], bank(par, BA)[:, 2 * P:3 * P]))
                    dve.wait_ge(q_done[par], n + 1)
                    for m in range(C):
                        nc.vector.scalar_tensor_tensor(out=qT[par][:, m, 0:P], in0=bank(par, BB)[:, m * P:(m + 1) * P],
                                                       scalar=w_in[:, m:m + 1], in1=srs_rows[par][:, :],
                                                       op0=ALU.mult, op1=ALU.mult).then_inc(q_ready[par], 1)

                def centre(pair, n, par):
                    dve.wait_ge(scores_done[par], n + 1)
                    sc = bank(par, BA)[:, 0:TB * 3 * S].rearrange("p (n s) -> p n s", s=S)
                    order.after(nc.vector.tensor_reduce(top[par][:, :], sc, AX.X, ALU.max))
                    order.after(nc.vector.tensor_tensor(shifted[par][:, :, :], sc, top[par][:, :].unsqueeze(2)
                                                        .broadcast_to(wide), ALU.subtract))
                    dve.wait_ge(rms_ready[par], pair + 1)
                    nc.vector.tensor_tensor(shifted[par][:, :, :], shifted[par][:, :, :],
                                            rms[par][:, :, :].rearrange("p b t -> p (b t)").unsqueeze(2)
                                            .broadcast_to(wide), ALU.mult).then_inc(centred[par], 1)

                def shares(pair, n, par):
                    dve.wait_ge(e_ready[par], n + 1)
                    order.after(nc.vector.tensor_reduce(total[par][:, :], e[par][:, :, :], AX.X, ALU.add))
                    order.after(nc.vector.reciprocal(inv[par][:, :], total[par][:, :]))
                    order.after(nc.vector.tensor_tensor(inv[par][:, :], inv[par][:, :],
                                                        k.const("last_key")[:, bass.ds((pair * 2 + par) * TB * 3, TB * 3)],
                                                        ALU.mult))
                    nc.vector.tensor_tensor(invr[par][:, :], inv[par][:, :],
                                            rms[par][:, :, :].rearrange("p b t -> p (b t)"), ALU.mult
                                            ).then_inc(inv_ready[par], 1)
                    nc.vector.tensor_tensor(share[par][:, :, :], e[par][:, :, :],
                                            inv[par][:, :].unsqueeze(2).broadcast_to(wide), ALU.mult
                                            ).then_inc(share_ready[par], 1)

                def updates_out(n, par):
                    dve.wait_ge(totals_done[par], n + 1)
                    order.after(nc.vector.tensor_scalar(colinv[par][:, :], bank(par, BA)[:, 3 * P:4 * P], 1e-6, None,
                                                        ALU.add))
                    order.after(nc.vector.reciprocal(colinv[par][:, :], colinv[par][:, :]))
                    dve.wait_ge(u_done[par], n + 1)
                    nc.vector.tensor_tensor(uT[par][:, :, :], bank(par, BB)[:, 0:2 * P].rearrange("p (c n) -> p c n", c=C),
                                            colinv[par][:, :].unsqueeze(1).broadcast_to([P, C, P]), ALU.mult
                                            ).then_inc(uT_ready[par], 1)

                def new_slots(pair, r, n, par, follows):
                    dve.wait_ge(trz_ready[par], n + 1)
                    order.after(nc.vector.scalar_tensor_tensor(out=pre[par][:, :], in0=trz[par][:, 0:D], scalar=1.0,
                                                               in1=bank(par, BN)[:, D:2 * D], op0=ALU.add, op1=ALU.mult))
                    nc.vector.scalar_tensor_tensor(out=pre[par][:, :], in0=pre[par][:, :], scalar=0.5,
                                                   in1=bank(par, BN)[:, 0:D], op0=ALU.mult, op1=ALU.add
                                                   ).then_inc(pre_ready[par], 1)
                    dve.wait_ge(cand_ready[par], n + 1)
                    order.after(nc.vector.tensor_tensor(diff[par][:, :], slots[par][:, :], cand[par][:, :], ALU.subtract))
                    order.after(nc.vector.scalar_tensor_tensor(out=diff[par][:, :], in0=trz[par][:, D:2 * D], scalar=1.0,
                                                               in1=diff[par][:, :], op0=ALU.add, op1=ALU.mult))
                    last = nc.vector.scalar_tensor_tensor(out=slots[par][:, :], in0=diff[par][:, :], scalar=0.5,
                                                          in1=cand[par][:, :], op0=ALU.mult, op1=ALU.add)
                    if r < ROUNDS - 1:
                        last.then_inc(slots_ready[par], 1)
                        dve.wait_ge(slots_ready[par], n + 2)
                        square(par)
                        return
                    order.after(last)
                    tile = bass.ds(pair * 2 + par, 1)
                    x_tile = k.x[:, tile, :].rearrange("p t d -> p (t d)")
                    order.after(nc.vector.tensor_tensor(x_tile, x_tile, slots[par][:, :], ALU.add))
                    if follows:
                        nc.vector.tensor_copy(slots[par][:, :], k.z[:, bass.ds(pair * 2 + 2 + par, 1), :]
                                              .rearrange("p t d -> p (t d)")).then_inc(slots_ready[par], 1)
                        dve.wait_ge(slots_ready[par], n + 2)
                        square(par)
                    order.after(nc.vector.bn_stats(cst[par][:, 0, :], x_tile))
                    own_wait(dve, k)
                    order.after(nc.vector.bn_aggr(cmv[par][:, 0, :], cst[par][:, 0, :]))
                    nc.vector.tensor_copy(k.mean_var[:, tile, :].rearrange("p t d -> p (t d)"), cmv[par][:, 0, :]
                                          ).then_inc(residual.mean_ready, 1)

                for par in range(2):
                    nc.vector.tensor_copy(slots[par][:, :], k.z[:, par, :]).then_inc(slots_ready[par], 1)
                for par in range(2):
                    dve.wait_ge(slots_ready[par], 1)
                    square(par)
                queries_out(0, 0)
                dve.wait_ge(last_loaded, 16 * 3)
                order.after(nc.vector.bn_stats(last_st[:, :], last_rows[:, :]))
                order.after(nc.vector.bn_aggr(last_mv[:, :], last_st[:, :]))
                order.after(nc.vector.scalar_tensor_tensor(out=last_ms[:, :], in0=last_mv[:, 0:1], scalar=last_mv[:, 0:1],
                                                           in1=last_mv[:, 1:2], op0=ALU.mult, op1=ALU.add))
                context_squares(0, 0)
                centre(0, 0, 0)
                shares(0, 0, 0)

                def round_(pair, r, n, follows):
                    updates_out(n, 0)
                    queries_out(n, 1)
                    if r == 0:
                        context_squares(pair, 1)
                    new_slots(pair, r, n, 0, follows)
                    centre(pair, n, 1)
                    if follows:
                        queries_out(n + 1, 0)
                    shares(pair, n, 1)
                    for t in complete(pair, r):
                        residual.normalise(dve, t)
                    if follows:
                        next_pair = pair + 1 if r == ROUNDS - 1 else pair
                        if r == ROUNDS - 1:
                            context_squares(pair + 1, 0)
                        centre(next_pair, n + 1, 0)
                        shares(next_pair, n + 1, 0)
                    updates_out(n, 1)
                    new_slots(pair, r, n, 1, follows)
                all_rounds(dve, round_, order, 2 * (ROUNDS * (1 + 2 + 3 + 2 + 3) + 3 + 4))
                residual.normalise(dve, NT - 1)
                residual.zT.vector(dve)


def causal_attention(nc, k):
    self_attention(nc, k, "ra", float(HD) ** -0.5, [k.const("causal_pen")], True, k.const("ones"))


def per_slot(eng, body):
    body(0, 0, 0, True)
    body(1, 0, 1, True)
    with eng.Fori(1, SLOTS // 2) as pair:
        for par in range(2):
            body(pair * 2 + par, pair, par, True)
    body(SLOTS - 1, SLOTS // 2, 0, False)


def experts(nc, k, name, gated):
    ins, ps = k.ins, k.ps
    pre = "L1_ffn_" if gated else "L0_ffn_"
    with ExitStack() as ctx:
        def sb(n, shape, dt=F32):
            return ctx.enter_context(nc.sbuf_tensor(name + "_" + n, shape, dt))

        def sem(n):
            return k.sem(name + "_" + n)

        w_route, b_route = k.route[name]
        logits, rest, tie, first, second, both = (
            sb(n, [P, NT, E]) for n in ("logits", "rest", "tie", "first", "second", "both"))
        best = sb("best", [P, 4, NT])
        gap, share1, share2 = (sb(n, [P, NT]) for n in ("gap", "share1", "share2"))
        counted = sb("counted", [P, 2, NT, E])
        earlier = sb("earlier", [P, NT + 1, E])
        over = sb("over", [P, E, SLOTS_EACH])
        slots_of = sb("slots_of", [P, E])
        start_of = sb("start_of", [P, E])
        place = sb("place", [P, NT, E])
        at = sb("at", [P, 2, NT])
        row = sb("row", [P, 2, NT], I32)
        begun = sb("begun", [P, SLOTS, E])
        expert_f = sb("expert_f", [P, SLOTS])
        expert = sb("expert", [P, SLOTS], I32)

        win = [sb("win%d" % i, [P, 2, C, FF]) for i in range(1 + gated)]
        bin_ = [sb("bin%d" % i, [P, 2, FF // P]) for i in range(1 + gated)]
        wout = sb("wout", [P, 2, FF // P, D])
        bout = sb("bout", [P, 2, D])
        rows = sb("rows", [P, 2, SLOT // P, D])
        xT = sb("xT", [P, C, SLOT])
        hT = sb("hT", [P, 2, FF // P, SLOT])
        y = sb("y", [P, 2, SLOT // P, D])
        mixed1, mixed2 = sb("mixed1", [P, NT, D]), sb("mixed2", [P, NT, D])
        if gated:
            halfb = sb("halfb", [P, 2, FF // P])
            gelu, tanh = (sb(n, [P, 2, SLOT]) for n in ("gelu", "tanh"))
            g_e, b_e = sb("g_e", [P, 2, D]), sb("b_e", [P, 2, D])
            rbias = sb("rbias", [P, 2, SLOT // P, D])
            resid = sb("resid", [P, SLOT // P, D])
            st = sb("st", [P, SLOT // P, 6])
            mv = sb("mv", [P, SLOT // P, 2])
            rs = sb("rs", [P, SLOT // P])
        else:
            gamma, beta = sb("gamma", [P, D]), sb("beta", [P, D])

        if not gated:
            residual, fold = Residual(nc, k, name), Fold(nc, k, sb)
            mix_ready, mix_stats, mix_mean, mix_var, mix_rstd, mix_norm, mix_scaled = (
                sem(n) for n in ("mix_ready", "mix_stats", "mix_mean", "mix_var", "mix_rstd", "mix_norm", "mix_scaled"))
        else:
            x_ready, x_stored = sem("x_ready"), sem("x_stored")
        route_loaded, places_known = k.loaded[name], sem("places_known")
        small_loaded, logits_done, gap_ready, exp_ready, both_ready, counted_done, experts_known, scattered = (
            sem(n) for n in ("small_loaded", "logits_done", "gap_ready", "exp_ready", "both_ready", "counted_done",
                             "experts_known", "scattered"))
        rows_loaded, in_loaded, out_loaded = (
            [sem(n + "0"), sem(n + "1")] for n in ("rows_loaded", "in_loaded", "out_loaded"))
        xt_done, xt_ready, h_done, h_ready, y_done, y_read, y_ready = (
            sem(n) for n in ("xt_done", "xt_ready", "h_done", "h_ready", "y_done", "y_read", "y_ready"))
        y_stored = [sem("y_stored0"), sem("y_stored1")]
        gathered = [[sem("gathered%d%d" % (way, half)) for half in range(2)] for way in range(2)]
        order_sem = sem("vector_order")
        if gated:
            halfb_ready, act_done, rbias_ready = (
                sem(n) for n in ("halfb_ready", "act_done", "rbias_ready"))
            rstats_ready, rvar_ready, rrstd_ready = (sem(n) for n in ("rstats_ready", "rvar_ready", "rrstd_ready"))
        HB, XB, YB = 0, 4, 5
        FOLD_BANKS = (6, 7, 0, 1, 2, 3)
        HC_N = FF // P
        PER_IN, PER_OUT = (4, 4) if gated else (2, 2)
        ff_names = ("Wi", "Wg") if gated else ("W1",)
        fb_names = ("bi", "bg") if gated else ("b1",)
        out_w, out_b = ("Wo", "bo") if gated else ("W2", "b2")

        with nc.Block() as block:
            @block.sync
            def _(sp):
                if not gated:
                    load_attention(k, sp, "ra")
                    load_slot_weights(k, sp)
                    fold.sync(sp)
                    load_route(k, sp, "e2")
                    sp.dma_start(gamma[:, :], ins[pre + "gamma"].partition_broadcast(P)).then_inc(small_loaded, 16)
                    sp.dma_start(beta[:, :], ins[pre + "beta"].partition_broadcast(P)).then_inc(small_loaded, 16)
                sp.wait_ge(experts_known, 1)

                def load_in(s, par):
                    one = bass.ds(sp.value_load(expert[0:1, bass.ds(s, 1)], min_val=0, max_val=E - 1), 1)
                    for n, t in zip(ff_names, win):
                        sp.dma_start(t[:, par, :, :], ins[pre + n][one, :, :].rearrange("e (c p) h -> p (e c) h", p=P)
                                     ).then_inc(in_loaded[par], 16)
                    for n, t in zip(fb_names, bin_):
                        sp.dma_start(t[:, par, :], ins[pre + n][one, :, :].rearrange("e p n -> p (e n)")
                                     ).then_inc(in_loaded[par], 16)

                def load_out(s, par):
                    one = bass.ds(sp.value_load(expert[0:1, bass.ds(s, 1)], min_val=0, max_val=E - 1), 1)
                    sp.dma_start(wout[:, par, :, :], ins[pre + out_w][one, :, :].rearrange("e (c p) d -> p (e c) d", p=P)
                                 ).then_inc(out_loaded[par], 16)
                    for n, t in [(out_b, bout)] + ([("gamma", g_e), ("beta", b_e)] if gated else []):
                        sp.dma_start(t[:, par, :], ins[pre + n][one, :].rearrange("e d -> (e d)").partition_broadcast(P)
                                     ).then_inc(out_loaded[par], 16)

                def load_rows(s, par):
                    sp.dma_start(rows[:, par, :, :], k.sorted_x.ap()[bass.ds(s * SLOT, SLOT), :]
                                 .rearrange("(t p) d -> p t d", p=P)).then_inc(rows_loaded[par], 16)

                def load_ahead(s, par):
                    sp.wait_ge(h_ready, HC_N * s + HC_N)
                    own_wait(sp, k)
                    if gated:
                        sp.wait_ge(rbias_ready, s + 1)
                        own_wait(sp, k)
                    load_rows(s + 2, par)
                    load_in(s + 2, par)

                def store(s, par):
                    sp.wait_ge(y_ready, s + 1)
                    sp.dma_start(k.sorted_y.ap()[bass.ds(s * SLOT, SLOT), :].rearrange("(t p) d -> p t d", p=P),
                                 y[:, par, :, :]).then_inc(y_stored[par], 16)
                load_in(0, 0)
                load_out(0, 0)
                sp.wait_ge(scattered, 16 * 2 * NT)
                for par in range(2):
                    load_rows(par, par)
                load_in(1, 1)
                load_out(1, 1)
                with sp.Fori(0, SLOTS // 2 - 1) as pair:
                    for par in range(2):
                        load_ahead(pair * 2 + par, par)
                        store(pair * 2 + par, par)
                        load_out(pair * 2 + par + 2, par)
                load_ahead(SLOTS - 3, 0)
                store(SLOTS - 3, 0)
                load_out(SLOTS - 1, 0)
                store(SLOTS - 2, 1)
                store(SLOTS - 1, 0)
                for par in range(2):
                    sp.wait_ge(y_stored[par], 16 * ((SLOTS + 1 - par) // 2))
                if gated:
                    for half in range(2):
                        lo, hi = half * NT // 2, (half + 1) * NT // 2
                        sp.wait_ge(x_ready, hi)
                        sp.dma_start(k.out.rearrange("b s d -> (b s) d").rearrange("(t p) d -> p t d", p=P)[:, lo:hi, :],
                                     k.x[:, lo:hi, :]).then_inc(x_stored, 16)
                    sp.wait_ge(x_stored, 16 * 2)

            @block.gpsimd
            def _(pool):
                pool.wait_ge(k.cleared, 16)
                pool.wait_ge(places_known, 1)
                for t in range(NT):
                    for way in range(2):
                        pool.indirect_dma_start(out=k.sorted_x.ap(), in_=k.z[:, t, :], in_offset=None,
                                                out_offset=bass.IndirectOffsetOnAxis(ap=row[:, way, t:t + 1], axis=0)
                                                ).then_inc(scattered, 16)
                if gated:
                    def prepare(s, pair, par):
                        pool.wait_ge(in_loaded[par], 16 * PER_IN * (pair + 1))
                        if seen(s, 2):
                            pool.wait_ge(y_ready, s - 1)
                        own_wait(pool, k)
                        nc.gpsimd.tensor_scalar(halfb[:, par, :], bin_[1][:, par, :], 0.5, None, ALU.mult
                                                ).then_inc(halfb_ready, 1)
                        pool.wait_ge(rows_loaded[par], 16 * (pair + 1))
                        pool.wait_ge(out_loaded[par], 16 * PER_OUT * (pair + 1))
                        own_wait(pool, k)
                        nc.gpsimd.tensor_tensor(rbias[:, par, :, :], rows[:, par, :, :],
                                                bout[:, par, :].unsqueeze(1).broadcast_to([P, SLOT // P, D]), ALU.add
                                                ).then_inc(rbias_ready, 1)
                    prepare(0, 0, 0)

                    def body(s, pair, par, has_next):
                        if has_next:
                            prepare(s + 1, pair if par == 0 else pair + 1, 1 - par)
                        pool.wait_ge(rstats_ready, s + 1)
                        own_wait(pool, k)
                        nc.gpsimd.tensor_scalar(rs[:, :], mv[:, :, 1], 1e-12, None, ALU.add).then_inc(rvar_ready, 1)
                        pool.wait_ge(rvar_ready, s + 1)
                        own_wait(pool, k)
                        nc.gpsimd.tensor_tensor(rs[:, :], rs[:, :], k.const("minus_half")[:, 0:SLOT // P], ALU.pow
                                                ).then_inc(rrstd_ready, 1)
                    per_slot(pool, body)
                for par in range(2):
                    pool.wait_ge(y_stored[par], 16 * ((SLOTS + 1 - par) // 2))
                for way, dst in enumerate((mixed1, mixed2)):
                    for t in range(NT):
                        pool.indirect_dma_start(out=dst[:, t, :], out_offset=None, in_=k.sorted_y.ap(),
                                                in_offset=bass.IndirectOffsetOnAxis(ap=row[:, way, t:t + 1], axis=0)
                                                ).then_inc(gathered[way][t // (NT // 2)], 16)
                if not gated:
                    for t in range(NT):
                        pool.wait_ge(mix_mean, t + 1)
                        nc.gpsimd.tensor_scalar(k.rstd[:, t:t + 1], k.mean_var[:, t, 1:2], 1e-5, None, ALU.add
                                                ).then_inc(mix_var, 1)
                        pool.wait_ge(mix_var, t + 1)
                        nc.gpsimd.tensor_tensor(k.rstd[:, t:t + 1], k.rstd[:, t:t + 1], k.const("minus_half")[:, 0:1],
                                                ALU.pow).then_inc(mix_rstd, 1)
                    residual.gpsimd(pool)

            @block.tensor
            def _(pe):
                pe.wait_ge(route_loaded, 16 * 2)
                for t in range(NT):
                    dst = ps[:, 4, t * E:(t + 1) * E]
                    for c in range(C):
                        last = nc.tensor.matmul(dst, k.zT[:, c, t * P:(t + 1) * P], w_route[:, c, :],
                                                start=c == 0, stop=c == C - 1)
                last.then_inc(logits_done, 1)
                pe.wait_ge(both_ready, 1)
                chosen = both[:, :, :].rearrange("p t e -> p (t e)")
                nc.tensor.matmul(ps[:, 5, 0:NT * E], k.const("before"), chosen, start=True, stop=True)
                nc.tensor.matmul(ps[:, 5, NT * E:2 * NT * E], k.const("ones"), chosen, start=True, stop=True
                                 ).then_inc(counted_done, 1)

                if not gated:
                    fold.tensor(pe, FOLD_BANKS)

                def transpose_rows(pair, par):
                    pe.wait_ge(rows_loaded[par], 16 * (pair + 1))
                    for c in range(C):
                        for t in range(SLOT // P):
                            last = nc.tensor.transpose(ps[:, XB, (c * (SLOT // P) + t) * P:(c * (SLOT // P) + t + 1) * P],
                                                       rows[:, par, t, c * P:(c + 1) * P], k.ident)
                    last.then_inc(xt_done, 1)

                pe.wait_ge(experts_known, 1)
                transpose_rows(0, 0)
                if not gated:
                    pe.wait_ge(fold.ready, 6)

                def body(s, pair, par, has_next):
                    pe.wait_ge(xt_ready, s + 1)
                    pe.wait_ge(in_loaded[par], 16 * PER_IN * (pair + 1))
                    own_wait(pe, k)
                    for n in range(HC_N):
                        if seen(s, 1) or n >= 4:
                            pe.wait_ge(h_ready, HC_N * s + n - 3)
                        for i, w in enumerate(win):
                            for c in range(C):
                                last = nc.tensor.matmul(ps[:, HB + n % 4, i * SLOT:(i + 1) * SLOT],
                                                        w[:, par, c, n * P:(n + 1) * P], xT[:, c, :],
                                                        start=c == 0, stop=c == C - 1)
                        last.then_inc(h_done, 1)
                    if has_next:
                        transpose_rows(pair if par == 0 else pair + 1, 1 - par)
                    if seen(s, 1):
                        pe.wait_ge(y_read if gated else y_ready, s)
                    pe.wait_ge(out_loaded[par], 16 * PER_OUT * (pair + 1))
                    own_wait(pe, k)
                    for n in range(HC_N):
                        pe.wait_ge(h_ready, HC_N * s + n + 1)
                        for t in range(SLOT // P):
                            last = nc.tensor.matmul(ps[:, YB, t * D:(t + 1) * D], hT[:, par, n, t * P:(t + 1) * P],
                                                    wout[:, par, n, :], start=n == 0 and t == 0, stop=n == HC_N - 1,
                                                    skip_group_check=True)
                    last.then_inc(y_done, 1)
                per_slot(pe, body)
                if not gated:
                    residual.tensor(pe)

            @block.scalar
            def _(act):
                act.wait_ge(gap_ready, 1)
                nc.scalar.activation(share2[:, :], gap[:, :], ACT.Exp).then_inc(exp_ready, 1)
                if not gated:
                    fold.scalar(act, FOLD_BANKS)

                def rows_out(s):
                    act.wait_ge(xt_done, s + 1)
                    nc.scalar.copy(xT[:, :, :].rearrange("p c n -> p (c n)"), ps[:, XB, :]).then_inc(xt_ready, 1)
                rows_out(0)

                def body(s, pair, par, has_next):
                    if gated:
                        act.wait_ge(halfb_ready, s + 1)
                    elif seen(s, 2):
                        act.wait_ge(y_done, s - 1)
                    for n in range(HC_N):
                        act.wait_ge(h_done, HC_N * s + n + 1)
                        if gated:
                            if seen(s, 1) or n >= 2:
                                act.wait_ge(h_ready, HC_N * s + n - 1)
                            nc.scalar.activation(gelu[:, n % 2, :], ps[:, HB + n % 4, 0:SLOT], ACT.Gelu,
                                                 bias=bin_[0][:, par, n:n + 1])
                            nc.scalar.activation(tanh[:, n % 2, :], ps[:, HB + n % 4, SLOT:2 * SLOT], ACT.Tanh,
                                                 bias=halfb[:, par, n:n + 1], scale=0.5).then_inc(act_done, 1)
                        else:
                            nc.scalar.activation(hT[:, par, n, :], ps[:, HB + n % 4, 0:SLOT], ACT.Gelu,
                                                 bias=bin_[0][:, par, n:n + 1]).then_inc(h_ready, 1)
                    if has_next:
                        rows_out(s + 1)
                per_slot(act, body)
                if not gated:
                    residual.scalar(act)

            @block.vector
            def _(dve):
                order = Count(dve, order_sem)
                dve.wait_ge(route_loaded, 16 * 2)
                dve.wait_ge(logits_done, 1)
                order.after(nc.vector.tensor_tensor(logits[:, :, :], ps[:, 4, 0:NT * E].rearrange("p (t e) -> p t e", e=E),
                                                    b_route[:, :].unsqueeze(1).broadcast_to([P, NT, E]), ALU.add))

                def pick(src, chosen, value, winner):
                    order.after(nc.vector.tensor_reduce(best[:, value, :], src, AX.X, ALU.max))
                    order.after(nc.vector.tensor_tensor(tie[:, :, :], src, best[:, value, :].unsqueeze(2)
                                                        .broadcast_to([P, NT, E]), ALU.is_equal))
                    order.after(nc.vector.tensor_tensor(tie[:, :, :], tie[:, :, :], k.const("prefer").unsqueeze(1)
                                                        .broadcast_to([P, NT, E]), ALU.mult))
                    order.after(nc.vector.tensor_reduce(best[:, winner, :], tie[:, :, :], AX.X, ALU.max))
                    order.after(nc.vector.tensor_tensor(chosen, tie[:, :, :], best[:, winner, :].unsqueeze(2)
                                                        .broadcast_to([P, NT, E]), ALU.is_equal))
                pick(logits[:, :, :], first[:, :, :], 0, 2)
                order.after(nc.vector.scalar_tensor_tensor(out=rest[:, :, :], in0=first[:, :, :], scalar=-3.0e38,
                                                           in1=logits[:, :, :], op0=ALU.mult, op1=ALU.add))
                pick(rest[:, :, :], second[:, :, :], 1, 3)
                nc.vector.tensor_tensor(both[:, :, :], first[:, :, :], second[:, :, :], ALU.add).then_inc(both_ready, 1)
                nc.vector.tensor_tensor(gap[:, :], best[:, 1, :], best[:, 0, :], ALU.subtract).then_inc(gap_ready, 1)
                dve.wait_ge(exp_ready, 1)
                order.after(nc.vector.tensor_scalar(gap[:, :], share2[:, :], 1.0, None, ALU.add))
                order.after(nc.vector.reciprocal(share1[:, :], gap[:, :]))
                order.after(nc.vector.tensor_tensor(share2[:, :], share2[:, :], share1[:, :], ALU.mult))
                dve.wait_ge(counted_done, 1)
                order.after(nc.vector.tensor_copy(counted[:, :, :, :].rearrange("p a t e -> p (a t e)"), ps[:, 5, 0:2 * NT * E]))
                order.after(nc.vector.memset(earlier[:, 0, :], 0.0))
                for t in range(NT):
                    order.after(nc.vector.tensor_tensor(earlier[:, t + 1, :], earlier[:, t, :], counted[:, 1, t, :], ALU.add))
                order.after(nc.vector.tensor_tensor(
                    over[:, :, :], earlier[:, NT, :].unsqueeze(2).broadcast_to([P, E, SLOTS_EACH]),
                    k.const("slot_floor").unsqueeze(1).broadcast_to([P, E, SLOTS_EACH]), ALU.is_gt))
                order.after(nc.vector.tensor_reduce(slots_of[:, :], over[:, :, :], AX.X, ALU.add))
                order.after(nc.vector.memset(start_of[:, 0:1], 0.0))
                for e in range(1, E):
                    order.after(nc.vector.tensor_tensor(start_of[:, e:e + 1], start_of[:, e - 1:e], slots_of[:, e - 1:e],
                                                        ALU.add))
                order.after(nc.vector.tensor_tensor(place[:, :, :], earlier[:, 0:NT, :], counted[:, 0, :, :], ALU.add))
                order.after(nc.vector.scalar_tensor_tensor(out=place[:, :, :], in0=start_of[:, :].unsqueeze(1)
                                                           .broadcast_to([P, NT, E]), scalar=float(SLOT),
                                                           in1=place[:, :, :], op0=ALU.mult, op1=ALU.add))
                for way, chosen in enumerate((first, second)):
                    order.after(nc.vector.tensor_tensor(tie[:, :, :], chosen[:, :, :], place[:, :, :], ALU.mult))
                    order.after(nc.vector.tensor_reduce(at[:, way, :], tie[:, :, :], AX.X, ALU.add))
                nc.vector.tensor_copy(row[:, :, :], at[:, :, :]).then_inc(places_known, 1)
                order.after(nc.vector.tensor_tensor(
                    begun[:, :, :], k.const("slot").unsqueeze(2).broadcast_to([P, SLOTS, E]),
                    start_of[:, :].unsqueeze(1).broadcast_to([P, SLOTS, E]), ALU.is_ge))
                order.after(nc.vector.tensor_reduce(expert_f[:, :], begun[:, :, :], AX.X, ALU.add))
                nc.vector.tensor_scalar(expert[:, :], expert_f[:, :], -1.0, None, ALU.add).then_inc(experts_known, 1)

                def body(s, pair, par, has_next):
                    if gated:
                        if seen(s, 2):
                            dve.wait_ge(y_done, s - 1)
                        for n in range(HC_N):
                            dve.wait_ge(act_done, HC_N * s + n + 1)
                            nc.vector.scalar_tensor_tensor(out=hT[:, par, n, :], in0=tanh[:, n % 2, :], scalar=1.0,
                                                           in1=gelu[:, n % 2, :], op0=ALU.add, op1=ALU.mult
                                                           ).then_inc(h_ready, 1)
                    dve.wait_ge(y_done, s + 1)
                    if gated:
                        dve.wait_ge(rbias_ready, s + 1)
                        nc.vector.scalar_tensor_tensor(out=resid[:, :, :].rearrange("p t d -> p (t d)"), in0=ps[:, YB, :],
                                                       scalar=0.5, in1=rbias[:, par, :, :].rearrange("p t d -> p (t d)"),
                                                       op0=ALU.mult, op1=ALU.add).then_inc(y_read, 1)
                        dve.wait_ge(y_read, s + 1)
                        for t in range(SLOT // P):
                            last = nc.vector.bn_stats(st[:, t, :], resid[:, t, :])
                        order.after(last)
                        own_wait(dve, k)
                        for t in range(SLOT // P):
                            last = nc.vector.bn_aggr(mv[:, t, :], st[:, t, :])
                        last.then_inc(rstats_ready, 1)
                        dve.wait_ge(rrstd_ready, s + 1)
                        for t in range(SLOT // P):
                            last = nc.vector.tensor_scalar(resid[:, t, :], resid[:, t, :], mv[:, t, 0:1], rs[:, t:t + 1],
                                                           ALU.subtract, ALU.mult)
                        order.after(last)
                        order.after(nc.vector.tensor_tensor(resid[:, :, :], resid[:, :, :],
                                                            g_e[:, par, :].unsqueeze(1).broadcast_to([P, SLOT // P, D]),
                                                            ALU.mult))
                        if seen(s, 2):
                            dve.wait_ge(y_stored[par], 16 * pair)
                        nc.vector.tensor_tensor(y[:, par, :, :], resid[:, :, :],
                                                b_e[:, par, :].unsqueeze(1).broadcast_to([P, SLOT // P, D]),
                                                ALU.add).then_inc(y_ready, 1)
                    else:
                        if seen(s, 2):
                            dve.wait_ge(y_stored[par], 16 * pair)
                        nc.vector.tensor_tensor(y[:, par, :, :], ps[:, YB, :].rearrange("p (t d) -> p t d", d=D),
                                                bout[:, par, :].unsqueeze(1).broadcast_to([P, SLOT // P, D]),
                                                ALU.add).then_inc(y_ready, 1)
                if not gated:
                    fold.vector(dve, order)
                if gated:
                    body(0, 0, 0, True)
                    body(1, 0, 1, True)
                    with dve.Fori(1, SLOTS // 2) as pair:
                        order.enter(pair - 1, 6)
                        for par in range(2):
                            body(pair * 2 + par, pair, par, True)
                        order.leave(SLOTS // 2 - 1)
                    body(SLOTS - 1, SLOTS // 2, 0, False)
                else:
                    per_slot(dve, body)

                def mix(way, t, src, dst):
                    if t % (NT // 2) == 0:
                        dve.wait_ge(gathered[way][t // (NT // 2)], 16 * (NT // 2))
                    mixed, share = ((mixed1, share1), (mixed2, share2))[way]
                    return nc.vector.scalar_tensor_tensor(out=dst[:, t, :], in0=mixed[:, t, :], scalar=share[:, t:t + 1],
                                                          in1=src[:, t, :], op0=ALU.mult, op1=ALU.add)
                if gated:
                    for t in range(NT):
                        last = mix(0, t, k.x, k.x)
                    order.after(last)
                    for t in range(NT):
                        mix(1, t, k.x, k.x).then_inc(x_ready, 1)
                else:
                    dve.wait_ge(small_loaded, 16 * 2)
                    nc.vector.tensor_tensor(k.x[:, :, :], k.x[:, :, :], beta[:, :].unsqueeze(1).broadcast_to([P, NT, D]),
                                            ALU.add)
                    for t in range(NT):
                        last = mix(0, t, k.z, mixed1)
                    order.after(last)
                    for n in range(NT + 5):
                        if n < NT:
                            mix(1, n, mixed1, mixed1).then_inc(mix_ready, 1)
                        t = n - 1
                        if 0 <= t < NT:
                            dve.wait_ge(mix_ready, t + 1)
                            nc.vector.bn_stats(k.stats[:, t, :], mixed1[:, t, :]).then_inc(mix_stats, 1)
                        t = n - 2
                        if 0 <= t < NT:
                            dve.wait_ge(mix_stats, t + 1)
                            nc.vector.bn_aggr(k.mean_var[:, t, :], k.stats[:, t, :]).then_inc(mix_mean, 1)
                        t = n - 4
                        if 0 <= t < NT:
                            dve.wait_ge(mix_rstd, t + 1)
                            nc.vector.tensor_scalar(mixed1[:, t, :], mixed1[:, t, :], k.mean_var[:, t, 0:1],
                                                    k.rstd[:, t:t + 1], ALU.subtract, ALU.mult).then_inc(mix_norm, 1)
                        t = n - 5
                        if 0 <= t < NT:
                            dve.wait_ge(mix_norm, t + 1)
                            nc.vector.tensor_tensor(mixed1[:, t, :], mixed1[:, t, :], gamma[:, :], ALU.mult
                                                    ).then_inc(mix_scaled, 1)

                    def add(t):
                        dve.wait_ge(mix_scaled, t + 1)
                        return nc.vector.tensor_tensor(k.x[:, t, :], k.x[:, t, :], mixed1[:, t, :], ALU.add)
                    residual.vector(dve, add)


def experts_one(nc, k):
    experts(nc, k, "e1", False)


def experts_two(nc, k):
    experts(nc, k, "e2", True)


def constants():
    import numpy as np
    table = np.zeros((P, CONST_WIDTH), np.float32)

    def put(name, value):
        a, b = CONST_COLS[name]
        table[:, a:b] = np.broadcast_to(value, (P, b - a))
    row = np.arange(P)[:, None]
    put("ident", row == np.arange(P))
    put("ones", 1.0)
    put("before", row < np.arange(P))
    put("head_of_row", row // HD == np.arange(HC))
    put("group_of_row", row // S == np.arange(HG))
    put("query", row % S == np.arange(P) % S)
    put("minus_half", -0.5)
    put("prefer", E - np.arange(E))
    put("slot_floor", SLOT * np.arange(SLOTS_EACH))
    put("slot", np.arange(SLOTS))
    valid = np.ones((P, B, 3), np.float32)
    valid[:, :, 2] = row == np.arange(B)
    put("last_key", valid.reshape(P, -1))
    q, key = row % S, np.arange(S)
    pair, key_pair = q // 2, key // 2
    for w in range(2):
        first = pair - w
        a = CONST_COLS["window_pen"][0] + w * S
        table[:, a:a + S] = np.where((key_pair == first) | (key_pair == first + 1), 0.0, MASKED)
        on = (first >= 0) & (first + 1 < S // 2)
        table[:, CONST_COLS["window_on"][0] + w] = on[:, 0]
    put("window_count", np.where((pair == 0) | (pair == S // 2 - 1), 1.0, 2.0))
    put("causal_pen", np.where(key <= q, 0.0, MASKED))
    theta = np.repeat((np.float32(10000.0) ** (-np.arange(0, D, 2, dtype=np.float32) / np.float32(D))), 2)
    angle = (np.arange(S, dtype=np.float32)[:, None] * theta[None, :])[np.arange(P) % S]
    put("cos", np.cos(angle))
    put("sin", np.sin(angle) * np.where(np.arange(D) % 2 == 0, -1.0, 1.0))
    return table


_DIRECT = ["x", "L0_xattn_Wq", "L0_xattn_Wk", "L0_xattn_Wv", "L0_xattn_Wo", "L0_xattn_bo",
           "L0_attn_w_qkv", "L0_attn_w_out", "L0_attn_b_out", "L1_attn_bo"] + [
    "L0_ffn_" + n for n in ("Wg", "bg", "W1", "W2", "b2", "gamma", "beta")] + [
    "L1_xattn_" + n for n in ("Wq", "Wk", "Wv", "gru_bih", "gru_bhh")] + [
    "L1_ffn_" + n for n in ("Wr", "br", "Wi", "Wg", "Wo", "bo", "gamma", "beta")]
_EXPERT_COLUMNS = ["L0_ffn_b1", "L1_ffn_bi", "L1_ffn_bg"]
_TURNED = ["L1_attn_Wq", "L1_attn_Wk", "L1_attn_Wv", "L1_attn_Wo", "L1_xattn_gru_wih", "L1_xattn_gru_whh"]
_COLUMNS = ["L0_xattn_bq", "L0_xattn_bk", "L0_xattn_bv", "L1_xattn_slot_norm_w", "L1_xattn_input_norm_w"]


def kernel(**inputs):
    import numpy as _np
    import concourse.bacc as _bacc
    from concourse import mybir as _mybir
    from concourse.bass_utils import run_bass_kernel_spmd as _run

    laid_out = {name: _np.ascontiguousarray(inputs[name]) for name in _DIRECT}
    for name in _TURNED:
        laid_out[name + "T"] = _np.ascontiguousarray(_np.asarray(inputs[name]).T)
    for name in _COLUMNS:
        laid_out[name] = _np.ascontiguousarray(_np.asarray(inputs[name]).reshape(-1, P).T)
    for name in _EXPERT_COLUMNS:
        laid_out[name] = _np.ascontiguousarray(_np.transpose(_np.asarray(inputs[name]).reshape(E, -1, P), (0, 2, 1)))
    laid_out["mask"] = _np.ascontiguousarray(inputs["mask_Bx1xSxS2_if1"])
    laid_out["ctx"] = _np.ascontiguousarray(inputs["ctx_1024"])
    laid_out["ctxT"] = _np.ascontiguousarray(_np.transpose(inputs["ctx_1024"], (2, 0, 1)))
    laid_out["ctx_lastT"] = _np.ascontiguousarray(inputs["ctx_1024"][:, KEYS - 1, :].T)
    laid_out["consts"] = constants()
    nc = _bacc.Bacc("TRN2", target_bir_lowering=False, num_devices=1)
    arrays, args = {}, {}
    for name, a in laid_out.items():
        arrays[f"in_{name}_dram"] = a
        args[name] = nc.dram_tensor(f"in_{name}_dram", a.shape, _mybir.dt.from_np(a.dtype), kind="ExternalInput").ap()
    out = nc.dram_tensor("out_0_dram", (B, S, D), _mybir.dt.float32, kind="ExternalOutput").ap()
    build(nc, args, out)
    r = _run(nc, [arrays], core_ids=[0])
    return r.results[0]["out_0_dram"]
```
